# Optimizing a Trainium2 kernel written in Bass

```python
import numpy as np
import jax
import jax.numpy as jnp

def _softmax(x, axis=-1):
    return jax.nn.softmax(x, axis=axis)

def _gelu(x):
    return jax.nn.gelu(x, approximate=True)

def _silu(x):
    return jax.nn.silu(x)

def _sigmoid(x):
    return jax.nn.sigmoid(x)

def _layernorm(x, axis=-1, eps=1e-05):
    m = jnp.mean(x, axis=axis, keepdims=True)
    v = jnp.var(x, axis=axis, keepdims=True)
    return (x - m) / jnp.sqrt(v + eps)

def _scatter_add(tgt, idx, src, axis=0):
    return tgt.at[idx].add(src)

def _segment_sum(src, seg, n):
    return jax.ops.segment_sum(src, seg, n)
kernel_name = 'mk_hybrid_d2_jaxref_r8_4ea434'

def setup_inputs(seed: int=0):
    np.random.seed(seed)
    _w = jnp.asarray

    def _L0_attn_a_setup():
        import jax, jax.numpy as jnp
        import numpy as np
        D_MODEL = 128
        N_HEADS = 16
        D_HEAD = D_MODEL // N_HEADS
        K_WIN = 8
        DILATION = 2
        EPS = 1e-06

        def _dilated_mask(N):
            i = jnp.arange(N)[:, None]
            j = jnp.arange(N)[None, :]
            diff = j - i
            return (jnp.abs(diff) <= K_WIN * DILATION) & (jnp.mod(diff, DILATION) == 0)
        key = jax.random.key(seed)
        ks = jax.random.split(key, 5)
        B, N = (2, 256)
        s_in = 1.0 / np.sqrt(D_MODEL)
        x = jax.random.normal(ks[0], (B, N, D_MODEL), dtype=jnp.float32)
        qkv_w = jax.random.uniform(ks[1], (3 * D_MODEL, D_MODEL), dtype=jnp.float32, minval=-s_in, maxval=s_in)
        qkv_b = jax.random.uniform(ks[2], (3 * D_MODEL,), dtype=jnp.float32, minval=-s_in, maxval=s_in)
        out_w = jax.random.uniform(ks[3], (D_MODEL, D_MODEL), dtype=jnp.float32, minval=-s_in, maxval=s_in)
        out_b = jax.random.uniform(ks[4], (D_MODEL,), dtype=jnp.float32, minval=-s_in, maxval=s_in)
        return {'x': x, 'qkv_w': qkv_w, 'qkv_b': qkv_b, 'out_w': out_w, 'out_b': out_b}
    _L0_attn_a_in = _L0_attn_a_setup()

    def _L0_attn_b_setup():
        import jax, jax.numpy as jnp
        import numpy as np
        D = 128
        B, T = (4, 256)

        def _scan_combine(c1, c2):
            a1, b1 = c1
            a2, b2 = c2
            return (a2 * a1, a2 * b1 + b2)
        key = jax.random.key(seed)
        ks = jax.random.split(key, 7)
        s = 0.02
        return {'x': jax.random.normal(ks[0], (B, T, D), dtype=jnp.float32), 'W_in': s * jax.random.normal(ks[1], (2 * D, D), dtype=jnp.float32), 'b_in': jnp.zeros((2 * D,), dtype=jnp.float32), 'W_s': s * jax.random.normal(ks[2], (D, D), dtype=jnp.float32), 'b_s': jnp.zeros((D,), dtype=jnp.float32), 'W_o': s * jax.random.normal(ks[3], (D, D), dtype=jnp.float32), 'b_o': jnp.zeros((D,), dtype=jnp.float32)}
    _L0_attn_b_in = _L0_attn_b_setup()

    def _L0_ffn_setup():
        import jax, jax.numpy as jnp
        import numpy as np
        DIM = 128
        HIDDEN = 384
        SCALE = 1.0 / 127.0

        def _dequant(w_int, dtype):
            return w_int.astype(dtype) * jnp.asarray(SCALE, dtype)
        key = jax.random.key(seed)
        k_x, k_g, k_u, k_d = jax.random.split(key, 4)
        x = jax.random.normal(k_x, (4, 256, DIM), dtype=jnp.float32)
        w_gate = jax.random.randint(k_g, (HIDDEN, DIM), -127, 128, dtype=jnp.int32)
        w_up = jax.random.randint(k_u, (HIDDEN, DIM), -127, 128, dtype=jnp.int32)
        w_down = jax.random.randint(k_d, (DIM, HIDDEN), -127, 128, dtype=jnp.int32)
        return {'x': x, 'w_gate': w_gate, 'w_up': w_up, 'w_down': w_down}
    _L0_ffn_in = _L0_ffn_setup()

    def _L1_attn_a_setup():
        import jax, jax.numpy as jnp
        import numpy as np
        import math
        B, S, D = (4, 256, 128)
        H = 16
        HD = D // H
        DL = 32
        LAMBDA_DECAY = 0.01
        key = jax.random.key(seed)
        ks = jax.random.split(key, 8)
        sc = lambda fan_in: 1.0 / math.sqrt(fan_in)
        return {'x': jax.random.normal(ks[0], (B, S, D), dtype=jnp.float32), 'W_q': jax.random.normal(ks[1], (D, D), dtype=jnp.float32) * sc(D), 'W_k': jax.random.normal(ks[2], (D, D), dtype=jnp.float32) * sc(D), 'W_v': jax.random.normal(ks[3], (D, D), dtype=jnp.float32) * sc(D), 'W_o': jax.random.normal(ks[4], (D, D), dtype=jnp.float32) * sc(D), 'W_down_kv': jax.random.normal(ks[5], (D, DL), dtype=jnp.float32) * sc(D), 'W_up_k': jax.random.normal(ks[6], (DL, D), dtype=jnp.float32) * sc(DL), 'W_up_v': jax.random.normal(ks[7], (DL, D), dtype=jnp.float32) * sc(DL)}
    _L1_attn_a_in = _L1_attn_a_setup()

    def _L1_attn_b_setup():
        import jax, jax.numpy as jnp
        import numpy as np
        DM, DS, KW, GROUPS = (128, 16, 4, 8)
        BATCH, SEQ = (4, 256)
        EPS = 1e-05

        def _layer_norm(x, g, b):
            mu = jnp.mean(x, axis=-1, keepdims=True)
            var = jnp.var(x, axis=-1, keepdims=True)
            return (x - mu) * jax.lax.rsqrt(var + EPS) * g + b

        def _group_norm(y_bcl, g, b):
            B_, C_, L_ = y_bcl.shape
            yg = y_bcl.reshape(B_, GROUPS, C_ // GROUPS, L_)
            mu = jnp.mean(yg, axis=(2, 3), keepdims=True)
            var = jnp.var(yg, axis=(2, 3), keepdims=True)
            yg = (yg - mu) * jax.lax.rsqrt(var + EPS)
            return yg.reshape(B_, C_, L_) * g[None, :, None] + b[None, :, None]

        def _forward(u, in_proj_w, conv_w, conv_b, out_proj_w, ln_g, ln_b, gn_g, gn_b, A_log, D):
            B_, L_, _ = u.shape
            h = _layer_norm(u, ln_g, ln_b)
            proj = jnp.einsum('bld,od->blo', h, in_proj_w)
            x = proj[..., 0 * DM:1 * DM]
            z = proj[..., 1 * DM:2 * DM]
            dt_raw = proj[..., 2 * DM:3 * DM]
            res = proj[..., 3 * DM:4 * DM]
            Bm = proj[..., 4 * DM:4 * DM + DS]
            Cm = proj[..., 4 * DM + DS:4 * DM + 2 * DS]
            sg = proj[..., 4 * DM + 2 * DS:4 * DM + 3 * DS]
            xc = jax.lax.conv_general_dilated(x.transpose(0, 2, 1), conv_w, window_strides=(1,), padding=[(KW - 1, 0)], feature_group_count=DM, dimension_numbers=('NCH', 'OIH', 'NCH'))
            xc = jax.nn.silu(xc + conv_b[None, :, None]).transpose(0, 2, 1)
            dt = jax.nn.softplus(dt_raw)
            A = -jnp.exp(A_log)

            def step(hstate, t_in):
                dt_t, B_t, C_t, sg_t, x_t = t_in
                dA = jnp.exp(dt_t[..., None] * A)
                hstate = dA * hstate + dt_t[..., None] * B_t[:, None, :] * x_t[..., None]
                y_t = jnp.sum(hstate * C_t[:, None, :], axis=-1)
                s_t = jnp.mean(hstate * jax.nn.sigmoid(sg_t)[:, None, :], axis=1)
                return (hstate, (y_t, s_t))
            tm = lambda a: jnp.swapaxes(a, 0, 1)
            h0 = jnp.zeros((B_, DM, DS), dtype=u.dtype)
            _, (ys, ss) = jax.lax.scan(step, h0, (tm(dt), tm(Bm), tm(Cm), tm(sg), tm(xc)))
            y = tm(ys) + xc * D
            s_seq = tm(ss)
            y = _group_norm(y.transpose(0, 2, 1), gn_g, gn_b).transpose(0, 2, 1)
            y = y * jax.nn.silu(z)
            out = jnp.einsum('blf,of->blo', jnp.concatenate([y, s_seq], axis=-1), out_proj_w)
            return out + res + u
        key = jax.random.key(seed)
        ks = jax.random.split(key, 8)
        proj_dim = 3 * DS + 4 * DM
        A_log = jnp.log(jnp.broadcast_to(jnp.arange(1, DS + 1, dtype=jnp.float32), (DM, DS)))
        return {'u': jax.random.normal(ks[0], (BATCH, SEQ, DM), dtype=jnp.float32), 'in_proj_w': jax.random.normal(ks[1], (proj_dim, DM), dtype=jnp.float32) / np.sqrt(DM), 'conv_w': jax.random.normal(ks[2], (DM, 1, KW), dtype=jnp.float32) / np.sqrt(KW), 'conv_b': jnp.zeros((DM,), dtype=jnp.float32), 'out_proj_w': jax.random.normal(ks[3], (DM, DS + DM), dtype=jnp.float32) / np.sqrt(DS + DM), 'ln_g': jnp.ones((DM,), dtype=jnp.float32), 'ln_b': jnp.zeros((DM,), dtype=jnp.float32), 'gn_g': jnp.ones((DM,), dtype=jnp.float32), 'gn_b': jnp.zeros((DM,), dtype=jnp.float32), 'A_log': A_log, 'D': jnp.ones((DM,), dtype=jnp.float32)}
    _L1_attn_b_in = _L1_attn_b_setup()

    def _L1_ffn_setup():
        import jax, jax.numpy as jnp
        import numpy as np
        D_IN, D_HID = (128, 512)

        def _ternary(key, shape):
            return jax.random.randint(key, shape, -1, 2).astype(jnp.float32)

        def _tlin(x, w, s):
            return jnp.einsum('bsi,oi->bso', x, w) * s
        key = jax.random.key(seed)
        ks = jax.random.split(key, 12)
        inv = lambda fan: 1.0 / np.sqrt(fan).astype(np.float32)
        return {'x': jax.random.normal(ks[0], (4, 256, D_IN), dtype=jnp.float32), 'w1_w': _ternary(ks[1], (D_HID, D_IN)), 'w1_s': jax.random.uniform(ks[2], (D_HID,), dtype=jnp.float32) * inv(D_IN), 'w2_w': _ternary(ks[3], (D_HID, D_IN)), 'w2_s': jax.random.uniform(ks[4], (D_HID,), dtype=jnp.float32) * inv(D_IN), 'h1_w': _ternary(ks[5], (D_HID, D_HID)), 'h1_s': jax.random.uniform(ks[6], (D_HID,), dtype=jnp.float32) * inv(D_HID), 'h2_w': _ternary(ks[7], (D_HID, D_HID)), 'h2_s': jax.random.uniform(ks[8], (D_HID,), dtype=jnp.float32) * inv(D_HID), 'w3_w': _ternary(ks[9], (D_IN, D_HID)), 'w3_s': jax.random.uniform(ks[10], (D_IN,), dtype=jnp.float32) * inv(D_HID)}
    _L1_ffn_in = _L1_ffn_setup()
    _d = {'L0_attn_a_x': _L0_attn_a_in['x'], 'L0_attn_a_qkv_w': _L0_attn_a_in['qkv_w'], 'L0_attn_a_qkv_b': _L0_attn_a_in['qkv_b'], 'L0_attn_a_out_w': _L0_attn_a_in['out_w'], 'L0_attn_a_out_b': _L0_attn_a_in['out_b'], 'L0_attn_b_W_in': _L0_attn_b_in['W_in'], 'L0_attn_b_b_in': _L0_attn_b_in['b_in'], 'L0_attn_b_W_s': _L0_attn_b_in['W_s'], 'L0_attn_b_b_s': _L0_attn_b_in['b_s'], 'L0_attn_b_W_o': _L0_attn_b_in['W_o'], 'L0_attn_b_b_o': _L0_attn_b_in['b_o'], 'L0_ffn_w_gate': _L0_ffn_in['w_gate'], 'L0_ffn_w_up': _L0_ffn_in['w_up'], 'L0_ffn_w_down': _L0_ffn_in['w_down'], 'L1_attn_a_W_q': _L1_attn_a_in['W_q'], 'L1_attn_a_W_k': _L1_attn_a_in['W_k'], 'L1_attn_a_W_v': _L1_attn_a_in['W_v'], 'L1_attn_a_W_o': _L1_attn_a_in['W_o'], 'L1_attn_a_W_down_kv': _L1_attn_a_in['W_down_kv'], 'L1_attn_a_W_up_k': _L1_attn_a_in['W_up_k'], 'L1_attn_a_W_up_v': _L1_attn_a_in['W_up_v'], 'L1_attn_b_in_proj_w': _L1_attn_b_in['in_proj_w'], 'L1_attn_b_conv_w': _L1_attn_b_in['conv_w'], 'L1_attn_b_conv_b': _L1_attn_b_in['conv_b'], 'L1_attn_b_out_proj_w': _L1_attn_b_in['out_proj_w'], 'L1_attn_b_ln_g': _L1_attn_b_in['ln_g'], 'L1_attn_b_ln_b': _L1_attn_b_in['ln_b'], 'L1_attn_b_gn_g': _L1_attn_b_in['gn_g'], 'L1_attn_b_gn_b': _L1_attn_b_in['gn_b'], 'L1_attn_b_A_log': _L1_attn_b_in['A_log'], 'L1_attn_b_D': _L1_attn_b_in['D'], 'L1_ffn_w1_w': _L1_ffn_in['w1_w'], 'L1_ffn_w1_s': _L1_ffn_in['w1_s'], 'L1_ffn_w2_w': _L1_ffn_in['w2_w'], 'L1_ffn_w2_s': _L1_ffn_in['w2_s'], 'L1_ffn_h1_w': _L1_ffn_in['h1_w'], 'L1_ffn_h1_s': _L1_ffn_in['h1_s'], 'L1_ffn_h2_w': _L1_ffn_in['h2_w'], 'L1_ffn_h2_s': _L1_ffn_in['h2_s'], 'L1_ffn_w3_w': _L1_ffn_in['w3_w'], 'L1_ffn_w3_s': _L1_ffn_in['w3_s']}
    _x0 = _d['L0_attn_a_x']
    _d['L0_attn_a_x'] = jax.random.normal(jax.random.fold_in(jax.random.key(seed), 1), (2, 1024, 128), dtype=_x0.dtype)
    del _x0
    return _d

def reference(L0_attn_a_x, L0_attn_a_qkv_w, L0_attn_a_qkv_b, L0_attn_a_out_w, L0_attn_a_out_b, L0_attn_b_W_in, L0_attn_b_b_in, L0_attn_b_W_s, L0_attn_b_b_s, L0_attn_b_W_o, L0_attn_b_b_o, L0_ffn_w_gate, L0_ffn_w_up, L0_ffn_w_down, L1_attn_a_W_q, L1_attn_a_W_k, L1_attn_a_W_v, L1_attn_a_W_o, L1_attn_a_W_down_kv, L1_attn_a_W_up_k, L1_attn_a_W_up_v, L1_attn_b_in_proj_w, L1_attn_b_conv_w, L1_attn_b_conv_b, L1_attn_b_out_proj_w, L1_attn_b_ln_g, L1_attn_b_ln_b, L1_attn_b_gn_g, L1_attn_b_gn_b, L1_attn_b_A_log, L1_attn_b_D, L1_ffn_w1_w, L1_ffn_w1_s, L1_ffn_w2_w, L1_ffn_w2_s, L1_ffn_h1_w, L1_ffn_h1_s, L1_ffn_h2_w, L1_ffn_h2_s, L1_ffn_w3_w, L1_ffn_w3_s):

    def _L0_attn_a_ref(x, qkv_w, qkv_b, out_w, out_b):
        import jax, jax.numpy as jnp
        import numpy as np
        D_MODEL = 128
        N_HEADS = 16
        D_HEAD = D_MODEL // N_HEADS
        K_WIN = 8
        DILATION = 2
        EPS = 1e-06

        def _dilated_mask(N):
            i = jnp.arange(N)[:, None]
            j = jnp.arange(N)[None, :]
            diff = j - i
            return (jnp.abs(diff) <= K_WIN * DILATION) & (jnp.mod(diff, DILATION) == 0)
        B, N, D = x.shape
        qkv = x @ qkv_w.T + qkv_b
        q, k, v = jnp.split(qkv, 3, axis=-1)

        def heads(t):
            return t.reshape(B, N, N_HEADS, D_HEAD).transpose(0, 2, 1, 3)
        q, k, v = (heads(q), heads(k), heads(v))
        q = q / (jnp.linalg.norm(q, axis=-1, keepdims=True) + EPS)
        k = k / (jnp.linalg.norm(k, axis=-1, keepdims=True) + EPS)
        scale = jnp.float32(1.0)
        allowed = _dilated_mask(N)
        scores = jnp.einsum('bhnd,bhmd->bhnm', q, k) * scale
        scores = jnp.where(allowed[None, None], scores, -jnp.inf)
        attn = jax.nn.softmax(scores, axis=-1)
        out = jnp.einsum('bhnm,bhmd->bhnd', attn, v)
        out = out.transpose(0, 2, 1, 3).reshape(B, N, D)
        return out @ out_w.T + out_b

    def _L0_attn_b_ref(x, W_in, b_in, W_s, b_s, W_o, b_o):
        import jax, jax.numpy as jnp
        import numpy as np
        D = 128
        B, T = (4, 256)

        def _scan_combine(c1, c2):
            a1, b1 = c1
            a2, b2 = c2
            return (a2 * a1, a2 * b1 + b2)
        gv = jnp.einsum('btd,ed->bte', x, W_in) + b_in
        gate = jax.nn.sigmoid(gv[..., :D])
        val = gv[..., D:]
        sv = jnp.tanh(jnp.einsum('btd,ed->bte', val, W_s) + b_s)
        a = 1.0 - gate
        b = gate * sv
        _, h = jax.lax.associative_scan(_scan_combine, (a, b), axis=1)
        out = jnp.einsum('btd,ed->bte', h, W_o) + b_o
        return x + out

    def _L0_ffn_ref(x, w_gate, w_up, w_down):
        import jax, jax.numpy as jnp
        import numpy as np
        DIM = 128
        HIDDEN = 384
        SCALE = 1.0 / 127.0

        def _dequant(w_int, dtype):
            return w_int.astype(dtype) * jnp.asarray(SCALE, dtype)
        wg = _dequant(w_gate, x.dtype)
        wu = _dequant(w_up, x.dtype)
        wd = _dequant(w_down, x.dtype)
        gate = jnp.einsum('bsd,hd->bsh', x, wg)
        up = jnp.einsum('bsd,hd->bsh', x, wu)
        h = jax.nn.silu(gate) * up
        return jnp.einsum('bsh,dh->bsd', h, wd)

    def _L1_attn_a_ref(x, W_q, W_k, W_v, W_o, W_down_kv, W_up_k, W_up_v):
        import jax, jax.numpy as jnp
        import numpy as np
        import math
        B, S, D = (4, 256, 128)
        H = 16
        HD = D // H
        DL = 32
        LAMBDA_DECAY = 0.01
        b, s, d = x.shape
        q = x @ W_q
        k = x @ W_k
        v = x @ W_v
        latent_kv = (k + v) @ W_down_kv
        k_rec = (latent_kv @ W_up_k).reshape(b, s, H, HD).transpose(0, 2, 1, 3)
        v_rec = (latent_kv @ W_up_v).reshape(b, s, H, HD).transpose(0, 2, 1, 3)
        qh = q.reshape(b, s, H, HD).transpose(0, 2, 1, 3)
        scores = jnp.einsum('bhqd,bhkd->bhqk', qh, k_rec) / math.sqrt(d)
        t = jnp.arange(s, dtype=jnp.float32)
        decay = jnp.exp(-LAMBDA_DECAY * jnp.abs(t[:, None] - t[None, :]))
        scores = scores * decay[None, None, :, :]
        attn = jax.nn.softmax(scores, axis=-1)
        out = jnp.einsum('bhqk,bhkd->bhqd', attn, v_rec)
        out = out.transpose(0, 2, 1, 3).reshape(b, s, d)
        return out @ W_o

    def _L1_attn_b_ref(u, in_proj_w, conv_w, conv_b, out_proj_w, ln_g, ln_b, gn_g, gn_b, A_log, D):
        import jax, jax.numpy as jnp
        import numpy as np
        DM, DS, KW, GROUPS = (128, 16, 4, 8)
        BATCH, SEQ = (4, 256)
        EPS = 1e-05

        def _layer_norm(x, g, b):
            mu = jnp.mean(x, axis=-1, keepdims=True)
            var = jnp.var(x, axis=-1, keepdims=True)
            return (x - mu) * jax.lax.rsqrt(var + EPS) * g + b

        def _group_norm(y_bcl, g, b):
            B_, C_, L_ = y_bcl.shape
            yg = y_bcl.reshape(B_, GROUPS, C_ // GROUPS, L_)
            mu = jnp.mean(yg, axis=(2, 3), keepdims=True)
            var = jnp.var(yg, axis=(2, 3), keepdims=True)
            yg = (yg - mu) * jax.lax.rsqrt(var + EPS)
            return yg.reshape(B_, C_, L_) * g[None, :, None] + b[None, :, None]

        def _forward(u, in_proj_w, conv_w, conv_b, out_proj_w, ln_g, ln_b, gn_g, gn_b, A_log, D):
            B_, L_, _ = u.shape
            h = _layer_norm(u, ln_g, ln_b)
            proj = jnp.einsum('bld,od->blo', h, in_proj_w)
            x = proj[..., 0 * DM:1 * DM]
            z = proj[..., 1 * DM:2 * DM]
            dt_raw = proj[..., 2 * DM:3 * DM]
            res = proj[..., 3 * DM:4 * DM]
            Bm = proj[..., 4 * DM:4 * DM + DS]
            Cm = proj[..., 4 * DM + DS:4 * DM + 2 * DS]
            sg = proj[..., 4 * DM + 2 * DS:4 * DM + 3 * DS]
            xc = jax.lax.conv_general_dilated(x.transpose(0, 2, 1), conv_w, window_strides=(1,), padding=[(KW - 1, 0)], feature_group_count=DM, dimension_numbers=('NCH', 'OIH', 'NCH'))
            xc = jax.nn.silu(xc + conv_b[None, :, None]).transpose(0, 2, 1)
            dt = jax.nn.softplus(dt_raw)
            A = -jnp.exp(A_log)

            def step(hstate, t_in):
                dt_t, B_t, C_t, sg_t, x_t = t_in
                dA = jnp.exp(dt_t[..., None] * A)
                hstate = dA * hstate + dt_t[..., None] * B_t[:, None, :] * x_t[..., None]
                y_t = jnp.sum(hstate * C_t[:, None, :], axis=-1)
                s_t = jnp.mean(hstate * jax.nn.sigmoid(sg_t)[:, None, :], axis=1)
                return (hstate, (y_t, s_t))
            tm = lambda a: jnp.swapaxes(a, 0, 1)
            h0 = jnp.zeros((B_, DM, DS), dtype=u.dtype)
            _, (ys, ss) = jax.lax.scan(step, h0, (tm(dt), tm(Bm), tm(Cm), tm(sg), tm(xc)))
            y = tm(ys) + xc * D
            s_seq = tm(ss)
            y = _group_norm(y.transpose(0, 2, 1), gn_g, gn_b).transpose(0, 2, 1)
            y = y * jax.nn.silu(z)
            out = jnp.einsum('blf,of->blo', jnp.concatenate([y, s_seq], axis=-1), out_proj_w)
            return out + res + u
        return _forward(u, in_proj_w, conv_w, conv_b, out_proj_w, ln_g, ln_b, gn_g, gn_b, A_log, D)

    def _L1_ffn_ref(x, w1_w, w1_s, w2_w, w2_s, h1_w, h1_s, h2_w, h2_s, w3_w, w3_s):
        import jax, jax.numpy as jnp
        import numpy as np
        D_IN, D_HID = (128, 512)

        def _ternary(key, shape):
            return jax.random.randint(key, shape, -1, 2).astype(jnp.float32)

        def _tlin(x, w, s):
            return jnp.einsum('bsi,oi->bso', x, w) * s
        h = jax.nn.silu(_tlin(x, w1_w, w1_s)) * _tlin(x, w2_w, w2_s)
        h = jax.nn.gelu(_tlin(h, h1_w, h1_s), approximate=False)
        h = jax.nn.gelu(_tlin(h, h2_w, h2_s), approximate=False)
        return _tlin(h, w3_w, w3_s)
    x = L0_attn_a_x
    x = x + _L0_attn_a_ref(_layernorm(x, axis=-1), L0_attn_a_qkv_w, L0_attn_a_qkv_b, L0_attn_a_out_w, L0_attn_a_out_b)
    x = x + _L0_ffn_ref(_layernorm(x, axis=-1), L0_ffn_w_gate, L0_ffn_w_up, L0_ffn_w_down)
    x = x + _L0_attn_b_ref(_layernorm(x, axis=-1), L0_attn_b_W_in, L0_attn_b_b_in, L0_attn_b_W_s, L0_attn_b_b_s, L0_attn_b_W_o, L0_attn_b_b_o)
    x = x + _L0_ffn_ref(_layernorm(x, axis=-1), L0_ffn_w_gate, L0_ffn_w_up, L0_ffn_w_down)
    x = x + _L1_attn_a_ref(_layernorm(x, axis=-1), L1_attn_a_W_q, L1_attn_a_W_k, L1_attn_a_W_v, L1_attn_a_W_o, L1_attn_a_W_down_kv, L1_attn_a_W_up_k, L1_attn_a_W_up_v)
    x = x + _L1_ffn_ref(_layernorm(x, axis=-1), L1_ffn_w1_w, L1_ffn_w1_s, L1_ffn_w2_w, L1_ffn_w2_s, L1_ffn_h1_w, L1_ffn_h1_s, L1_ffn_h2_w, L1_ffn_h2_s, L1_ffn_w3_w, L1_ffn_w3_s)
    x = x + _L1_attn_b_ref(_layernorm(x, axis=-1), L1_attn_b_in_proj_w, L1_attn_b_conv_w, L1_attn_b_conv_b, L1_attn_b_out_proj_w, L1_attn_b_ln_g, L1_attn_b_ln_b, L1_attn_b_gn_g, L1_attn_b_gn_b, L1_attn_b_A_log, L1_attn_b_D)
    x = x + _L1_ffn_ref(_layernorm(x, axis=-1), L1_ffn_w1_w, L1_ffn_w1_s, L1_ffn_w2_w, L1_ffn_w2_s, L1_ffn_h1_w, L1_ffn_h1_s, L1_ffn_h2_w, L1_ffn_h2_s, L1_ffn_w3_w, L1_ffn_w3_s)
    return x

_drawn_inputs = setup_inputs


def setup_inputs(seed=0):
    import zlib

    import numpy as np

    out = dict(_drawn_inputs(seed))
    spreads = {'L0_attn_b_b_in': (0.0, 0.1),
     'L0_attn_b_b_s': (0.0, 0.1),
     'L0_attn_b_b_o': (0.0, 0.1),
     'L1_attn_b_conv_b': (0.0, 0.1),
     'L1_attn_b_ln_g': (1.0, 0.2),
     'L1_attn_b_ln_b': (0.0, 0.1),
     'L1_attn_b_gn_g': (1.0, 0.2),
     'L1_attn_b_gn_b': (0.0, 0.1),
     'L1_attn_b_D': (1.0, 0.2)}
    factors = {}
    for name, (base, spread) in spreads.items():
        noise = np.random.default_rng([zlib.crc32(name.encode()), seed]).standard_normal(out[name].shape)
        drawn = base * np.exp(spread * noise) if base else spread * noise
        out[name] = jnp.asarray(drawn.astype(out[name].dtype))
    for name, factor in factors.items():
        out[name] = (out[name] * factor).astype(out[name].dtype)
    return out
```

```python
from contextlib import ExitStack

import numpy as np
import concourse.bass as bass
from concourse import mybir

F32 = mybir.dt.float32
BF16 = mybir.dt.bfloat16
I32 = mybir.dt.int32
U8 = mybir.dt.uint8
ALU = mybir.AluOpType
ACT = mybir.ActivationFunctionType
AX_X = mybir.AxisListType.X

P = 128
B, S = 2, 1024
TOK = B * S
CH = 512
NCH = TOK // CH
H, HD = 16, 8
GH = 4
NG = H // GH
EPS = 1e-5
NORM_EPS = 1e-6
WIN = 8
QT = P - 2 * WIN
NT0 = -(-CH // QT)
HID0, HID1 = 384, 512
NJ0, NJ1 = HID0 // P, HID1 // P
QSCALE = 1.0 / 127.0
DS, KW = 16, 4
NKT = S // P
LAMBDA = 0.01
KP = 48
MROW = 96
NGRP = B * NG
NEG = -1.0e30


def win_start(t):
    return min(max(QT * t - WIN, 0), CH - P)


def win_queries(t):
    return QT * t, min(QT * (t + 1), CH)


def shape_constants():
    p = np.arange(P)
    f = np.float32
    same = lambda w: (p[:, None] // w == p[None, :] // w).astype(f)
    c = {}
    c["center"] = (np.eye(P) - 1.0 / P).astype(f)
    c["mean"] = np.full((P, P), 1.0 / P, f)
    c["headsum"] = same(HD)
    c["groupmean"] = same(P // 8) / 16
    spread = np.zeros((P, P), f)
    for g in range(GH):
        spread[32 * g + HD, 32 * g:32 * g + 32] = 1
    c["spread"] = spread
    c["ident"] = np.eye(P, dtype=f)
    c["headmask"] = (p[:, None] // HD == np.arange(H)[None, :]).astype(f)
    m = np.full((P, CH), NEG, f)
    for t in range(NT0):
        q0, q1 = win_queries(t)
        ok = np.abs(win_start(t) + p[:, None] - np.arange(q0, q1)[None, :]) <= WIN
        m[:, q0:q1][ok] = 0
    c["window"] = m
    oh = np.zeros((P, DS // 4, 32), f)
    for i in range(DS // 4):
        oh[:, i, i] = 1.0 / P
    c["statecol"] = oh.reshape(P, -1)
    t = np.arange(S, dtype=np.float64) - S // 2
    c["fall"] = np.tile(np.exp(-LAMBDA * t), (P, 1)).astype(f)
    c["rise"] = np.tile(np.exp(LAMBDA * t), (P, 1)).astype(f)
    i = p[:, None].astype(np.float64)
    strip = np.ones((P, 2 * S - P), f)
    strip[:, S - P:S] = np.exp(-2 * LAMBDA * np.maximum(p[None, :] - i, 0))
    c["strip"] = strip
    c["fixT"] = np.tile(np.exp(-2 * LAMBDA * np.maximum(i - p[None, :], 0)), (1, GH)).astype(f)
    return c


def build(nc, W, out, last_stage=8):
    ctx = ExitStack()
    with ctx:
        def sb(name, shape, dt=F32):
            return ctx.enter_context(nc.sbuf_tensor(name, shape, dt))

        sems = {}

        def sem(name):
            if name not in sems:
                sems[name] = ctx.enter_context(nc.semaphore(name))
            return sems[name]

        PS = ctx.enter_context(nc.psum_tensor("PS", [P, 8, CH], F32))
        XP = sb("XP", [P, TOK])
        XR = sb("XR", [P, TOK])
        XN = sb("XN", [P, TOK])
        RS = sb("RS", [P, 2, CH])
        SQ = sb("SQ", [P, 2, CH])

        loads = []

        ARENA = 124 * 1024
        arena = sb("arena", [P, ARENA], U8)
        early_at = {"ffn0i": ARENA - 4 * 3 * HID0, "window": ARENA - 4 * (3 * HID0 + CH)}

        def load(name, width, dt=F32):
            if name in early_at:
                t = arena[:, early_at[name]:early_at[name] + 4 * width].bitcast(dt)
            else:
                t = sb("w_" + name, [P, width], dt)
            loads.append((t, name))
            return t

        center, mean = load("center", P), load("mean", P)
        qkvT = load("qkvT", 3 * P)
        bqk = load("bqk", 2)
        bvrow = load("bvrow", P)
        headsum, headmask = load("headsum", P), load("headmask", H)
        ident, spread = load("ident", P), load("spread", P)
        windowf = load("window", CH)
        wo0, bo0 = load("wo0", NG * P), load("bo0", 1)
        ffn0i = load("ffn0i", 3 * HID0, I32)
        winb, bin_ = load("winb", 2 * P), load("binb", 2)
        wsT, bs_ = load("wsT", P), load("bs", 1)
        woT, bo_ = load("woT", P), load("bob", 1)
        N_EARLY = len(loads)
        w1T, w2T = load("w1T", HID1), load("w2T", HID1)
        h1T, h2T = load("h1T", NJ1 * HID1), load("h2T", NJ1 * HID1)
        w3T = load("w3T", HID1)
        scl = load("scl", 4 * NJ1 + 1)
        wqkv1, wlow = load("wqkv1", 3 * P), load("wlow", 3 * P)
        wo1 = load("wo1", NG * P)
        fixT = load("fixT", GH * P)
        minT = load("minT", 6 * P)
        mout = load("mout", 2 * P)
        mvec = load("mvec", 2 + KW + 1 + 2 + 1 + DS)
        groupmean, statecol = load("groupmean", P), load("statecol", (DS // 4) * 32)
        identb = sb("identb", [P, P], BF16)
        windowb = sb("windowb", [P, CH], BF16)
        ffn0 = sb("ffn0", [P, 3 * HID0])
        tiny = sb("tiny", [P, 32])

        arena_at = [0]

        def place(free, dt=F32, at=None):
            size = int(np.prod(free)) * (2 if dt == BF16 else 4)
            if at is None:
                at = arena_at[0]
                arena_at[0] += size
            assert at + size <= ARENA, (at, size)
            v = arena[:, at:at + size].bitcast(dt)
            if len(free) == 2:
                v = v.rearrange("p (a b) -> p a b", a=free[0])
            if len(free) == 3:
                v = v.rearrange("p (a b c) -> p a b c", a=free[0], b=free[1])
            if len(free) == 4:
                v = v.rearrange("p (a b c d) -> p a b c d", a=free[0], b=free[1], c=free[2])
            return v

        def chunk(c, n=CH):
            return bass.ts(c, n)

        def pairs(eng, body):
            with eng.Fori(0, NCH // 2) as i:
                for j in range(2):
                    body(i * 2 + j, j)

        x_ready = sem("x_ready")
        x_in, w_in, w_late = sem("x_in"), sem("w_in"), sem("w_late")
        consts_ready = sem("consts_ready")

        def apart(eng):
            eng.sem_inc(passed[eng.engine], 1)
        passed = {nc.scalar.engine: sem("passed_act"), nc.vector.engine: sem("passed_dve")}

        ln_centered, ln_squared, ln_var = sem("ln_centered"), sem("ln_squared"), sem("ln_var")
        ln_rstd_free, ln_free = sem("ln_rstd_free"), sem("ln_free")

        def ln_count(k, c):
            return 2 + NCH * k + c + 1

        def ln_pe(t, k, stage, src=None, all_banks=False):
            src = src if src is not None else XP if stage < 2 else XR
            if all_banks:
                t.wait_ge(x_ready, 1 + NCH * stage)
            with t.Fori(0, NCH // 2) as i:
                for j in range(2):
                    c = i * 2 + j
                    if src is XN:
                        t.wait_ge(ln_free, ln_count(k - 1, 0) + c)
                    elif stage > 0:
                        t.wait_ge(x_ready, 2 + NCH * (stage - 1) + (i * 2 + 1 if stage == 2 else c))
                    t.wait_ge(ln_free, NCH * k + c + 1)
                    t.matmul(PS[:, 5 + j, :], center[:], src[:, chunk(c)], start=True,
                             stop=True).then_inc(ln_centered, 1)
                for j in range(2):
                    c = i * 2 + j
                    t.wait_ge(ln_squared, NCH * k + c + 1)
                    t.wait_ge(ln_rstd_free, NCH * k + c + 1)
                    t.matmul(PS[:, 7, :], mean[:], SQ[:, j, :], start=True, stop=True).then_inc(ln_var, 1)

        def ln_act(a, k):
            def body(c, j):
                a.wait_ge(ln_centered, NCH * k + c + 1)
                nc.scalar.activation(SQ[:, j, :], PS[:, 5 + j, :], ACT.Square).then_inc(ln_squared, 1)

            def root(c, j):
                a.wait_ge(ln_var, NCH * k + c + 1)
                nc.scalar.activation(RS[:, j, :], PS[:, 7, :], ACT.Sqrt, bias=eps_col[:]).then_inc(ln_rstd_free, 1)
            with a.Fori(0, NCH // 2) as i:
                for j in range(2):
                    body(i * 2 + j, j)
                for j in range(2):
                    root(i * 2 + j, j)

        def ln_dve(v, k, dst=None, affine=None):
            dst = XN if dst is None else dst

            def body(c, j):
                v.wait_ge(ln_rstd_free, NCH * k + c + 2)
                v.reciprocal(RS[:, j, :], RS[:, j, :]).then_inc(ln_inverse, 1)
                v.wait_ge(ln_inverse, NCH * k + c + 1)
                if affine is None:
                    v.tensor_tensor(dst[:, chunk(c)], PS[:, 5 + j, :], RS[:, j, :], ALU.mult).then_inc(ln_free, 1)
                else:
                    v.tensor_tensor(dst[:, chunk(c)], PS[:, 5 + j, :], RS[:, j, :], ALU.mult).then_inc(ln_affine, 1)
                    v.wait_ge(ln_affine, c + 1)
                    v.tensor_scalar(dst[:, chunk(c)], dst[:, chunk(c)], affine[0], affine[1], ALU.mult,
                                    ALU.add).then_inc(ln_free, 1)
            pairs(v, body)
        ln_affine = sem("ln_affine")
        ln_inverse = sem("ln_inverse")
        eps_col = sb("eps_col", [P, 1])

        arena_at[0] = 0
        Q0, K0, QS, KS = place([CH]), place([CH]), place([CH]), place([CH])
        NQ, NK = place([CH]), place([CH])
        KZ = place([GH, CH])
        E0 = place([2, 2, CH])
        VW = place([NT0, H, 32])
        X0 = place([CH])
        OS, R0 = place([2, CH]), place([CH])
        ON0 = place([2, CH])
        a0_qk, a0_v, a0_sq, a0_ssq = sem("a0_qk"), sem("a0_v"), sem("a0_sq"), sem("a0_ssq")
        a0_vw, a0_norm, a0_kn, a0_kz = sem("a0_vw"), sem("a0_norm"), sem("a0_kn"), sem("a0_kz")
        a0_kz_free, a0_s_free, a0_e_free = (sem("a0_kz_free"), sem("a0_s_free"), sem("a0_e_free"))
        a0_o_free, a0_bc, a0_bc_free = sem("a0_o_free"), sem("a0_bc"), sem("a0_bc_free")
        a0_root, a0_on, a0_y, a0_x = sem("a0_root"), sem("a0_on"), sem("a0_y"), sem("a0_x")
        SBANK = [0, 1, 6, 7]

        def a0_pe(t):
            t.wait_ge(ln_free, ln_count(0, NCH - 1))
            with t.Fori(0, NCH) as c:
                t.wait_ge(x_ready, c + 1)
                t.wait_ge(a0_x, c + 1)
                x = X0
                t.matmul(PS[:, 0, :], qkvT[:, 0:P], x, start=True, stop=True)
                t.matmul(PS[:, 1, :], qkvT[:, P:2 * P], x, start=True, stop=True).then_inc(a0_qk, 1)
                for w in range(NT0):
                    xw = X0[:, win_start(w):win_start(w) + P]
                    mm = t.matmul(PS[:, 2 + w // 4, (w % 4) * P:(w % 4 + 1) * P], xw, qkvT[:, 2 * P:3 * P],
                                  start=(w % 4 == 0), stop=(w % 4 == 3 or w == NT0 - 1), skip_group_check=True)
                mm.then_inc(a0_v, 1)
                t.wait_ge(a0_sq, c * 2 + 1)
                t.matmul(PS[:, 4, :], headsum[:], QS, start=True, stop=True).then_inc(a0_ssq, 1)
                t.wait_ge(a0_sq, c * 2 + 2)
                t.matmul(PS[:, 5, :], headsum[:], KS, start=True, stop=True).then_inc(a0_ssq, 1)
                t.wait_ge(a0_kn, c * 2 + 2)
                for hp in range(11):
                    if hp < 8:
                        t.wait_ge(a0_s_free, c * 8 + hp + 1)
                        for h in (2 * hp, 2 * hp + 1):
                            bank = SBANK[h % 4]
                            t.wait_ge(a0_kz, c * H + h + 1)
                            t.matmul(PS[:, bank, :], identb[:], windowb[:], start=True, stop=False,
                                     skip_group_check=True)
                            for w in range(NT0):
                                q0, q1 = win_queries(w)
                                mm = t.matmul(PS[:, bank, q0:q1], KZ[:, h % GH, win_start(w):win_start(w) + P],
                                              Q0[:, q0:q1], start=False, stop=True, skip_group_check=True)
                            mm.then_inc(a0_kz_free, 1)
                    if 1 <= hp <= 8:
                        pr = hp - 1
                        t.wait_ge(a0_s_free, c * 8 + pr + 1 + 2)
                        if pr % 2 == 0:
                            t.wait_ge(a0_o_free, c * NG + pr // 2 + 1)
                        if pr == 0:
                            t.wait_ge(a0_vw, c + 2)
                        for h in (2 * pr, 2 * pr + 1):
                            g = h % GH
                            for w in range(NT0):
                                q0, q1 = win_queries(w)
                                mm = t.matmul(PS[32 * g:32 * g + 32, 2 + (h // GH) % 2, q0:q1], VW[:, w, h, :],
                                              E0[:, pr % 2, h % 2, q0:q1], start=(w == 0), stop=(w == NT0 - 1),
                                              skip_group_check=True)
                        mm.then_inc(a0_e_free, 1)
                    if hp >= 3 and hp % 2 == 1:
                        a = (hp - 3) // 2
                        t.wait_ge(a0_o_free, c * NG + a + 1 + 2)
                        t.wait_ge(a0_bc_free, c * NG + a + 1)
                        t.matmul(PS[:, 4, :], spread[:], OS[:, a % 2, :], start=True, stop=True).then_inc(a0_bc, 1)
                    if hp >= 4 and hp % 2 == 0:
                        a = (hp - 4) // 2
                        t.wait_ge(a0_on, c * NG + a + 1)
                        mm = t.matmul(PS[:, 5, :], wo0[:, a * P:(a + 1) * P], ON0[:, a % 2, :], start=(a == 0),
                                      stop=(a == NG - 1))
                mm.then_inc(a0_y, 1)

        def a0_act(a):
            with a.Fori(0, NCH) as c:
                a.wait_ge(ln_free, ln_count(0, 0) + c)
                apart(a)
                nc.scalar.copy(X0, XN[:, chunk(c)]).then_inc(a0_x, 1)
                a.wait_ge(a0_qk, c + 1)
                nc.scalar.activation(QS, PS[:, 0, :], ACT.Square, bias=bqk[:, 0:1]).then_inc(a0_sq, 1)
                nc.scalar.activation(KS, PS[:, 1, :], ACT.Square, bias=bqk[:, 1:2]).then_inc(a0_sq, 1)
                for n, nrm in enumerate((NQ, NK)):
                    a.wait_ge(a0_ssq, c * 2 + n + 1)
                    nc.scalar.activation(nrm, PS[:, 4 + n, :], ACT.Sqrt).then_inc(a0_root, 1)
                for pr in range(8):
                    a.wait_ge(a0_kz_free, GH + c * H + 2 * pr + 2)
                    a.wait_ge(a0_e_free, c * 8 + pr + 1)
                    b0 = SBANK[(2 * pr) % 4]
                    nc.scalar.activation(E0[:, pr % 2, :, :], PS[:, b0:b0 + 2, :], ACT.Exp).then_inc(a0_s_free, 1)

        def a0_dve(v):
            with v.Fori(0, NCH) as c:
                v.wait_ge(a0_v, c + 1)
                v.tensor_tensor(VW[:, 0:4, :, 0:HD], PS[:, 2, :].rearrange("p (w h d) -> p w h d", w=4, h=H),
                                bvrow[:].rearrange("p (w h d) -> p w h d", w=1, h=H).broadcast_to((P, 4, H, HD)),
                                ALU.add)
                v.tensor_tensor(VW[:, 4, :, 0:HD], PS[:, 3, 0:P].rearrange("p (h d) -> p h d", h=H),
                                bvrow[:].rearrange("p (h d) -> p h d", h=H), ALU.add).then_inc(a0_vw, 1)
                for n, (raw, nrm, bank) in enumerate(((Q0, NQ, 0), (K0, NK, 1))):
                    v.wait_ge(a0_root, c * 2 + n + 1)
                    v.tensor_scalar(nrm, nrm, NORM_EPS, None, ALU.add).then_inc(a0_norm, 1)
                    v.wait_ge(a0_norm, c * 4 + 2 * n + 1)
                    v.reciprocal(nrm, nrm).then_inc(a0_norm, 1)
                    v.wait_ge(a0_norm, c * 4 + 2 * n + 2)
                    v.scalar_tensor_tensor(out=raw, in0=PS[:, bank, :], scalar=bqk[:, n:n + 1], in1=nrm, op0=ALU.add,
                                           op1=ALU.mult).then_inc(a0_kn, 1)
                v.wait_ge(a0_kn, c * 2 + 2)

                def kz(h):
                    v.wait_ge(a0_kz_free, c * H + h + 1)
                    v.tensor_scalar(KZ[:, h % GH, :], K0, headmask[:, h:h + 1], None, ALU.mult).then_inc(a0_kz, 1)

                def take_o(a):
                    v.wait_ge(a0_e_free, 2 + c * 8 + 2 * a + 2)
                    v.tensor_copy(OS[:, a % 2, :], PS[:, 2 + a % 2, :]).then_inc(a0_o_free, 1)

                def norm_o(a):
                    v.wait_ge(a0_bc, c * NG + a + 1)
                    v.reciprocal(R0, PS[:, 4, :]).then_inc(a0_bc_free, 1)
                    v.wait_ge(a0_bc_free, c * NG + a + 2)
                    v.tensor_tensor(ON0[:, a % 2, :], OS[:, a % 2, :], R0, ALU.mult).then_inc(a0_on, 1)

                for h in range(GH):
                    kz(h)
                for hp in range(2, 11):
                    if hp < 8:
                        kz(2 * hp)
                        kz(2 * hp + 1)
                    if hp % 2 == 0:
                        take_o((hp - 2) // 2) if hp <= 8 else None
                    if hp % 2 == 1:
                        norm_o((hp - 3) // 2)
                v.wait_ge(a0_y, c + 1)
                v.scalar_tensor_tensor(out=XP[:, chunk(c)], in0=PS[:, 5, :], scalar=bo0[:, 0:1], in1=XP[:, chunk(c)],
                                       op0=ALU.add, op1=ALU.add).then_inc(x_ready, 1)

        arena_at[0] = 0
        F0_SG, F0_H = place([2, CH]), place([2, NJ0, CH])
        f0_gu, f0_silu, f0_h_free, f0_y = sem("f0_gu"), sem("f0_silu"), sem("f0_h_free"), sem("f0_y")

        def f0_pe(t, use, k):
            def up(c, j):
                t.wait_ge(ln_free, ln_count(k, 0) + c)
                for b in range(NJ0):
                    m = NJ0 * NCH * use + NJ0 * c + b
                    r = (NJ0 * j + b) % 2
                    t.wait_ge(f0_h_free, m + 1)
                    x = XN[:, chunk(c)]
                    t.matmul(PS[:, r, :], ffn0[:, b * P:(b + 1) * P], x, start=True, stop=True)
                    t.matmul(PS[:, 2 + r, :], ffn0[:, HID0 + b * P:HID0 + (b + 1) * P], x, start=True,
                             stop=True).then_inc(f0_gu, 1)

            def down(c, j):
                t.wait_ge(f0_h_free, 2 + NJ0 * NCH * use + NJ0 * c + NJ0)
                stage = (1, 3)[use]
                t.wait_ge(x_ready, 1 + NCH * stage + c)
                for b in range(NJ0):
                    mm = t.matmul(PS[:, 4, :], ffn0[:, 2 * HID0 + b * P:2 * HID0 + (b + 1) * P], F0_H[:, j, b, :],
                                  start=(b == 0), stop=(b == NJ0 - 1))
                mm.then_inc(f0_y, 1)
            with t.Fori(0, NCH // 2) as i:
                up(i * 2, 0)
                up(i * 2 + 1, 1)
                down(i * 2, 0)
                down(i * 2 + 1, 1)

        def f0_act(a, use):
            def body(c, j):
                for b in range(NJ0):
                    m = NJ0 * NCH * use + NJ0 * c + b
                    r = (NJ0 * j + b) % 2
                    a.wait_ge(f0_gu, m + 1)
                    a.wait_ge(f0_h_free, m + 1)
                    nc.scalar.activation(F0_SG[:, r, :], PS[:, r, :], ACT.Silu).then_inc(f0_silu, 1)
            pairs(a, body)

        def f0_dve(v, use, natural):
            def up(c, j):
                for b in range(NJ0):
                    m = NJ0 * NCH * use + NJ0 * c + b
                    r = (NJ0 * j + b) % 2
                    v.wait_ge(f0_silu, m + 1)
                    v.tensor_tensor(F0_H[:, j, b, :], F0_SG[:, r, :], PS[:, 2 + r, :], ALU.mult).then_inc(f0_h_free, 1)

            def down(c, j):
                v.wait_ge(f0_y, NCH * use + c + 1)
                if natural:
                    dst = XR[:, bass.ds((c - j) * CH, S)].rearrange("p (a two) -> p a two", two=2)[:, :, j]
                    v.tensor_tensor(dst, PS[:, 4, :], XP[:, chunk(c)], ALU.add).then_inc(x_ready, 1)
                else:
                    v.tensor_tensor(XR[:, chunk(c)], PS[:, 4, :], XR[:, chunk(c)], ALU.add).then_inc(x_ready, 1)
            with v.Fori(0, NCH // 2) as i:
                up(i * 2, 0)
                up(i * 2 + 1, 1)
                down(i * 2, 0)
                down(i * 2 + 1, 1)

        arena_at[0] = 0
        XV, GT, SV, SA, SBB = place([2, CH]), place([2, CH]), place([2, CH]), place([2, CH]), place([2, CH])
        HS = place([2, CH])
        XS = place([2, CH])
        b0_gv, b0_gate, b0_val, b0_s, b0_sv = sem("b0_gv"), sem("b0_gate"), sem("b0_val"), sem("b0_s"), sem("b0_sv")
        b0_a, b0_b, b0_h, b0_y, b0_t = sem("b0_a"), sem("b0_b"), sem("b0_h"), sem("b0_y"), sem("b0_t")

        def b0_pe(t, k):
            t.wait_ge(ln_free, ln_count(k, NCH - 1))
            with t.Fori(0, NCH // 2) as i:
                for j in range(2):
                    c = i * 2 + j
                    t.wait_ge(x_ready, 1 + NCH * 2 + i * 2)
                    x = XN[:, chunk(c)]
                    t.matmul(PS[:, 4 * j, :], winb[:, 0:P], x, start=True, stop=True)
                    t.matmul(PS[:, 4 * j + 1, :], winb[:, P:2 * P], x, start=True, stop=True).then_inc(b0_gv, 1)
                for j in range(2):
                    c = i * 2 + j
                    t.wait_ge(b0_val, c + 1)
                    t.matmul(PS[:, 4 * j + 2, :], wsT[:], XV[:, j, :], start=True, stop=True).then_inc(b0_s, 1)
                for j in range(2):
                    c = i * 2 + j
                    t.wait_ge(b0_h, c + 1)
                    t.matmul(PS[:, 4 * j + 3, :], woT[:], HS[:, j, :], start=True, stop=True).then_inc(b0_y, 1)

        def b0_act(a):
            with a.Fori(0, NCH // 2) as i:
                for j in range(2):
                    c = i * 2 + j
                    a.wait_ge(b0_gv, c + 1)
                    nc.scalar.activation(GT[:, j, :], PS[:, 4 * j, :], ACT.Sigmoid, bias=bin_[:, 0:1]).then_inc(b0_gate, 1)
                for j in range(2):
                    c = i * 2 + j
                    a.wait_ge(b0_s, c + 1)
                    nc.scalar.activation(SV[:, j, :], PS[:, 4 * j + 2, :], ACT.Tanh, bias=bs_[:, 0:1]).then_inc(b0_sv, 1)

        def b0_dve(v):
            with v.Fori(0, NCH // 2) as i:
                for j in range(2):
                    c = i * 2 + j
                    v.wait_ge(b0_gv, c + 1)
                    v.tensor_scalar(XV[:, j, :], PS[:, 4 * j + 1, :], bin_[:, 1:2], None, ALU.add).then_inc(b0_val, 1)
                for j in range(2):
                    c = i * 2 + j
                    v.wait_ge(b0_gate, c + 1)
                    v.tensor_scalar(SA[:, j, :], GT[:, j, :], -1.0, 1.0, ALU.mult, ALU.add).then_inc(b0_a, 1)
                    v.wait_ge(b0_sv, c + 1)
                    v.tensor_tensor(SBB[:, j, :], GT[:, j, :], SV[:, j, :], ALU.mult).then_inc(b0_b, 1)
                    v.wait_ge(b0_a, c + 1)
                    v.wait_ge(b0_b, c + 1)
                    if j == 1:
                        v.wait_ge(b0_h, c)
                    v.tensor_tensor_scan(HS[:, j, :], SA[:, j, :], SBB[:, j, :],
                                         0.0 if j == 0 else HS[:, 0, CH - 1:CH], ALU.mult, ALU.add).then_inc(b0_h, 1)
                for j in range(2):
                    c = i * 2 + j
                    v.wait_ge(b0_y, c + 1)
                    v.scalar_tensor_tensor(out=XS[:, j, :], in0=PS[:, 4 * j + 3, :], scalar=bo_[:, 0:1],
                                           in1=XN[:, chunk(c)], op0=ALU.add, op1=ALU.add).then_inc(b0_t, 1)
                    v.wait_ge(b0_t, c + 1)
                    v.tensor_tensor(XR[:, chunk(c)], XR[:, chunk(c)], XS[:, j, :], ALU.add).then_inc(x_ready, 1)

        arena_at[0] = 0
        F1_SG, F1_H = place([2, CH]), [place([2, NJ1, CH]), place([2, NJ1, CH])]
        f1_gu, f1_silu, f1_h_free = sem("f1_gu"), sem("f1_silu"), sem("f1_h_free")
        f1_p, f1_g, f1_y = sem("f1_p"), sem("f1_g"), sem("f1_y")
        S_W1, S_W2, S_H1, S_H2, S_W3 = 0, NJ1, 2 * NJ1, 3 * NJ1, 4 * NJ1

        def f1_pe(t, use, k, stage):
            t.wait_ge(ln_free, ln_count(k, NCH - 1))
            t.wait_ge(w_late, 16 * (len(loads) - N_EARLY))
            with t.Fori(0, NCH // 2) as i:
                t.wait_ge(x_ready, 1 + NCH * stage + i * 2)
                for j in range(2):
                    c = i * 2 + j
                    x = XN[:, chunk(c)]
                    for b in range(NJ1):
                        t.wait_ge(f1_h_free, NJ1 * NCH * use + NJ1 * c + b + 1)
                        r = b % 2
                        t.matmul(PS[:, r, :], w1T[:, b * P:(b + 1) * P], x, start=True, stop=True)
                        t.matmul(PS[:, 2 + r, :], w2T[:, b * P:(b + 1) * P], x, start=True, stop=True).then_inc(f1_gu, 1)
                for layer, w in ((0, h1T), (1, h2T)):
                    for j in range(2):
                        c = i * 2 + j
                        if layer == 0:
                            t.wait_ge(f1_h_free, 2 + NJ1 * NCH * use + NJ1 * c + NJ1)
                            if j == 0:
                                t.wait_ge(f1_h_free, 2 + NJ1 * NCH * use + NJ1 * c + 2 * NJ1)
                        else:
                            t.wait_ge(f1_g, 2 * NJ1 * NCH * use + i * 4 * NJ1 + NJ1 * (j + 1))
                        for b in range(NJ1):
                            for kk in range(NJ1):
                                mm = t.matmul(PS[:, 4 * j + b, :], w[:, kk * HID1 + b * P:kk * HID1 + (b + 1) * P],
                                              F1_H[layer][:, j, kk, :], start=(kk == 0), stop=(kk == NJ1 - 1))
                            mm.then_inc(f1_p, 1)
                for j in range(2):
                    c = i * 2 + j
                    t.wait_ge(f1_g, 2 * NJ1 * NCH * use + i * 4 * NJ1 + 2 * NJ1 + NJ1 * (j + 1))
                    for kk in range(NJ1):
                        mm = t.matmul(PS[:, 4 * j, :], w3T[:, kk * P:(kk + 1) * P], F1_H[0][:, j, kk, :],
                                      start=(kk == 0), stop=(kk == NJ1 - 1))
                    mm.then_inc(f1_y, 1)

        def f1_act(a, use):
            with a.Fori(0, NCH // 2) as i:
                for j in range(2):
                    for b in range(NJ1):
                        m = NJ1 * NCH * use + NJ1 * (i * 2 + j) + b
                        a.wait_ge(f1_gu, m + 1)
                        a.wait_ge(f1_h_free, m + 1)
                        nc.scalar.activation(F1_SG[:, b % 2, :], PS[:, b % 2, :], ACT.Silu,
                                             scale=scl[:, S_W1 + b:S_W1 + b + 1]).then_inc(f1_silu, 1)
                for layer, s0 in ((0, S_H1), (1, S_H2)):
                    for j in range(2):
                        for b in range(NJ1):
                            m = 2 * NJ1 * NCH * use + i * 4 * NJ1 + layer * 2 * NJ1 + j * NJ1 + b
                            a.wait_ge(f1_p, m + 1)
                            nc.scalar.activation(F1_H[1 - layer][:, j, b, :], PS[:, 4 * j + b, :], ACT.Gelu,
                                                 scale=scl[:, s0 + b:s0 + b + 1]).then_inc(f1_g, 1)

        def f1_dve(v, use):
            with v.Fori(0, NCH // 2) as i:
                for j in range(2):
                    for b in range(NJ1):
                        m = NJ1 * NCH * use + NJ1 * (i * 2 + j) + b
                        v.wait_ge(f1_silu, m + 1)
                        v.scalar_tensor_tensor(out=F1_H[0][:, j, b, :], in0=PS[:, 2 + b % 2, :],
                                               scalar=scl[:, S_W2 + b:S_W2 + b + 1], in1=F1_SG[:, b % 2, :],
                                               op0=ALU.mult, op1=ALU.mult).then_inc(f1_h_free, 1)
                for j in range(2):
                    c = i * 2 + j
                    v.wait_ge(f1_y, NCH * use + c + 1)
                    v.scalar_tensor_tensor(out=XR[:, chunk(c)], in0=PS[:, 4 * j, :], scalar=scl[:, S_W3:S_W3 + 1],
                                           in1=XR[:, chunk(c)], op0=ALU.mult, op1=ALU.add).then_inc(x_ready, 1)
        arena_at[0] = 0
        PK = place([2, GH, 4, S], BF16)
        PT = place([2, GH, CH])
        PD = place([2, GH * P])
        VG = place([2, NKT, GH, 32])
        on_at = arena_at[0]
        ON = place([NGRP, S])
        a1_end = arena_at[0]
        arena_at[0] = on_at
        V32 = place([4, CH])
        SPL = place([4, 3, CH], BF16)
        KV, LAT = place([CH]), place([CH])
        FALL, RISE = place([S]), place([S])
        STRIP = XP[:, 0:2 * S - P]
        JUNK = RS[:].rearrange("p a b -> p (a b)").bitcast(BF16).rearrange("p (a b) -> p a b", a=2)
        MX = SQ[:, 0, 0:P]
        MH = SQ[:, 1, 0:P].bitcast(BF16).rearrange("p (k q) -> p k q", k=2)
        VT = XN[:].rearrange("p (t a g d) -> p t a g d", t=TOK // P, a=NG, g=GH)
        scr = nc.dram_tensor("scr", (4, 3, B, P, S), BF16).ap()
        scr_heads = scr.rearrange("v k b (a g d) t -> v k (b a) g d t", a=NG, g=GH)
        mscr = nc.dram_tensor("mscr", (NGRP * 2, GH, S), BF16).ap()
        a1_qkv, a1_kv, a1_lat, a1_latc, a1_kr = sem("a1_qkv"), sem("a1_kv"), sem("a1_lat"), sem("a1_latc"), sem("a1_kr")
        a1_ver, a1_hi, a1_r1, a1_mid, a1_lo_free = sem("a1_ver"), sem("a1_hi"), sem("a1_r1"), sem("a1_mid"), sem("a1_lo_free")
        a1_v, a1_tab, a1_scr_free, a1_zero = sem("a1_v"), sem("a1_tab"), sem("a1_scr_free"), sem("a1_zero")
        pk_in = [[sem(f"pk_in{sl}{g}") for g in range(GH)] for sl in range(2)]
        pk_m, p1_s, p1_free = sem("pk_m"), sem("p1_s"), sem("p1_free")
        m_t, m_h, m_l, m_w = sem("m_t"), sem("m_h"), sem("m_l"), sem("m_w")
        dg_s, dg_fix, dg_m, dg_free = sem("dg_s"), sem("dg_fix"), sem("dg_m"), sem("dg_free")
        s_s, s_free, pv_free, o_free, vg_in = sem("s_s"), sem("s_free"), sem("pv_free"), sem("o_free"), sem("vg_in")
        a1_bc, a1_inv, a1_on, a1_y, a1_vg0 = sem("a1_bc"), sem("a1_inv"), sem("a1_on"), sem("a1_y"), sem("a1_vg0")
        SCALE = 1.0 / float(np.sqrt(P))
        NT1 = GH * NKT
        NS = 2 * NKT
        PV0 = NS + 2
        DG_PER = NKT
        PACKS = 12

        def is_diag(s):
            return s < NS and s % NKT // (NKT // 2) == s // NKT

        def diag_index(s):
            return sum(is_diag(r) for r in range(s))

        def a1_prep_pe(t):
            t.wait_ge(ln_free, ln_count(4, NCH - 1))
            t.wait_ge(w_late, 16 * (len(loads) - N_EARLY))
            with t.Fori(0, NCH) as c:
                x = XN[:, chunk(c)]
                t.wait_ge(a1_lo_free, 4 * c + 4)
                t.wait_ge(a1_v, c + 1)
                t.matmul(PS[:, 0, :], wqkv1[:, 0:P], x, start=True, stop=True)
                t.matmul(PS[:, 1, :], wqkv1[:, P:2 * P], x, start=True, stop=False)
                t.matmul(PS[:, 1, :], wqkv1[:, 2 * P:3 * P], x, start=False, stop=True).then_inc(a1_qkv, 1)
                t.wait_ge(a1_kv, c + 1)
                t.matmul(PS[:, 2, :], wlow[:, 0:P], KV, start=True, stop=True).then_inc(a1_lat, 1)
                t.wait_ge(a1_latc, c + 1)
                t.matmul(PS[:, 3, :], wlow[:, P:2 * P], LAT, start=True, stop=True)
                for w in range(CH // P):
                    mm = t.matmul(PS[:, 4, w * P:(w + 1) * P], LAT[:, w * P:(w + 1) * P], wlow[:, 2 * P:3 * P],
                                  start=True, stop=True, skip_group_check=True)
                mm.then_inc(a1_kr, 1)

        def a1_prep_act(a):
            with a.Fori(0, NCH) as c:
                a.wait_ge(a1_qkv, c + 1)
                nc.scalar.copy(KV, PS[:, 1, :]).then_inc(a1_kv, 1)
                a.wait_ge(a1_lat, c + 1)
                nc.scalar.copy(LAT, PS[:, 2, :]).then_inc(a1_latc, 1)
                a.wait_ge(a1_scr_free, 16 * (c + 1))
                for v in range(4):
                    a.wait_ge(a1_ver, 4 * c + v + 1)
                    nc.scalar.copy(SPL[:, v, 0, :], V32[:, v, :]).then_inc(a1_hi, 1)
                for v in range(4):
                    a.wait_ge(a1_r1, 4 * c + v + 1)
                    nc.scalar.copy(SPL[:, v, 1, :], V32[:, v, :]).then_inc(a1_mid, 1)

        def a1_prep_dve(v):
            v.wait_ge(a1_tab, 48)
            with v.Fori(0, B) as b:
                for j in range(2):
                    c = b * 2 + j
                    v.wait_ge(a1_qkv, c + 1)
                    for n, tab in ((0, FALL), (1, RISE), (2, RISE), (3, FALL)):
                        v.wait_ge(a1_lo_free, 4 * c + n + 1)
                        if n == 2:
                            v.wait_ge(a1_kr, c + 1)
                        v.scalar_tensor_tensor(out=V32[:, n, :], in0=PS[:, 0 if n < 2 else 3, :],
                                               scalar=SCALE if n < 2 else 1.0, in1=tab[:, j * CH:(j + 1) * CH],
                                               op0=ALU.mult, op1=ALU.mult).then_inc(a1_ver, 1)
                    v.tensor_copy(XN[:, chunk(c)], PS[:, 4, :]).then_inc(a1_v, 1)
                    for n in range(4):
                        v.wait_ge(a1_hi, 4 * c + n + 1)
                        v.tensor_tensor(V32[:, n, :], V32[:, n, :], SPL[:, n, 0, :], ALU.subtract).then_inc(a1_r1, 1)

        def a1_prep_pool(g):
            g.wait_ge(x_ready, 1 + NCH * 4)
            for r in (32, 64):
                nc.gpsimd.memset(PK[r:r + 32].rearrange("p a g v s -> p (a g v s)").bitcast(F32), 0.0).then_inc(a1_zero, 1)
                g.wait_ge(a1_zero, r // 32)
            g.wait_ge(a1_zero, 2)
            for sl in range(2):
                nc.gpsimd.memset(PK[MROW:MROW + 2, sl, :, 2:4, :], -1.0).then_inc(a1_zero, 1)
            g.wait_ge(a1_zero, 4)
            nc.gpsimd.memset(VG[:, :, :, :, :].rearrange("p a k g d -> p (a k g d)"), 0.0).then_inc(a1_vg0, 1)
            g.wait_ge(a1_vg0, 1)
            for sl in range(2):
                nc.gpsimd.memset(VG[:, sl, :, :, HD:HD + 1], 1.0).then_inc(a1_vg0, 1)
            with g.Fori(0, NCH) as c:
                for v in range(4):
                    g.wait_ge(a1_mid, 4 * c + v + 1)
                    nc.gpsimd.tensor_tensor(SPL[:, v, 2, :], V32[:, v, :], SPL[:, v, 1, :],
                                            ALU.subtract).then_inc(a1_lo_free, 1)

        def a1_pool(g):
            a1_prep_pool(g)
            g.wait_ge(a1_v, 1 + NCH)
            g.wait_ge(a1_vg0, 3)
            with g.Fori(0, B) as b:
                with g.Fori(0, NG // 2) as i:
                    for sl in range(2):
                        n = b * NG + i * 2 + sl
                        g.wait_ge(pv_free, PV0 + NS * (n - 1))
                        src = XN[:, bass.ds(b * S, S)].rearrange("p (t a w) -> p t a w", t=NKT, a=NG)
                        src = src[:, :, bass.ds(i * 2 + sl, 1), :]
                        src = src.rearrange("p t a (g d) -> p t (a g) d", g=GH)
                        nc.gpsimd.tensor_copy(VG[:, sl, :, :, 0:HD], src).then_inc(vg_in, 1)

        def p1_tile_pe(t, n, sl, tt, turn):
            g, q = tt // NKT, tt % NKT
            if q == 0:
                t.wait_ge(pk_in[sl][g], 16 * PACKS * (turn + 1))
            t.wait_ge(p1_free, NT1 * n + tt + 1)
            bank = 4 + 2 * (tt % 2)
            edge = P * (q + 1)
            for half in range(2):
                lo, hi = half * CH, (half + 1) * CH
                for v, k0, k1 in ((0, lo, min(hi, edge)), (1, max(lo, edge), hi)):
                    if k0 < k1:
                        mm = t.matmul(PS[:, bank + half, k0 - lo:k1 - lo], PK[0:MROW, sl, g, v, q * P:(q + 1) * P],
                                      PK[0:MROW, sl, g, 2 + v, k0:k1], start=True, stop=True, skip_group_check=True)
            mm.then_inc(p1_s, 1)

        def p1_tile_dve(v, n, tt):
            q = tt % NKT
            bank = 4 + 2 * (tt % 2)
            v.wait_ge(p1_s, NT1 * n + tt + 1)
            apart(v)
            v.tensor_tensor_reduce(JUNK[:, tt % 2, :], PS[:, bank:bank + 2, :].rearrange("p a b -> p (a b)"),
                                   STRIP[:, S - P - q * P:2 * S - P - q * P], 1.0, -3.0e38, ALU.mult, ALU.max,
                                   MX[:, tt:tt + 1]).then_inc(p1_free, 1)

        def maxima_pe(t, n):
            t.wait_ge(p1_free, 2 + NT1 * (n + 1))
            t.wait_ge(dg_free, 1 + DG_PER * n)
            t.transpose(PS[:, 2, 0:P], MX, ident[:]).then_inc(m_t, 1)

        def maxima_dve(v, n):
            v.wait_ge(m_t, n + 1)
            v.tensor_copy(MH[0:NT1, 0, :], PS[0:NT1, 2, 0:P]).then_inc(m_h, 1)
            v.wait_ge(m_h, n + 1)
            v.tensor_tensor(MH[0:NT1, 1, :], PS[0:NT1, 2, 0:P], MH[0:NT1, 0, :], ALU.subtract).then_inc(m_l, 1)

        def segments(s):
            hf, kt = s // NKT, s % NKT
            q0, q1 = hf * CH, (hf + 1) * CH
            d0, d1 = kt * P, (kt + 1) * P
            out_, at = [], 0
            for v, a_, b_ in ((1, q0, min(q1, d0)), (0, max(q0, d1), q1)):
                if a_ < b_:
                    out_.append((v, at, a_, b_))
                    at += b_ - a_
            return out_, at

        def diag_pe(t, n, sl, s):
            kt = s % NKT
            t.wait_ge(dg_free, DG_PER * n + diag_index(s) + 1)
            for g in range(GH):
                mm = t.matmul(PS[:, 2, g * P:(g + 1) * P], PK[0:MROW, sl, g, 2, kt * P:(kt + 1) * P],
                              PK[0:MROW, sl, g, 0, kt * P:(kt + 1) * P], start=(g == 0), stop=False,
                              skip_group_check=True)
            mm.then_inc(dg_s, 1)

        def diag_max_pe(t, n, sl, s):
            kt = s % NKT
            t.wait_ge(dg_fix, DG_PER * n + diag_index(s) + 1)
            for g in range(GH):
                mm = t.matmul(PS[:, 2, g * P:(g + 1) * P], PK[MROW:MROW + 2, sl, g, 2, kt * P:(kt + 1) * P],
                              PK[MROW:MROW + 2, sl, g, 0, kt * P:(kt + 1) * P], start=False, stop=True,
                              skip_group_check=True)
            mm.then_inc(dg_m, 1)

        def scores_pe(t, n, sl, s, g):
            kt = s % NKT
            t.wait_ge(s_free, NS * GH * n + GH * s + g + 1)
            for v, at, a_, b_ in segments(s)[0]:
                mm = t.matmul(PS[:, g % 2, at:at + b_ - a_], PK[0:MROW + 2, sl, g, 2 + v, kt * P:(kt + 1) * P],
                              PK[0:MROW + 2, sl, g, v, a_:b_], start=True, stop=True, skip_group_check=True)
            mm.then_inc(s_s, 1)

        def pv_pe(t, n, sl, s):
            hf, kt = s // NKT, s % NKT
            t.wait_ge(s_free, 2 + NS * GH * n + GH * (s + 1))
            if is_diag(s):
                t.wait_ge(dg_free, 1 + DG_PER * n + diag_index(s) + 1)
            if kt == 0:
                t.wait_ge(o_free, 2 * n + hf + 1)
            for g in range(GH):
                vg = VG[:, sl, kt, g, :]
                parts = [(PT[:, s % 2, g, at:at + b_ - a_], a_, b_) for _, at, a_, b_ in segments(s)[0]]
                if is_diag(s):
                    parts.append((PD[:, diag_index(s) % 2, g * P:(g + 1) * P], kt * P, (kt + 1) * P))
                for m, (rhs, a_, b_) in enumerate(parts):
                    mm = t.matmul(PS[32 * g:32 * g + 32, 3, a_ - hf * CH:b_ - hf * CH], vg, rhs,
                                  start=(kt == 0 and m == 0), stop=(kt == NKT - 1), skip_group_check=True)
            mm.then_inc(pv_free, 1)

        def group_pe(t, n, sl, turn, last=False):
            t.wait_ge(pk_m, 32 * (n + 1))
            t.wait_ge(vg_in, n + 1)
            diag_pe(t, n, sl, 0)
            diag_max_pe(t, n, sl, 0)
            for s in range(NS):
                scores_pe(t, n, sl, s, 0)
                scores_pe(t, n, sl, s, 1)
                if is_diag(s + 1):
                    diag_pe(t, n, sl, s + 1)
                if not last:
                    p1_tile_pe(t, n + 1, 1 - sl, 2 * s, turn + sl)
                scores_pe(t, n, sl, s, 2)
                scores_pe(t, n, sl, s, 3)
                if s > 0:
                    pv_pe(t, n, sl, s - 1)
                if not last:
                    p1_tile_pe(t, n + 1, 1 - sl, 2 * s + 1, turn + sl)
                if is_diag(s + 1):
                    diag_max_pe(t, n, sl, s + 1)
            pv_pe(t, n, sl, NS - 1)
            if not last:
                maxima_pe(t, n + 1)

        def group_act(a, n):
            for s in range(NS):
                a.wait_ge(pv_free, PV0 + NS * n + s - 1)
                if is_diag(s):
                    a.wait_ge(dg_m, DG_PER * n + diag_index(s) + 1)
                    nc.scalar.activation(PD[:, diag_index(s) % 2, :], PS[:, 2, :], ACT.Exp).then_inc(dg_free, 1)
                w = segments(s)[1]
                for g in range(GH):
                    a.wait_ge(s_s, NS * GH * n + GH * s + g + 1)
                    nc.scalar.activation(PT[:, s % 2, g, 0:w], PS[:, g % 2, 0:w], ACT.Exp).then_inc(s_free, 1)
                if s == NKT:
                    half_out(a, n, 0)
            half_out(a, n, 1)

        def half_out(a, n, hf):
            a.wait_ge(pv_free, PV0 + NS * n + NKT * (hf + 1))
            apart(a)
            nc.scalar.copy(ON[:, bass.ds(n, 1), hf * CH:(hf + 1) * CH], PS[:, 3:4, :]).then_inc(o_free, 1)

        def group_dve(v, n, last=False):
            def fix(s):
                v.wait_ge(dg_s, DG_PER * n + diag_index(s) + 1)
                v.tensor_tensor(PS[:, 2, :], PS[:, 2, :], fixT[:], ALU.mult).then_inc(dg_fix, 1)
            fix(0)
            for s in range(NS):
                if is_diag(s + 1):
                    fix(s + 1)
                if not last:
                    p1_tile_dve(v, n + 1, 2 * s)
                    p1_tile_dve(v, n + 1, 2 * s + 1)
            if not last:
                maxima_dve(v, n + 1)

        def a1_pe(t):
            a1_prep_pe(t)
            for tt in range(NT1):
                p1_tile_pe(t, 0, 0, tt, 0)
            maxima_pe(t, 0)
            with t.Fori(0, NGRP // 2 - 1) as i:
                group_pe(t, i * 2, 0, i)
                group_pe(t, i * 2 + 1, 1, i)
            group_pe(t, NGRP - 2, 0, NGRP // 2 - 1)
            group_pe(t, NGRP - 1, 1, NGRP // 2 - 1, last=True)
            with t.Fori(0, B) as b:
                for hf in range(2):
                    c = b * 2 + hf
                    t.wait_ge(x_ready, 1 + NCH * 4 + c)
                    for a in range(NG):
                        t.wait_ge(o_free, 1 + 2 * NGRP)
                        t.wait_ge(a1_inv, NG * c + a + 1)
                        on = ON[:, bass.ds(b * NG + a, 1), hf * CH:(hf + 1) * CH]
                        t.matmul(PS[:, 4 + a % 2:5 + a % 2, :], spread[:], on, start=True, stop=True).then_inc(a1_bc, 1)
                        if a > 0:
                            out_project(t, b, hf, c, a - 1)
                    out_project(t, b, hf, c, NG - 1)

        def out_project(t, b, hf, c, a):
            t.wait_ge(a1_on, NG * c + a + 1)
            on = ON[:, bass.ds(b * NG + a, 1), hf * CH:(hf + 1) * CH]
            mm = t.matmul(PS[:, 6:7, :], wo1[:, a * P:(a + 1) * P], on, start=(a == 0), stop=(a == NG - 1))
            if a == NG - 1:
                mm.then_inc(a1_y, 1)

        def a1_act(a):
            a1_prep_act(a)
            with a.Fori(0, NGRP) as n:
                group_act(a, n)

        def a1_dve(v):
            v.memset(MX, 0.0).then_inc(preload, 1)
            a1_prep_dve(v)
            v.wait_ge(preload, 2)
            for tt in range(NT1):
                p1_tile_dve(v, 0, tt)
            maxima_dve(v, 0)
            with v.Fori(0, NGRP - 1) as n:
                group_dve(v, n)
            group_dve(v, NGRP - 1, last=True)
            with v.Fori(0, B) as b:
                for hf in range(2):
                    c = b * 2 + hf
                    for a in range(NG):
                        v.wait_ge(a1_bc, NG * c + a + 1)
                        v.reciprocal(RS[:, a % 2, :], PS[:, 4 + a % 2, :]).then_inc(a1_inv, 1)
                        v.wait_ge(a1_inv, 2 + NG * c + a + 1)
                        on = ON[:, bass.ds(b * NG + a, 1), hf * CH:(hf + 1) * CH]
                        v.tensor_tensor(on, on, RS[:, a % 2:a % 2 + 1, :], ALU.mult).then_inc(a1_on, 1)
                    v.wait_ge(a1_y, c + 1)
                    v.tensor_tensor(XR[:, chunk(c)], PS[:, 6, :], XR[:, chunk(c)], ALU.add).then_inc(x_ready, 1)

        def a1_sp(sp):
            sp.wait_ge(x_ready, 1 + NCH * 4)
            for dst, name in ((STRIP, "strip"), (FALL, "fall"), (RISE, "rise")):
                sp.dma_start(dst, W[name]).then_inc(a1_tab, 16)
            with sp.Fori(0, B) as b:
                for j in range(2):
                    c = b * 2 + j
                    sp.wait_ge(a1_lo_free, 4 + 4 * (c + 1))
                    dst = scr[:, :, bass.ds(b, 1), :, j * CH:(j + 1) * CH].rearrange("v k b p t -> p (v k b) t")
                    sp.dma_start(dst, SPL.rearrange("p v k t -> p (v k) t")).then_inc(a1_scr_free, 16)
            sp.wait_ge(a1_scr_free, 16 * (1 + NCH))
            sp.wait_ge(a1_zero, 4)

            def packs(n, sl):
                for g in range(GH):
                    for side, orders in ((0, ((0, 3, 0), (1, 2, 3), (2, 1, 5))), (2, ((None, 3, 0), (None, 2, 3), (None, 1, 5)))):
                        for piece, reps, at in orders:
                            rows = slice(at * HD, (at + reps) * HD)
                            for v in (side, side + 1):
                                if piece is None:
                                    src = scr_heads[v, 0:reps, bass.ds(n, 1), g].rearrange("k n d t -> (k n) d t")
                                else:
                                    src = scr_heads[v, piece:piece + 1, bass.ds(n, 1), g].rearrange(
                                        "k n d t -> (k n) d t").broadcast_to((reps, HD, S))
                                sp.dma_start(PK[rows, sl, g, v, :], src).then_inc(pk_in[sl][g], 16)

            def maxima(n, sl):
                sp.wait_ge(m_l, n + 1)
                for k in range(2):
                    sp.dma_start(mscr[bass.ds(n * 2 + k, 1)].rearrange("n g (t q) -> (n g t) q", q=P),
                                 MH[0:NT1, k, :]).then_inc(m_w, 16)
                sp.wait_ge(m_w, 32 * (n + 1))
                for v in range(2):
                    sp.dma_start(PK[MROW:MROW + 2, sl, :, v, :], mscr[bass.ds(n * 2, 2)]).then_inc(pk_m, 16)

            packs(0, 0)
            packs(1, 1)
            maxima(0, 0)
            with sp.Fori(0, NGRP // 2 - 1) as i:
                maxima(i * 2 + 1, 1)
                sp.wait_ge(pv_free, PV0 + NS * (i * 2 + 1))
                packs(i * 2 + 2, 0)
                maxima(i * 2 + 2, 0)
                sp.wait_ge(pv_free, PV0 + NS * (i * 2 + 2))
                packs(i * 2 + 3, 1)
            maxima(NGRP - 1, 1)
        arena_at[0] = 0
        HN = place([TOK])
        XC = place([B, KW - 1 + S])
        XA, DT, DU, SZ, YY = place([TOK]), place([TOK]), place([TOK]), place([TOK]), place([TOK])
        SG, SS = place([TOK]), place([TOK])
        CV = place([2, CH])
        ESP = place([2, CH])
        BCP = place([3, TOK], BF16)
        BR = place([CH])
        DA, DBX, HH = place([4, CH]), place([2, CH]), place([4, CH])
        HC_ = place([4, CH])
        HL = place([DS])
        AN = place([DS])
        STT_, MV, GS = place([B, 2 * 6]), place([B, 2]), place([B, 8])
        m_norm = (HN, (mvec[:, 0:1], mvec[:, 1:2]))
        V_CW, V_CB, V_GG, V_GB, V_D, V_A = 2, 2 + KW, 3 + KW, 4 + KW, 5 + KW, 6 + KW
        m_p, m_x, m_gate, m_conv, m_silu = sem("m_p"), sem("m_x"), sem("m_gate"), sem("m_conv"), sem("m_silu")
        m_exp, m_sp, m_du, m_bc, m_an = sem("m_exp"), sem("m_sp"), sem("m_du"), sem("m_bc"), sem("m_an")
        m_done, m_pad = sem("m_done"), sem("m_pad")
        m_bb, m_cb, m_da, m_dbx, m_st, m_hc = (sem("m_bb"), sem("m_cb"), sem("m_da"), sem("m_dbx"), sem("m_st"), sem("m_hc"))
        m_hl, m_sy, m_y, m_gn, m_gt, m_gd, m_yn, m_out, m_tmp = (sem(f"m_{x}") for x in (
            "hl", "sy", "y", "gn", "gt", "gd", "yn", "out", "tmp"))

        def m_prep_pe(t):
            t.wait_ge(ln_free, ln_count(7, NCH - 1))
            with t.Fori(0, NCH) as c:
                t.wait_ge(m_done, c + 1)
                for n, bank in ((0, 0), (1, 1), (2, 2), (4, 3), (5, 4)):
                    mm = t.matmul(PS[:, bank, :], minT[:, n * P:(n + 1) * P], HN[:, chunk(c)], start=True, stop=True)
                mm.then_inc(m_p, 1)

        def m_prep_act(a):
            a.wait_ge(ln_free, ln_count(7, NCH - 1))
            nc.scalar.activation(AN, mvec[:, V_A:V_A + DS], ACT.Exp).then_inc(m_an, 1)
            a.wait_ge(m_pad, 1)
            with a.Fori(0, B) as b:
                for j in range(2):
                    c = b * 2 + j
                    a.wait_ge(m_p, c + 1)
                    apart(a)
                    nc.scalar.copy(XC[:, bass.ds(b, 1), KW - 1 + j * CH:KW - 1 + (j + 1) * CH], PS[:, 0:1, :]
                                   ).then_inc(m_x, 1)
                    nc.scalar.activation(SG[:, chunk(c)], PS[:, 4, :], ACT.Sigmoid).then_inc(m_gate, 1)
                    nc.scalar.activation(SZ[:, chunk(c)], PS[:, 1, :], ACT.Silu).then_inc(m_gate, 1)
                    a.wait_ge(m_conv, KW * (c + 1))
                    apart(a)
                    nc.scalar.activation(XA[:, chunk(c)], CV[:, 1, :], ACT.Silu).then_inc(m_silu, 1)
                    nc.scalar.activation(ESP[:, 0, :], PS[:, 2, :], ACT.Abs).then_inc(m_exp, 1)
                    a.wait_ge(m_exp, 3 * c + 1)
                    nc.scalar.activation(ESP[:, 1, :], ESP[:, 0, :], ACT.Exp, scale=-1.0).then_inc(m_exp, 1)
                    a.wait_ge(m_exp, 3 * c + 2)
                    nc.scalar.activation(ESP[:, 0, :], ESP[:, 1, :], ACT.Ln, bias=1.0).then_inc(m_exp, 1)

        def m_prep_dve(v):
            v.memset(XC[:, :, 0:KW - 1], 0.0).then_inc(m_pad, 1)
            v.wait_ge(m_an, 1)
            v.tensor_scalar(AN, AN, -1.0, None, ALU.mult).then_inc(m_an, 1)
            with v.Fori(0, B) as b:
                for j in range(2):
                    c = b * 2 + j
                    v.wait_ge(m_x, c + 1)
                    x = [XC[:, bass.ds(b, 1), k + j * CH:k + (j + 1) * CH].rearrange("p o t -> p (o t)") for k in range(KW)]
                    cv = [CV[:, k % 2, :] for k in range(KW)]
                    v.tensor_scalar(cv[0], x[0], mvec[:, V_CW:V_CW + 1], mvec[:, V_CB:V_CB + 1], ALU.mult,
                                    ALU.add).then_inc(m_conv, 1)
                    for k in range(1, KW):
                        v.wait_ge(m_conv, KW * c + k)
                        v.scalar_tensor_tensor(out=cv[k], in0=x[k], scalar=mvec[:, V_CW + k:V_CW + k + 1], in1=cv[k - 1],
                                               op0=ALU.mult, op1=ALU.add).then_inc(m_conv, 1)
                    v.tensor_copy(BCP[:, 0, chunk(c)], PS[:, 3, :]).then_inc(m_bc, 1)
                    v.wait_ge(m_bc, 4 * c + 1)
                    v.tensor_tensor(BR, PS[:, 3, :], BCP[:, 0, chunk(c)], ALU.subtract).then_inc(m_bc, 1)
                    v.wait_ge(m_bc, 4 * c + 2)
                    v.tensor_copy(BCP[:, 1, chunk(c)], BR).then_inc(m_bc, 1)
                    v.wait_ge(m_bc, 4 * c + 3)
                    v.tensor_tensor(BCP[:, 2, chunk(c)], BR, BCP[:, 1, chunk(c)], ALU.subtract).then_inc(m_bc, 1)
                    v.wait_ge(m_exp, 3 * c + 3)
                    v.scalar_tensor_tensor(out=DT[:, chunk(c)], in0=PS[:, 2, :], scalar=0.0, in1=ESP[:, 0, :],
                                           op0=ALU.max, op1=ALU.add).then_inc(m_du, 1)
                    v.wait_ge(m_du, c + 1)
                    v.wait_ge(m_silu, c + 1)
                    v.wait_ge(m_gate, 2 * c + 2)
                    v.wait_ge(m_bc, 4 * c + 4)
                    v.tensor_tensor(DU[:, chunk(c)], DT[:, chunk(c)], XA[:, chunk(c)], ALU.mult).then_inc(m_done, 1)

        def m_scan_pe(t):
            t.wait_ge(m_done, 1 + NCH)
            with t.Fori(0, NCH // 2) as i:
                for j in range(2):
                    c = i * 2 + j
                    for n in range(DS + 2):
                        u = DS * c + n
                        if n < DS:
                            t.wait_ge(m_dbx, u + 1)
                            for k in range(3):
                                mm = t.matmul(PS[:, n % 2, :], identb[:, n:n + 1].broadcast_to((P, P)),
                                              BCP[:, k, chunk(c)], start=(k == 0), stop=(k == 2))
                            mm.then_inc(m_bb, 1)
                            t.wait_ge(m_hc, u + 1)
                            for k in range(3):
                                mm = t.matmul(PS[:, 2 + n % 2, :], identb[:, DS + n:DS + n + 1].broadcast_to((P, P)),
                                              BCP[:, k, chunk(c)], start=(k == 0), stop=(k == 2))
                            mm.then_inc(m_cb, 1)
                        if n >= 2:
                            q = n - 2
                            uq = DS * c + q
                            if q == 0:
                                t.wait_ge(m_y, 2 * c + 2)
                            t.wait_ge(m_st, 4 + uq + 1)
                            t.matmul(PS[32 * (q % 4):32 * (q % 4) + 32, 5, :], statecol[:, (q // 4) * 32:(q // 4 + 1) * 32],
                                     HH[:, q % 4, :], start=(q < 4), stop=(q >= DS - 4), skip_group_check=True)
                            t.wait_ge(m_hc, 2 + uq + 1)
                            mm = t.matmul(PS[:, 4, :], ident[:], HC_[:, q % 4, :], start=(q == 0), stop=(q == DS - 1))
                            mm.then_inc(m_sy, 1)

        def m_scan_act(a):
            a.wait_ge(m_an, 2)
            a.wait_ge(m_done, 1 + NCH)
            with a.Fori(0, NCH // 2) as i:
                for j in range(2):
                    c = i * 2 + j
                    for n in range(DS):
                        u = DS * c + n
                        a.wait_ge(m_st, u + 1)
                        apart(a)
                        nc.scalar.activation(DA[:, n % 4, :], DT[:, chunk(c)], ACT.Exp, scale=AN[:, n:n + 1]
                                             ).then_inc(m_da, 1)

        def m_scan_dve(v):
            with v.Fori(0, NCH // 2) as i:
                for j in range(2):
                    c = i * 2 + j
                    for n in range(DS):
                        u = DS * c + n
                        v.wait_ge(m_bb, u + 1)
                        v.tensor_tensor(DBX[:, n % 2, :], DU[:, chunk(c)], PS[:, n % 2, :], ALU.mult).then_inc(m_dbx, 1)
                        v.wait_ge(m_dbx, 2 + u + 1)
                        v.wait_ge(m_da, u + 1)
                        v.wait_ge(m_sy, u + 1)
                        if j == 1:
                            v.wait_ge(m_hl, DS * i + n + 1)
                        v.tensor_tensor_scan(HH[:, n % 4, :], DA[:, n % 4, :], DBX[:, n % 2, :],
                                             0.0 if j == 0 else HL[:, n:n + 1], ALU.mult, ALU.add).then_inc(m_st, 1)
                        v.wait_ge(m_st, 4 + u + 1)
                        v.wait_ge(m_cb, u + 1)
                        v.tensor_tensor(HC_[:, n % 4, :], HH[:, n % 4, :], PS[:, 2 + n % 2, :], ALU.mult).then_inc(m_hc, 1)
                        if j == 0:
                            v.tensor_copy(HL[:, n:n + 1], HH[:, n % 3, CH - 1:CH]).then_inc(m_hl, 1)
                    v.wait_ge(m_sy, 4 + DS * (c + 1))
                    v.scalar_tensor_tensor(out=YY[:, chunk(c)], in0=XA[:, chunk(c)], scalar=mvec[:, V_D:V_D + 1],
                                           in1=PS[:, 4, :], op0=ALU.mult, op1=ALU.add).then_inc(m_y, 1)
                    v.tensor_tensor(SS[:, chunk(c)], SG[:, chunk(c)], PS[:, 5, :], ALU.mult).then_inc(m_y, 1)

        def m_tail_dve(v):
            v.wait_ge(m_y, 2 + 2 * NCH)
            for b in range(B):
                for j in range(2):
                    v.bn_stats(STT_[:, b, 6 * j:6 * j + 6], YY[:, (2 * b + j) * CH:(2 * b + j + 1) * CH]).then_inc(m_gn, 1)
                v.wait_ge(m_gn, 5 * b + 2)
                v.bn_aggr(MV[:, b, :], STT_[:, b, :]).then_inc(m_gn, 1)
                v.wait_ge(m_gn, 5 * b + 3)
                g = GS[:, b, :]
                v.tensor_tensor(g[:, 0:1], MV[:, b, 0:1], MV[:, b, 0:1], ALU.mult).then_inc(m_gn, 1)
                v.wait_ge(m_gn, 5 * b + 4)
                v.tensor_tensor(MV[:, b, 1:2], MV[:, b, 1:2], g[:, 0:1], ALU.add).then_inc(m_gn, 1)
            for b in range(B):
                g = GS[:, b, :]
                v.wait_ge(m_gt, b + 1)
                v.tensor_copy(g[:, 0:2], PS[:, 6 + b, 0:2]).then_inc(m_gd, 1)
                v.wait_ge(m_gd, 7 * b + 1)
                v.tensor_tensor(g[:, 2:3], g[:, 0:1], g[:, 0:1], ALU.mult).then_inc(m_gd, 1)
                v.wait_ge(m_gd, 7 * b + 2)
                v.tensor_tensor(g[:, 3:4], g[:, 1:2], g[:, 2:3], ALU.subtract).then_inc(m_gd, 1)
                v.wait_ge(m_gd, 7 * b + 4)
                v.reciprocal(g[:, 5:6], g[:, 4:5]).then_inc(m_gd, 1)
                v.wait_ge(m_gd, 7 * b + 5)
                v.tensor_tensor(g[:, 6:7], g[:, 5:6], mvec[:, V_GG:V_GG + 1], ALU.mult).then_inc(m_gd, 1)
                v.wait_ge(m_gd, 7 * b + 6)
                v.scalar_tensor_tensor(out=g[:, 7:8], in0=g[:, 0:1], scalar=g[:, 6:7], in1=mvec[:, V_GB:V_GB + 1],
                                       op0=ALU.mult, op1=ALU.subtract).then_inc(m_gd, 1)
                v.wait_ge(m_gd, 7 * b + 7)
                for j in range(2):
                    c = 2 * b + j
                    v.tensor_scalar(YY[:, chunk(c)], YY[:, chunk(c)], g[:, 6:7], g[:, 7:8], ALU.mult,
                                    ALU.subtract).then_inc(m_tmp, 1)
                    v.wait_ge(m_tmp, c + 1)
                    v.tensor_tensor(YY[:, chunk(c)], YY[:, chunk(c)], SZ[:, chunk(c)], ALU.mult).then_inc(m_yn, 1)
            for c in range(NCH):
                v.wait_ge(m_out, c + 1)
                v.tensor_tensor(CV[:, c % 2, :], PS[:, c % 4, :], XN[:, chunk(c)], ALU.add).then_inc(m_tmp, 1)
                v.wait_ge(m_tmp, NCH + c + 1)
                v.tensor_tensor(XR[:, chunk(c)], XR[:, chunk(c)], CV[:, c % 2, :], ALU.add).then_inc(x_ready, 1)

        def m_tail_act(a):
            for b in range(B):
                a.wait_ge(m_gd, 7 * b + 3)
                nc.scalar.activation(GS[:, b, 4:5], GS[:, b, 3:4], ACT.Sqrt, bias=eps_col[:]).then_inc(m_gd, 1)

        def m_tail_pe(t):
            for b in range(B):
                t.wait_ge(m_gn, 5 * (b + 1))
                t.matmul(PS[:, 6 + b, 0:2], groupmean[:], MV[:, b, :], start=True, stop=True).then_inc(m_gt, 1)
            for c in range(NCH):
                t.matmul(PS[:, c, :], minT[:, 3 * P:4 * P], HN[:, chunk(c)], start=True, stop=False)
                t.matmul(PS[:, c, :], mout[:, P:2 * P], SS[:, chunk(c)], start=False, stop=False)
                t.wait_ge(m_yn, c + 1)
                t.matmul(PS[:, c, :], mout[:, 0:P], YY[:, chunk(c)], start=False, stop=True).then_inc(m_out, 1)

        def m_pe(t):
            m_prep_pe(t)
            m_scan_pe(t)
            m_tail_pe(t)

        def m_act(a):
            m_prep_act(a)
            m_scan_act(a)
            m_tail_act(a)

        def m_dve(v):
            m_prep_dve(v)
            m_scan_dve(v)
            m_tail_dve(v)

        def m_pool(g):
            return
        PRELOADS = ((a1_lo_free, 4), (a1_v, 1), (a1_scr_free, 16), (p1_free, 2), (dg_free, 1), (s_free, 2), (pv_free, PV0),
                    (o_free, 1), (a1_inv, 2), (m_done, 1), (m_dbx, 2), (m_hc, 2), (m_st, 4), (m_sy, 4), (m_y, 2))
        out_done = sem("out_done")
        preload = sem("preload")

        block = ctx.enter_context(nc.Block())

        @block.sync
        def _(sp):
            sp.dma_start(XP[:], W["xT"]).then_inc(x_in, 16)
            for n, (t, name) in enumerate(loads):
                sp.dma_start(t if name in early_at else t[:], W[name]).then_inc(w_in if n < N_EARLY else w_late, 16)
            if last_stage > 4:
                a1_sp(sp)
            sp.wait_ge(x_ready, 1 + NCH * last_stage)
            sp.dma_start(out, (XR if last_stage > 1 else XP)[:]).then_inc(out_done, 16)
            sp.wait_ge(out_done, 16)

        @block.tensor
        def _(t):
            t.wait_ge(x_in, 16)
            t.wait_ge(w_in, 16 * N_EARLY)
            t.wait_ge(consts_ready, 4)
            ln_pe(t, 0, 0)
            a0_pe(t)
            if last_stage > 1:
                ln_pe(t, 1, 1, None, True)
                f0_pe(t, 0, 1)
            if last_stage > 2:
                ln_pe(t, 2, 2)
                b0_pe(t, 2)
            if last_stage > 3:
                ln_pe(t, 3, 3, None, True)
                f0_pe(t, 1, 3)
            if last_stage > 4:
                ln_pe(t, 4, 4)
                a1_pe(t)
            if last_stage > 5:
                ln_pe(t, 5, 5, None, True)
                f1_pe(t, 0, 5, 5)
            if last_stage > 6:
                ln_pe(t, 6, 6)
                ln_pe(t, 7, 6, XN)
                m_pe(t)
            if last_stage > 7:
                ln_pe(t, 8, 7, None, True)
                f1_pe(t, 1, 8, 7)

        @block.scalar
        def _(a):
            a.wait_ge(w_in, 16 * N_EARLY)
            nc.scalar.copy(identb[:], ident[:]).then_inc(consts_ready, 1)
            nc.scalar.copy(windowb[:], windowf).then_inc(consts_ready, 1)
            ln_act(a, 0)
            a0_act(a)
            if last_stage > 1:
                ln_act(a, 1)
                f0_act(a, 0)
            if last_stage > 2:
                ln_act(a, 2)
                b0_act(a)
            if last_stage > 3:
                ln_act(a, 3)
                f0_act(a, 1)
            if last_stage > 4:
                ln_act(a, 4)
                a1_act(a)
            if last_stage > 5:
                ln_act(a, 5)
                f1_act(a, 0)
            if last_stage > 6:
                ln_act(a, 6)
                ln_act(a, 7)
                m_act(a)
            if last_stage > 7:
                ln_act(a, 8)
                f1_act(a, 1)

        @block.vector
        def _(v):
            for at, (s, n) in enumerate(((x_ready, 1), (ln_rstd_free, 1), (ln_free, 2), (a0_kz_free, GH), (a0_s_free, 2),
                         (a0_e_free, 2), (a0_o_free, 2), (a0_bc_free, 1), (f0_h_free, 2), (f1_h_free, 2)) + PRELOADS):
                v.memset(tiny[:, at:at + 1], 0.0).then_inc(s, n)
            v.memset(eps_col[:], EPS).then_inc(consts_ready, 1)
            v.wait_ge(w_in, 16 * N_EARLY)
            v.wait_ge(x_in, 16)
            v.memset(VW, 0.0).then_inc(preload, 1)
            v.wait_ge(preload, 1)
            v.memset(VW[:, :, :, HD:HD + 1], 1.0).then_inc(a0_vw, 1)
            v.tensor_scalar(ffn0[:], ffn0i, QSCALE, None, ALU.mult).then_inc(consts_ready, 1)
            ln_dve(v, 0)
            a0_dve(v)
            if last_stage > 1:
                ln_dve(v, 1)
                f0_dve(v, 0, True)
            if last_stage > 2:
                ln_dve(v, 2)
                b0_dve(v)
            if last_stage > 3:
                ln_dve(v, 3)
                f0_dve(v, 1, False)
            if last_stage > 4:
                ln_dve(v, 4)
                a1_dve(v)
            if last_stage > 5:
                ln_dve(v, 5)
                f1_dve(v, 0)
            if last_stage > 6:
                ln_dve(v, 6)
                ln_dve(v, 7, *m_norm)
                m_dve(v)
            if last_stage > 7:
                ln_dve(v, 8)
                f1_dve(v, 1)

        @block.gpsimd
        def _(g):
            if last_stage > 4:
                a1_pool(g)
            if last_stage > 6:
                m_pool(g)


def pad_heads(w):
    n = w.shape[1]
    r = np.zeros((P, NG, n), w.dtype)
    for h in range(H):
        r[32 * (h % GH):32 * (h % GH) + HD, h // GH] = w[h * HD:(h + 1) * HD]
    return r.reshape(P, NG * n)


def kernel(**inputs):
    import concourse.bacc as bacc
    from concourse.bass_utils import run_bass_kernel_spmd as run

    i = {k: np.asarray(v) for k, v in inputs.items()}
    col = lambda a: a.reshape(-1, 1)
    w = shape_constants()
    w["xT"] = i["L0_attn_a_x"].reshape(B, S // 2, 2, P).transpose(3, 0, 2, 1).reshape(P, TOK)
    w["qkvT"] = i["L0_attn_a_qkv_w"].T
    w["bqk"] = i["L0_attn_a_qkv_b"][:2 * P].reshape(2, P).T
    w["bvrow"] = np.broadcast_to(i["L0_attn_a_qkv_b"][2 * P:], (P, P))
    w["wo0"], w["bo0"] = pad_heads(i["L0_attn_a_out_w"].T), col(i["L0_attn_a_out_b"])
    w["ffn0i"] = np.concatenate([i["L0_ffn_w_gate"].T, i["L0_ffn_w_up"].T,
                                 i["L0_ffn_w_down"].T.reshape(NJ0, P, P).transpose(1, 0, 2).reshape(P, HID0)], 1)
    w["winb"], w["binb"] = i["L0_attn_b_W_in"].T, i["L0_attn_b_b_in"].reshape(2, P).T
    w["wsT"], w["bs"] = i["L0_attn_b_W_s"].T, col(i["L0_attn_b_b_s"])
    w["woT"], w["bob"] = i["L0_attn_b_W_o"].T, col(i["L0_attn_b_b_o"])
    rows = lambda a: a.T.reshape(NJ1, P, -1).transpose(1, 0, 2).reshape(P, -1)
    w["w1T"], w["w2T"] = i["L1_ffn_w1_w"].T, i["L1_ffn_w2_w"].T
    w["h1T"], w["h2T"], w["w3T"] = rows(i["L1_ffn_h1_w"]), rows(i["L1_ffn_h2_w"]), rows(i["L1_ffn_w3_w"])
    w["scl"] = np.concatenate([i[f"L1_ffn_{n}_s"].reshape(-1, P).T for n in ("w1", "w2", "h1", "h2", "w3")], 1)
    w["wqkv1"] = np.concatenate([i[f"L1_attn_a_W_{n}"] for n in "qkv"], 1)
    DL = i["L1_attn_a_W_down_kv"].shape[1]
    low = np.zeros((P, 3, P), np.float32)
    low[:, 0, :DL], low[:DL, 1], low[:DL, 2] = (i["L1_attn_a_W_down_kv"], i["L1_attn_a_W_up_k"], i["L1_attn_a_W_up_v"])
    w["wlow"] = low.reshape(P, 3 * P)
    w["wo1"] = pad_heads(i["L1_attn_a_W_o"])
    inw = i["L1_attn_b_in_proj_w"]
    minT = np.zeros((P, 6, P), np.float32)
    for n in range(4):
        minT[:, n] = inw[n * P:(n + 1) * P].T
    minT[:, 4, :2 * DS] = inw[4 * P:4 * P + 2 * DS].T
    outw = i["L1_attn_b_out_proj_w"]
    mout = np.zeros((P, 2, P), np.float32)
    mout[:, 0] = outw[:, :P].T
    for n in range(DS):
        r = 32 * (n % 4) + n // 4
        minT[:, 5, r] = inw[4 * P + 2 * DS + n]
        mout[r, 1] = outw[:, P + n]
    w["minT"], w["mout"] = minT.reshape(P, -1), mout.reshape(P, -1)
    w["mvec"] = np.concatenate([col(i["L1_attn_b_ln_g"]), col(i["L1_attn_b_ln_b"]), i["L1_attn_b_conv_w"][:, 0],
                                col(i["L1_attn_b_conv_b"]), col(i["L1_attn_b_gn_g"]), col(i["L1_attn_b_gn_b"]),
                                col(i["L1_attn_b_D"]), i["L1_attn_b_A_log"]], 1)
    nc = bacc.Bacc("TRN2", target_bir_lowering=False, num_devices=1)
    w = {k: np.ascontiguousarray(v) for k, v in w.items()}
    aps = {k: nc.dram_tensor(k, v.shape, mybir.dt.from_np(v.dtype), kind="ExternalInput").ap() for k, v in w.items()}
    out = nc.dram_tensor("out_xT", (P, TOK), F32, kind="ExternalOutput").ap()
    build(nc, aps, out)
    r = run(nc, [w], core_ids=[0])
    return np.ascontiguousarray(r.results[0]["out_xT"].T.reshape(B, S, P))
```

```python
from contextlib import ExitStack

import numpy as np
import concourse.bass as bass
from concourse import mybir

F32 = mybir.dt.float32
BF16 = mybir.dt.bfloat16
I32 = mybir.dt.int32
U8 = mybir.dt.uint8
ALU = mybir.AluOpType
ACT = mybir.ActivationFunctionType
AX_X = mybir.AxisListType.X

P = 128
B, S = 2, 1024
TOK = B * S
CH = 512
NCH = TOK // CH
H, HD = 16, 8
GH = 4
NG = H // GH
EPS = 1e-5
NORM_EPS = 1e-6
WIN = 8
QT = P - 2 * WIN
NT0 = -(-CH // QT)
HID0, HID1 = 384, 512
NJ0, NJ1 = HID0 // P, HID1 // P
QSCALE = 1.0 / 127.0
DS, KW = 16, 4
NKT = S // P
LAMBDA = 0.01
KP = 48
MROW = 96
NGRP = B * NG
NEG = -1.0e30


def win_start(t):
    return min(max(QT * t - WIN, 0), CH - P)


def win_queries(t):
    return QT * t, min(QT * (t + 1), CH)


def shape_constants():
    p = np.arange(P)
    f = np.float32
    same = lambda w: (p[:, None] // w == p[None, :] // w).astype(f)
    c = {}
    c["center"] = (np.eye(P) - 1.0 / P).astype(f)
    c["mean"] = np.full((P, P), 1.0 / P, f)
    c["headsum"] = same(HD)
    c["groupmean"] = same(P // 8) / 16
    pick = np.zeros((P, NG, 2, NG, GH), f)
    for g in range(GH):
        for a in range(NG):
            pick[32 * g + HD, a, :, a, g] = 1
    c["pick"] = pick.reshape(P, NG * 32)
    c["ident"] = np.eye(P, dtype=f)
    c["headmask"] = (p[:, None] // HD == np.arange(H)[None, :]).astype(f)
    m = np.full((P, CH), NEG, f)
    for t in range(NT0):
        q0, q1 = win_queries(t)
        ok = np.abs(win_start(t) + p[:, None] - np.arange(q0, q1)[None, :]) <= WIN
        m[:, q0:q1][ok] = 0
    c["window"] = m
    oh = np.zeros((P, DS // 4, 32), f)
    for i in range(DS // 4):
        oh[:, i, i] = 1.0 / P
    c["statecol"] = oh.reshape(P, -1)
    t = np.arange(S, dtype=np.float64) - S // 2
    c["fall"] = np.tile(np.exp(-LAMBDA * t), (P, 1)).astype(f)
    c["rise"] = np.tile(np.exp(LAMBDA * t), (P, 1)).astype(f)
    i = p[:, None].astype(np.float64)
    strip = np.ones((P, 2 * S - P), f)
    strip[:, S - P:S] = np.exp(-2 * LAMBDA * np.maximum(p[None, :] - i, 0))
    c["strip"] = strip
    c["fixT"] = np.tile(np.exp(-2 * LAMBDA * np.maximum(i - p[None, :], 0)), (1, GH)).astype(f)
    return c


def build(nc, W, out, last_stage=8):
    ctx = ExitStack()
    with ctx:
        def sb(name, shape, dt=F32):
            return ctx.enter_context(nc.sbuf_tensor(name, shape, dt))

        sems = {}

        def sem(name):
            if name not in sems:
                sems[name] = ctx.enter_context(nc.semaphore(name))
            return sems[name]

        PS = ctx.enter_context(nc.psum_tensor("PS", [P, 8, CH], F32))
        XP = sb("XP", [P, TOK])
        XR = sb("XR", [P, TOK])
        XN = sb("XN", [P, TOK])
        RS = sb("RS", [P, 2, CH])
        SQ = sb("SQ", [P, 2, CH])

        loads = []

        ARENA = 124 * 1024
        arena = sb("arena", [P, ARENA], U8)
        early_at = {"ffn0i": ARENA - 4 * 3 * HID0, "window": ARENA - 4 * (3 * HID0 + CH)}

        def load(name, width, dt=F32):
            if name in early_at:
                t = arena[:, early_at[name]:early_at[name] + 4 * width].bitcast(dt)
            else:
                t = sb("w_" + name, [P, width], dt)
            loads.append((t, name))
            return t

        center, mean = load("center", P), load("mean", P)
        qkvT = load("qkvT", 3 * P)
        bqk = load("bqk", 2)
        bvrow = load("bvrow", P)
        headsum, headmask = load("headsum", P), load("headmask", H)
        ident, pick = load("ident", P), load("pick", NG * 32)
        windowf = load("window", CH)
        wo0, bo0 = load("wo0", NG * P), load("bo0", 1)
        ffn0i = load("ffn0i", 3 * HID0, I32)
        winb, bin_ = load("winb", 2 * P), load("binb", 2)
        wsT, bs_ = load("wsT", P), load("bs", 1)
        woT, bo_ = load("woT", P), load("bob", 1)
        N_EARLY = len(loads)
        w1T, w2T = load("w1T", HID1), load("w2T", HID1)
        h1T, h2T = load("h1T", NJ1 * HID1), load("h2T", NJ1 * HID1)
        w3T = load("w3T", HID1)
        scl = load("scl", 4 * NJ1 + 1)
        wqkv1, wlow = load("wqkv1", 3 * P), load("wlow", 3 * P)
        wo1 = load("wo1", NG * P)
        fixT = load("fixT", GH * P)
        minT = load("minT", 6 * P)
        mout = load("mout", 2 * P)
        mvec = load("mvec", 2 + KW + 1 + 2 + 1 + DS)
        groupmean, statecol = load("groupmean", P), load("statecol", (DS // 4) * 32)
        identb = sb("identb", [P, P], BF16)
        windowb = sb("windowb", [P, CH], BF16)
        ffn0 = sb("ffn0", [P, 3 * HID0])
        tiny = sb("tiny", [P, 32])

        arena_at = [0]

        def place(free, dt=F32, at=None):
            size = int(np.prod(free)) * (2 if dt == BF16 else 4)
            if at is None:
                at = arena_at[0]
                arena_at[0] += size
            assert at + size <= ARENA, (at, size)
            v = arena[:, at:at + size].bitcast(dt)
            if len(free) == 2:
                v = v.rearrange("p (a b) -> p a b", a=free[0])
            if len(free) == 3:
                v = v.rearrange("p (a b c) -> p a b c", a=free[0], b=free[1])
            if len(free) == 4:
                v = v.rearrange("p (a b c d) -> p a b c d", a=free[0], b=free[1], c=free[2])
            return v

        def chunk(c, n=CH):
            return bass.ts(c, n)

        def pairs(eng, body):
            with eng.Fori(0, NCH // 2) as i:
                for j in range(2):
                    body(i * 2 + j, j)

        x_ready = sem("x_ready")
        eps_col = sb("eps_col", [P, 1])
        x_in, w_in, w_late = sem("x_in"), sem("w_in"), sem("w_late")
        consts_ready = sem("consts_ready")

        def apart(eng):
            eng.sem_inc(passed[eng.engine], 1)
        passed = {nc.scalar.engine: sem("passed_act"), nc.vector.engine: sem("passed_dve")}

        NW = CH // P
        ln_centered, ln_squared, ln_var = sem("ln_centered"), sem("ln_squared"), sem("ln_var")
        ln_moved, ln_inverse, ln_spread = sem("ln_moved"), sem("ln_inverse"), sem("ln_spread")
        ln_affine, ln_free = sem("ln_affine"), sem("ln_free")
        minus_half = sb("minus_half", [P, 2 * NW])
        VAR = sb("VAR", [P, 2, 2 * NW])

        def spread_column(t, out_, column):
            return t.transpose(out_, column.broadcast_to((P, P)), ident[:])

        def ln_count(k, c):
            return 2 + NCH * k + c + 1

        def ln_pe(t, k, stage, src=None, all_banks=False):
            src = src if src is not None else XP if stage < 2 else XR
            if all_banks:
                t.wait_ge(x_ready, 1 + NCH * stage)
            with t.Fori(0, NCH // 2) as i:
                for j in range(2):
                    c = i * 2 + j
                    if src is XN:
                        t.wait_ge(ln_free, ln_count(k - 1, 0) + c)
                    elif stage > 0:
                        t.wait_ge(x_ready, 2 + NCH * (stage - 1) + (i * 2 + 1 if stage == 2 else c))
                    t.wait_ge(ln_free, NCH * k + c + 1)
                    t.matmul(PS[:, 5 + j, :], center[:], src[:, chunk(c)], start=True,
                             stop=True).then_inc(ln_centered, 1)
                for j in range(2):
                    t.wait_ge(ln_squared, 2 * (NCH * k + i * 2 + j + 1))
                    for w in range(NW):
                        mm = t.matmul(PS[:, 7, NW * j + w:NW * j + w + 1], SQ[:, j, w * P:(w + 1) * P], mean[:, 0:1],
                                      start=True, stop=True, skip_group_check=True)
                    mm.then_inc(ln_var, 1)
                t.wait_ge(ln_inverse, NCH // 2 * k + i + 1)
                for j in range(2):
                    for w in range(NW):
                        mm = spread_column(t, PS[:, 5 + j, w * P:(w + 1) * P], VAR[:, 1, NW * j + w:NW * j + w + 1])
                    mm.then_inc(ln_spread, 1)

        def ln_act(a, k, dst=None):
            dst = XN if dst is None else dst

            def body(c, j):
                a.wait_ge(ln_centered, NCH * k + c + 1)
                nc.scalar.activation(SQ[:, j, :], PS[:, 5 + j, :], ACT.Square).then_inc(ln_squared, 1)
                nc.scalar.copy(dst[:, chunk(c)], PS[:, 5 + j, :]).then_inc(ln_squared, 1)
            pairs(a, body)

        def ln_pool(g, k):
            with g.Fori(0, NCH // 2) as i:
                g.wait_ge(ln_moved, NCH // 2 * k + i + 1)
                nc.gpsimd.tensor_tensor(VAR[:, 1, :], VAR[:, 0, :], minus_half[:], ALU.pow).then_inc(ln_inverse, 1)

        def ln_dve(v, k, dst=None, affine=None):
            dst = XN if dst is None else dst
            with v.Fori(0, NCH // 2) as i:
                v.wait_ge(ln_var, NCH * k + i * 2 + 2)
                v.tensor_scalar(VAR[:, 0, :], PS[:, 7, 0:2 * NW], EPS, None, ALU.add).then_inc(ln_moved, 1)
                for j in range(2):
                    c = i * 2 + j
                    v.wait_ge(ln_spread, NCH * k + c + 1)
                    if affine is None:
                        v.tensor_tensor(dst[:, chunk(c)], dst[:, chunk(c)], PS[:, 5 + j, :],
                                        ALU.mult).then_inc(ln_free, 1)
                    else:
                        v.scalar_tensor_tensor(out=dst[:, chunk(c)], in0=dst[:, chunk(c)], scalar=affine[0],
                                               in1=PS[:, 5 + j, :], op0=ALU.mult, op1=ALU.mult).then_inc(ln_affine, 1)
                        v.wait_ge(ln_affine, c + 1)
                        v.tensor_scalar(dst[:, chunk(c)], dst[:, chunk(c)], affine[1], None, ALU.add).then_inc(ln_free, 1)

        RSUM = sb("RSUM", [P, 1, P])

        def sums_pe(t, bank, src, done):
            for a in range(NG):
                for w in range(NW):
                    mm = t.matmul(PS[32 * w:32 * w + 32, bank, 0:P], pick[:, 32 * a:32 * a + 32], src(a)[:, w * P:(w + 1) * P],
                                  start=(a == 0), stop=(a == NG - 1), skip_group_check=True)
            mm.then_inc(done, 1)

        def spread_sums_pe(t, bank, a, rsum, done):
            for w in range(NW):
                for g in range(GH):
                    row = 32 * w + GH * a + g
                    mm = t.matmul(PS[32 * g:32 * g + 32, bank, w * P:(w + 1) * P],
                                  ident[:, row:row + 1].broadcast_to((P, 32)), rsum, start=True, stop=True,
                                  skip_group_check=True)
            mm.then_inc(done, 1)

        arena_at[0] = 0
        Q0, K0, QS, KS = place([CH]), place([CH]), place([CH]), place([CH])
        NQ, NK = place([CH]), place([CH])
        KZ = place([GH, CH])
        E0 = place([2, 2, CH])
        VW = place([NT0, H, 32])
        X0 = place([CH])
        OS = place([NG, CH])
        a0_qk, a0_v, a0_sq, a0_ssq = sem("a0_qk"), sem("a0_v"), sem("a0_sq"), sem("a0_ssq")
        a0_vw, a0_norm, a0_kn, a0_kz = sem("a0_vw"), sem("a0_norm"), sem("a0_kn"), sem("a0_kz")
        a0_kz_free, a0_s_free, a0_e_free = (sem("a0_kz_free"), sem("a0_s_free"), sem("a0_e_free"))
        a0_o_free, a0_bc, a0_sum, a0_rs = sem("a0_o_free"), sem("a0_bc"), sem("a0_sum"), sem("a0_rs")
        a0_root, a0_on, a0_y, a0_x = sem("a0_root"), sem("a0_on"), sem("a0_y"), sem("a0_x")
        SBANK = [0, 1, 6, 7]

        def a0_pe(t):
            t.wait_ge(ln_free, ln_count(0, NCH - 1))
            with t.Fori(0, NCH) as c:
                t.wait_ge(x_ready, c + 1)
                t.wait_ge(a0_x, c + 1)
                x = X0
                t.matmul(PS[:, 0, :], qkvT[:, 0:P], x, start=True, stop=True)
                t.matmul(PS[:, 1, :], qkvT[:, P:2 * P], x, start=True, stop=True).then_inc(a0_qk, 1)
                for w in range(NT0):
                    xw = X0[:, win_start(w):win_start(w) + P]
                    mm = t.matmul(PS[:, 2 + w // 4, (w % 4) * P:(w % 4 + 1) * P], xw, qkvT[:, 2 * P:3 * P],
                                  start=(w % 4 == 0), stop=(w % 4 == 3 or w == NT0 - 1), skip_group_check=True)
                mm.then_inc(a0_v, 1)
                t.wait_ge(a0_sq, c * 2 + 1)
                t.matmul(PS[:, 4, :], headsum[:], QS, start=True, stop=True).then_inc(a0_ssq, 1)
                t.wait_ge(a0_sq, c * 2 + 2)
                t.matmul(PS[:, 5, :], headsum[:], KS, start=True, stop=True).then_inc(a0_ssq, 1)
                t.wait_ge(a0_kn, c * 2 + 2)
                for hp in range(9):
                    if hp < 8:
                        t.wait_ge(a0_s_free, c * 8 + hp + 1)
                        for h in (2 * hp, 2 * hp + 1):
                            bank = SBANK[h % 4]
                            t.wait_ge(a0_kz, c * H + h + 1)
                            t.matmul(PS[:, bank, :], identb[:], windowb[:], start=True, stop=False,
                                     skip_group_check=True)
                            for w in range(NT0):
                                q0, q1 = win_queries(w)
                                mm = t.matmul(PS[:, bank, q0:q1], KZ[:, h % GH, win_start(w):win_start(w) + P],
                                              Q0[:, q0:q1], start=False, stop=True, skip_group_check=True)
                            mm.then_inc(a0_kz_free, 1)
                    if 1 <= hp <= 8:
                        pr = hp - 1
                        t.wait_ge(a0_s_free, c * 8 + pr + 1 + 2)
                        if pr % 2 == 0:
                            t.wait_ge(a0_o_free, c * NG + pr // 2 + 1)
                        if pr == 0:
                            t.wait_ge(a0_vw, c + 2)
                        for h in (2 * pr, 2 * pr + 1):
                            g = h % GH
                            for w in range(NT0):
                                q0, q1 = win_queries(w)
                                mm = t.matmul(PS[32 * g:32 * g + 32, 2 + (h // GH) % 2, q0:q1], VW[:, w, h, :],
                                              E0[:, pr % 2, h % 2, q0:q1], start=(w == 0), stop=(w == NT0 - 1),
                                              skip_group_check=True)
                        mm.then_inc(a0_e_free, 1)
                t.wait_ge(a0_o_free, c * NG + NG + 2)
                sums_pe(t, 4, lambda a: OS[:, a, :], a0_sum)
                t.wait_ge(a0_rs, c + 1)
                for a in range(NG + 1):
                    if a < NG:
                        t.wait_ge(a0_on, 2 + c * NG + a - 1)
                        spread_sums_pe(t, 6 + a % 2, a, RSUM[:, 0, :], a0_bc)
                    if a > 0:
                        t.wait_ge(a0_on, 2 + c * NG + a)
                        mm = t.matmul(PS[:, 5, :], wo0[:, (a - 1) * P:a * P], OS[:, a - 1, :], start=(a == 1), stop=(a == NG))
                mm.then_inc(a0_y, 1)

        def a0_act(a):
            with a.Fori(0, NCH) as c:
                a.wait_ge(ln_free, ln_count(0, 0) + c)
                apart(a)
                nc.scalar.copy(X0, XN[:, chunk(c)]).then_inc(a0_x, 1)
                a.wait_ge(a0_qk, c + 1)
                nc.scalar.activation(QS, PS[:, 0, :], ACT.Square, bias=bqk[:, 0:1]).then_inc(a0_sq, 1)
                nc.scalar.activation(KS, PS[:, 1, :], ACT.Square, bias=bqk[:, 1:2]).then_inc(a0_sq, 1)
                for n, nrm in enumerate((NQ, NK)):
                    a.wait_ge(a0_ssq, c * 2 + n + 1)
                    nc.scalar.activation(nrm, PS[:, 4 + n, :], ACT.Sqrt).then_inc(a0_root, 1)
                for pr in range(8):
                    a.wait_ge(a0_kz_free, GH + c * H + 2 * pr + 2)
                    a.wait_ge(a0_e_free, c * 8 + pr + 1)
                    b0 = SBANK[(2 * pr) % 4]
                    nc.scalar.activation(E0[:, pr % 2, :, :], PS[:, b0:b0 + 2, :], ACT.Exp).then_inc(a0_s_free, 1)

        def a0_dve(v):
            with v.Fori(0, NCH) as c:
                v.wait_ge(a0_v, c + 1)
                v.tensor_tensor(VW[:, 0:4, :, 0:HD], PS[:, 2, :].rearrange("p (w h d) -> p w h d", w=4, h=H),
                                bvrow[:].rearrange("p (w h d) -> p w h d", w=1, h=H).broadcast_to((P, 4, H, HD)),
                                ALU.add)
                v.tensor_tensor(VW[:, 4, :, 0:HD], PS[:, 3, 0:P].rearrange("p (h d) -> p h d", h=H),
                                bvrow[:].rearrange("p (h d) -> p h d", h=H), ALU.add).then_inc(a0_vw, 1)
                for n, (raw, nrm, bank) in enumerate(((Q0, NQ, 0), (K0, NK, 1))):
                    v.wait_ge(a0_root, c * 2 + n + 1)
                    v.tensor_scalar(nrm, nrm, NORM_EPS, None, ALU.add).then_inc(a0_norm, 1)
                    v.wait_ge(a0_norm, c * 4 + 2 * n + 1)
                    v.reciprocal(nrm, nrm).then_inc(a0_norm, 1)
                    v.wait_ge(a0_norm, c * 4 + 2 * n + 2)
                    v.scalar_tensor_tensor(out=raw, in0=PS[:, bank, :], scalar=bqk[:, n:n + 1], in1=nrm, op0=ALU.add,
                                           op1=ALU.mult).then_inc(a0_kn, 1)
                v.wait_ge(a0_kn, c * 2 + 2)

                def kz(h):
                    v.wait_ge(a0_kz_free, c * H + h + 1)
                    v.tensor_scalar(KZ[:, h % GH, :], K0, headmask[:, h:h + 1], None, ALU.mult).then_inc(a0_kz, 1)

                def take_o(a):
                    v.wait_ge(a0_e_free, 2 + c * 8 + 2 * a + 2)
                    v.tensor_copy(OS[:, a, :], PS[:, 2 + a % 2, :]).then_inc(a0_o_free, 1)

                def norm_o(a):
                    v.wait_ge(a0_bc, c * NG + a + 1)
                    v.tensor_tensor(OS[:, a, :], OS[:, a, :], PS[:, 6 + a % 2, :], ALU.mult).then_inc(a0_on, 1)

                for h in range(GH):
                    kz(h)
                for hp in range(2, 9):
                    if hp < 8:
                        kz(2 * hp)
                        kz(2 * hp + 1)
                    if hp % 2 == 0:
                        take_o((hp - 2) // 2)
                v.wait_ge(a0_sum, c + 1)
                v.reciprocal(RSUM[:, 0, :], PS[:, 4, 0:P]).then_inc(a0_rs, 1)
                for a in range(NG):
                    norm_o(a)
                v.wait_ge(a0_y, c + 1)
                v.scalar_tensor_tensor(out=XP[:, chunk(c)], in0=PS[:, 5, :], scalar=bo0[:, 0:1], in1=XP[:, chunk(c)],
                                       op0=ALU.add, op1=ALU.add).then_inc(x_ready, 1)

        arena_at[0] = 0
        F0_SG, F0_H = place([2, CH]), place([2, NJ0, CH])
        f0_gu, f0_silu, f0_h_free, f0_y = sem("f0_gu"), sem("f0_silu"), sem("f0_h_free"), sem("f0_y")

        def f0_pe(t, use, k):
            def up(c, j):
                t.wait_ge(ln_free, ln_count(k, 0) + c)
                for b in range(NJ0):
                    m = NJ0 * NCH * use + NJ0 * c + b
                    r = (NJ0 * j + b) % 2
                    t.wait_ge(f0_h_free, m + 1)
                    x = XN[:, chunk(c)]
                    t.matmul(PS[:, r, :], ffn0[:, b * P:(b + 1) * P], x, start=True, stop=True)
                    t.matmul(PS[:, 2 + r, :], ffn0[:, HID0 + b * P:HID0 + (b + 1) * P], x, start=True,
                             stop=True).then_inc(f0_gu, 1)

            def down(c, j):
                t.wait_ge(f0_h_free, 2 + NJ0 * NCH * use + NJ0 * c + NJ0)
                stage = (1, 3)[use]
                t.wait_ge(x_ready, 1 + NCH * stage + c)
                for b in range(NJ0):
                    mm = t.matmul(PS[:, 4, :], ffn0[:, 2 * HID0 + b * P:2 * HID0 + (b + 1) * P], F0_H[:, j, b, :],
                                  start=(b == 0), stop=(b == NJ0 - 1))
                mm.then_inc(f0_y, 1)
            with t.Fori(0, NCH // 2) as i:
                up(i * 2, 0)
                up(i * 2 + 1, 1)
                down(i * 2, 0)
                down(i * 2 + 1, 1)

        def f0_act(a, use):
            def body(c, j):
                for b in range(NJ0):
                    m = NJ0 * NCH * use + NJ0 * c + b
                    r = (NJ0 * j + b) % 2
                    a.wait_ge(f0_gu, m + 1)
                    a.wait_ge(f0_h_free, m + 1)
                    nc.scalar.activation(F0_SG[:, r, :], PS[:, r, :], ACT.Silu).then_inc(f0_silu, 1)
            pairs(a, body)

        def f0_dve(v, use, natural):
            def up(c, j):
                for b in range(NJ0):
                    m = NJ0 * NCH * use + NJ0 * c + b
                    r = (NJ0 * j + b) % 2
                    v.wait_ge(f0_silu, m + 1)
                    v.tensor_tensor(F0_H[:, j, b, :], F0_SG[:, r, :], PS[:, 2 + r, :], ALU.mult).then_inc(f0_h_free, 1)

            def down(c, j):
                v.wait_ge(f0_y, NCH * use + c + 1)
                if natural:
                    dst = XR[:, bass.ds((c - j) * CH, S)].rearrange("p (a two) -> p a two", two=2)[:, :, j]
                    v.tensor_tensor(dst, PS[:, 4, :], XP[:, chunk(c)], ALU.add).then_inc(x_ready, 1)
                else:
                    v.tensor_tensor(XR[:, chunk(c)], PS[:, 4, :], XR[:, chunk(c)], ALU.add).then_inc(x_ready, 1)
            with v.Fori(0, NCH // 2) as i:
                up(i * 2, 0)
                up(i * 2 + 1, 1)
                down(i * 2, 0)
                down(i * 2 + 1, 1)

        arena_at[0] = 0
        XV, GT, SV, SA, SBB = place([2, CH]), place([2, CH]), place([2, CH]), place([2, CH]), place([2, CH])
        HS = place([2, CH])
        XS = place([2, CH])
        b0_gv, b0_gate, b0_val, b0_s, b0_sv = sem("b0_gv"), sem("b0_gate"), sem("b0_val"), sem("b0_s"), sem("b0_sv")
        b0_a, b0_b, b0_h, b0_y, b0_t = sem("b0_a"), sem("b0_b"), sem("b0_h"), sem("b0_y"), sem("b0_t")

        def b0_pe(t, k):
            t.wait_ge(ln_free, ln_count(k, NCH - 1))
            with t.Fori(0, NCH // 2) as i:
                for j in range(2):
                    c = i * 2 + j
                    t.wait_ge(x_ready, 1 + NCH * 2 + i * 2)
                    x = XN[:, chunk(c)]
                    t.matmul(PS[:, 4 * j, :], winb[:, 0:P], x, start=True, stop=True)
                    t.matmul(PS[:, 4 * j + 1, :], winb[:, P:2 * P], x, start=True, stop=True).then_inc(b0_gv, 1)
                for j in range(2):
                    c = i * 2 + j
                    t.wait_ge(b0_val, c + 1)
                    t.matmul(PS[:, 4 * j + 2, :], wsT[:], XV[:, j, :], start=True, stop=True).then_inc(b0_s, 1)
                for j in range(2):
                    c = i * 2 + j
                    t.wait_ge(b0_h, c + 1)
                    t.matmul(PS[:, 4 * j + 3, :], woT[:], HS[:, j, :], start=True, stop=True).then_inc(b0_y, 1)

        def b0_act(a):
            with a.Fori(0, NCH // 2) as i:
                for j in range(2):
                    c = i * 2 + j
                    a.wait_ge(b0_gv, c + 1)
                    nc.scalar.activation(GT[:, j, :], PS[:, 4 * j, :], ACT.Sigmoid, bias=bin_[:, 0:1]).then_inc(b0_gate, 1)
                for j in range(2):
                    c = i * 2 + j
                    a.wait_ge(b0_s, c + 1)
                    nc.scalar.activation(SV[:, j, :], PS[:, 4 * j + 2, :], ACT.Tanh, bias=bs_[:, 0:1]).then_inc(b0_sv, 1)

        def b0_dve(v):
            with v.Fori(0, NCH // 2) as i:
                for j in range(2):
                    c = i * 2 + j
                    v.wait_ge(b0_gv, c + 1)
                    v.tensor_scalar(XV[:, j, :], PS[:, 4 * j + 1, :], bin_[:, 1:2], None, ALU.add).then_inc(b0_val, 1)
                for j in range(2):
                    c = i * 2 + j
                    v.wait_ge(b0_gate, c + 1)
                    v.tensor_scalar(SA[:, j, :], GT[:, j, :], -1.0, 1.0, ALU.mult, ALU.add).then_inc(b0_a, 1)
                    v.wait_ge(b0_sv, c + 1)
                    v.tensor_tensor(SBB[:, j, :], GT[:, j, :], SV[:, j, :], ALU.mult).then_inc(b0_b, 1)
                    v.wait_ge(b0_a, c + 1)
                    v.wait_ge(b0_b, c + 1)
                    if j == 1:
                        v.wait_ge(b0_h, c)
                    v.tensor_tensor_scan(HS[:, j, :], SA[:, j, :], SBB[:, j, :],
                                         0.0 if j == 0 else HS[:, 0, CH - 1:CH], ALU.mult, ALU.add).then_inc(b0_h, 1)
                for j in range(2):
                    c = i * 2 + j
                    v.wait_ge(b0_y, c + 1)
                    v.scalar_tensor_tensor(out=XS[:, j, :], in0=PS[:, 4 * j + 3, :], scalar=bo_[:, 0:1],
                                           in1=XN[:, chunk(c)], op0=ALU.add, op1=ALU.add).then_inc(b0_t, 1)
                    v.wait_ge(b0_t, c + 1)
                    v.tensor_tensor(XR[:, chunk(c)], XR[:, chunk(c)], XS[:, j, :], ALU.add).then_inc(x_ready, 1)

        arena_at[0] = 0
        F1_SG, F1_H = place([2, CH]), [place([2, NJ1, CH]), place([2, NJ1, CH])]
        f1_gu, f1_silu, f1_h_free = sem("f1_gu"), sem("f1_silu"), sem("f1_h_free")
        f1_p, f1_g, f1_y = sem("f1_p"), sem("f1_g"), sem("f1_y")
        S_W1, S_W2, S_H1, S_H2, S_W3 = 0, NJ1, 2 * NJ1, 3 * NJ1, 4 * NJ1

        def f1_pe(t, use, k, stage):
            t.wait_ge(ln_free, ln_count(k, NCH - 1))
            t.wait_ge(w_late, 16 * (len(loads) - N_EARLY))
            with t.Fori(0, NCH // 2) as i:
                t.wait_ge(x_ready, 1 + NCH * stage + i * 2)
                for j in range(2):
                    c = i * 2 + j
                    x = XN[:, chunk(c)]
                    for b in range(NJ1):
                        t.wait_ge(f1_h_free, NJ1 * NCH * use + NJ1 * c + b + 1)
                        r = b % 2
                        t.matmul(PS[:, r, :], w1T[:, b * P:(b + 1) * P], x, start=True, stop=True)
                        t.matmul(PS[:, 2 + r, :], w2T[:, b * P:(b + 1) * P], x, start=True, stop=True).then_inc(f1_gu, 1)
                for layer, w in ((0, h1T), (1, h2T)):
                    for j in range(2):
                        c = i * 2 + j
                        if layer == 0:
                            t.wait_ge(f1_h_free, 2 + NJ1 * NCH * use + NJ1 * c + NJ1)
                            if j == 0:
                                t.wait_ge(f1_h_free, 2 + NJ1 * NCH * use + NJ1 * c + 2 * NJ1)
                        else:
                            t.wait_ge(f1_g, 2 * NJ1 * NCH * use + i * 4 * NJ1 + NJ1 * (j + 1))
                        for b in range(NJ1):
                            for kk in range(NJ1):
                                mm = t.matmul(PS[:, 4 * j + b, :], w[:, kk * HID1 + b * P:kk * HID1 + (b + 1) * P],
                                              F1_H[layer][:, j, kk, :], start=(kk == 0), stop=(kk == NJ1 - 1))
                            mm.then_inc(f1_p, 1)
                for j in range(2):
                    c = i * 2 + j
                    t.wait_ge(f1_g, 2 * NJ1 * NCH * use + i * 4 * NJ1 + 2 * NJ1 + NJ1 * (j + 1))
                    for kk in range(NJ1):
                        mm = t.matmul(PS[:, 4 * j, :], w3T[:, kk * P:(kk + 1) * P], F1_H[0][:, j, kk, :],
                                      start=(kk == 0), stop=(kk == NJ1 - 1))
                    mm.then_inc(f1_y, 1)

        def f1_act(a, use):
            with a.Fori(0, NCH // 2) as i:
                for j in range(2):
                    for b in range(NJ1):
                        m = NJ1 * NCH * use + NJ1 * (i * 2 + j) + b
                        a.wait_ge(f1_gu, m + 1)
                        a.wait_ge(f1_h_free, m + 1)
                        nc.scalar.activation(F1_SG[:, b % 2, :], PS[:, b % 2, :], ACT.Silu,
                                             scale=scl[:, S_W1 + b:S_W1 + b + 1]).then_inc(f1_silu, 1)
                for layer, s0 in ((0, S_H1), (1, S_H2)):
                    for j in range(2):
                        for b in range(NJ1):
                            m = 2 * NJ1 * NCH * use + i * 4 * NJ1 + layer * 2 * NJ1 + j * NJ1 + b
                            a.wait_ge(f1_p, m + 1)
                            nc.scalar.activation(F1_H[1 - layer][:, j, b, :], PS[:, 4 * j + b, :], ACT.Gelu,
                                                 scale=scl[:, s0 + b:s0 + b + 1]).then_inc(f1_g, 1)

        def f1_dve(v, use):
            with v.Fori(0, NCH // 2) as i:
                for j in range(2):
                    for b in range(NJ1):
                        m = NJ1 * NCH * use + NJ1 * (i * 2 + j) + b
                        v.wait_ge(f1_silu, m + 1)
                        v.scalar_tensor_tensor(out=F1_H[0][:, j, b, :], in0=PS[:, 2 + b % 2, :],
                                               scalar=scl[:, S_W2 + b:S_W2 + b + 1], in1=F1_SG[:, b % 2, :],
                                               op0=ALU.mult, op1=ALU.mult).then_inc(f1_h_free, 1)
                for j in range(2):
                    c = i * 2 + j
                    v.wait_ge(f1_y, NCH * use + c + 1)
                    v.scalar_tensor_tensor(out=XR[:, chunk(c)], in0=PS[:, 4 * j, :], scalar=scl[:, S_W3:S_W3 + 1],
                                           in1=XR[:, chunk(c)], op0=ALU.mult, op1=ALU.add).then_inc(x_ready, 1)
        arena_at[0] = 0
        ON = place([NGRP, S])
        PK = place([2, GH, 4, S], BF16)
        VG = place([2, NKT, GH, 32])
        PT = place([2, GH, CH])
        PD = place([2, GH * P])
        arena_at[0] = 0
        V32 = place([4, CH])
        SPL = place([4, 3, CH], BF16)
        KV, LAT = place([CH]), place([CH])
        FALL, RISE = place([S]), place([S])
        STRIP = XP[:, 0:2 * S - P]
        JUNK = RS[:].rearrange("p a b -> p (a b)").bitcast(BF16).rearrange("p (a b) -> p a b", a=2)
        MX = SQ[:, 0, 0:P]
        MH = SQ[:, 1, 0:P].bitcast(BF16).rearrange("p (k q) -> p k q", k=2)
        VT = XN[:].rearrange("p (t a g d) -> p t a g d", t=TOK // P, a=NG, g=GH)
        scr = nc.dram_tensor("scr", (2, 3, B, P, 2, S), BF16).ap()
        scr_heads = scr.rearrange("s k b (a g d) v t -> s k (b a) g d (v t)", a=NG, g=GH)
        mscr = nc.dram_tensor("mscr", (NGRP * 2, GH, S), BF16).ap()
        a1_qkv, a1_kv, a1_lat, a1_latc, a1_kr = sem("a1_qkv"), sem("a1_kv"), sem("a1_lat"), sem("a1_latc"), sem("a1_kr")
        a1_ver, a1_hi, a1_r1, a1_mid, a1_lo_free = sem("a1_ver"), sem("a1_hi"), sem("a1_r1"), sem("a1_mid"), sem("a1_lo_free")
        a1_v, a1_tab, a1_scr_free, a1_zero = sem("a1_v"), sem("a1_tab"), sem("a1_scr_free"), sem("a1_zero")
        pk_in = [[sem(f"pk_in{sl}{g}") for g in range(GH)] for sl in range(2)]
        pk_m, p1_s, p1_free = sem("pk_m"), sem("p1_s"), sem("p1_free")
        m_t, m_h, m_l, m_w = sem("m_t"), sem("m_h"), sem("m_l"), sem("m_w")
        dg_s, dg_fix, dg_m, dg_free = sem("dg_s"), sem("dg_fix"), sem("dg_m"), sem("dg_free")
        s_s, s_free, pv_free, o_free, vg_in = sem("s_s"), sem("s_free"), sem("pv_free"), sem("o_free"), sem("vg_in")
        a1_bc, a1_inv, a1_y, a1_vg0 = sem("a1_bc"), sem("a1_inv"), sem("a1_y"), sem("a1_vg0")
        a1_sum, a1_rs = sem("a1_sum"), sem("a1_rs")
        SCALE = 1.0 / float(np.sqrt(P))
        NT1 = GH * NKT
        NS = 2 * NKT
        PV0 = NS + 2
        DG_PER = NKT
        PACKS = 6

        def is_diag(s):
            return s < NS and s % NKT // (NKT // 2) == s // NKT

        def diag_index(s):
            return sum(is_diag(r) for r in range(s))

        def a1_prep_pe(t):
            t.wait_ge(ln_free, ln_count(4, NCH - 1))
            t.wait_ge(w_late, 16 * (len(loads) - N_EARLY))
            with t.Fori(0, NCH) as c:
                x = XN[:, chunk(c)]
                t.wait_ge(a1_v, c + 1)
                t.matmul(PS[:, 0, :], wqkv1[:, 0:P], x, start=True, stop=True)
                t.matmul(PS[:, 1, :], wqkv1[:, P:2 * P], x, start=True, stop=False)
                t.matmul(PS[:, 1, :], wqkv1[:, 2 * P:3 * P], x, start=False, stop=True).then_inc(a1_qkv, 1)
                t.wait_ge(a1_kv, c + 1)
                t.matmul(PS[:, 2, :], wlow[:, 0:P], KV, start=True, stop=True).then_inc(a1_lat, 1)
                t.wait_ge(a1_latc, c + 1)
                t.matmul(PS[:, 3, :], wlow[:, P:2 * P], LAT, start=True, stop=True)
                for w in range(CH // P):
                    mm = t.matmul(PS[:, 4, w * P:(w + 1) * P], LAT[:, w * P:(w + 1) * P], wlow[:, 2 * P:3 * P],
                                  start=True, stop=True, skip_group_check=True)
                mm.then_inc(a1_kr, 1)

        def a1_prep_act(a):
            def take_kv(c):
                a.wait_ge(a1_qkv, c + 1)
                nc.scalar.copy(KV, PS[:, 1, :]).then_inc(a1_kv, 1)

            def take_latent(c):
                a.wait_ge(a1_lat, c + 1)
                nc.scalar.copy(LAT, PS[:, 2, :]).then_inc(a1_latc, 1)

            def split(c, more=True):
                a.wait_ge(a1_scr_free, 64 * (c + 1))
                for v in range(4):
                    a.wait_ge(a1_ver, 4 * c + v + 1)
                    nc.scalar.copy(SPL[:, v, 0, :], V32[:, v, :]).then_inc(a1_hi, 1)
                if more:
                    take_kv(c + 1)
                for v in range(4):
                    a.wait_ge(a1_r1, 4 * c + v + 1)
                    nc.scalar.copy(SPL[:, v, 1, :], V32[:, v, :]).then_inc(a1_mid, 1)
                if more:
                    take_latent(c + 1)
            take_kv(0)
            take_latent(0)
            with a.Fori(0, NCH - 1) as c:
                split(c)
            split(NCH - 1, more=False)

        def a1_prep_dve(v):
            v.wait_ge(a1_tab, 48)
            with v.Fori(0, B) as b:
                for j in range(2):
                    c = b * 2 + j
                    v.wait_ge(a1_qkv, c + 1)
                    for n, tab in ((0, FALL), (1, RISE), (2, RISE), (3, FALL)):
                        v.wait_ge(a1_lo_free, 4 * c + n + 1)
                        if n == 2:
                            v.wait_ge(a1_kr, c + 1)
                        v.scalar_tensor_tensor(out=V32[:, n, :], in0=PS[:, 0 if n < 2 else 3, :],
                                               scalar=SCALE if n < 2 else 1.0, in1=tab[:, j * CH:(j + 1) * CH],
                                               op0=ALU.mult, op1=ALU.mult).then_inc(a1_ver, 1)
                    v.tensor_copy(XN[:, chunk(c)], PS[:, 4, :]).then_inc(a1_v, 1)
                    for n in range(4):
                        v.wait_ge(a1_hi, 4 * c + n + 1)
                        v.tensor_tensor(V32[:, n, :], V32[:, n, :], SPL[:, n, 0, :], ALU.subtract).then_inc(a1_r1, 1)

        def a1_zeros(g, r, norms):
            if r == 32:
                g.wait_ge(x_ready, 1 + NCH)
            g.wait_ge(ln_inverse, NCH // 2 * norms)
            nc.gpsimd.memset(PK[r:r + 32].rearrange("p a g v s -> p (a g v s)").bitcast(F32), 0.0).then_inc(a1_zero, 1)
            g.wait_ge(a1_zero, r // 32)

        def a1_ones(g):
            for sl in range(2):
                nc.gpsimd.memset(PK[MROW:MROW + 2, sl, :, 2:4, :], -1.0).then_inc(a1_zero, 1)
            g.wait_ge(a1_zero, 4)
            nc.gpsimd.memset(VG[:, :, :, :, :].rearrange("p a k g d -> p (a k g d)"), 0.0).then_inc(a1_vg0, 1)
            g.wait_ge(a1_vg0, 1)
            for sl in range(2):
                nc.gpsimd.memset(VG[:, sl, :, :, HD:HD + 1], 1.0).then_inc(a1_vg0, 1)
            g.wait_ge(a1_vg0, 3)

        def a1_prep_pool(g):
            g.wait_ge(ln_inverse, NCH // 2 * 5)
            with g.Fori(0, NCH) as c:
                for v in range(4):
                    g.wait_ge(a1_mid, 4 * c + v + 1)
                    nc.gpsimd.tensor_tensor(SPL[:, v, 2, :], V32[:, v, :], SPL[:, v, 1, :],
                                            ALU.subtract).then_inc(a1_lo_free, 1)

        def a1_pool(g):
            a1_prep_pool(g)
            g.wait_ge(a1_v, 1 + NCH)
            g.wait_ge(a1_vg0, 3)
            with g.Fori(0, B) as b:
                with g.Fori(0, NG // 2) as i:
                    for sl in range(2):
                        n = b * NG + i * 2 + sl
                        g.wait_ge(pv_free, PV0 + NS * (n - 1))
                        src = XN[:, bass.ds(b * S, S)].rearrange("p (t a w) -> p t a w", t=NKT, a=NG)
                        src = src[:, :, bass.ds(i * 2 + sl, 1), :]
                        src = src.rearrange("p t a (g d) -> p t (a g) d", g=GH)
                        nc.gpsimd.tensor_copy(VG[:, sl, :, :, 0:HD], src).then_inc(vg_in, 1)

        P1_FROM, P1_TO = 1, 14

        def p1_tiles(s):
            at = lambda k: min(max(k - P1_FROM, 0), P1_TO - P1_FROM) * NT1 // (P1_TO - P1_FROM)
            return range(at(s), at(s + 1))

        def p1_tile_pe(t, n, sl, tt, turn):
            g, q = tt // NKT, tt % NKT
            if q == 0:
                t.wait_ge(pk_in[sl][g], 16 * PACKS * (turn + 1))
            t.wait_ge(p1_free, NT1 * n + tt + 1)
            bank = 4 + 2 * (tt % 2)
            edge = P * (q + 1)
            for half in range(2):
                lo, hi = half * CH, (half + 1) * CH
                for v, k0, k1 in ((0, lo, min(hi, edge)), (1, max(lo, edge), hi)):
                    if k0 < k1:
                        mm = t.matmul(PS[:, bank + half, k0 - lo:k1 - lo], PK[0:MROW, sl, g, v, q * P:(q + 1) * P],
                                      PK[0:MROW, sl, g, 2 + v, k0:k1], start=True, stop=True, skip_group_check=True)
            mm.then_inc(p1_s, 1)

        def p1_tile_dve(v, n, tt):
            q = tt % NKT
            bank = 4 + 2 * (tt % 2)
            v.wait_ge(p1_s, NT1 * n + tt + 1)
            apart(v)
            v.tensor_tensor_reduce(JUNK[:, tt % 2, :], PS[:, bank:bank + 2, :].rearrange("p a b -> p (a b)"),
                                   STRIP[:, S - P - q * P:2 * S - P - q * P], 1.0, -3.0e38, ALU.mult, ALU.max,
                                   MX[:, tt:tt + 1]).then_inc(p1_free, 1)

        def maxima_pe(t, n):
            t.wait_ge(p1_free, 2 + NT1 * (n + 1))
            t.transpose(PS[:, 4, 0:P], MX, ident[:]).then_inc(m_t, 1)

        def maxima_dve(v, n):
            v.wait_ge(m_t, n + 1)
            v.tensor_copy(MH[0:NT1, 0, :], PS[0:NT1, 4, 0:P]).then_inc(m_h, 1)
            v.wait_ge(m_h, n + 1)
            v.tensor_tensor(MH[0:NT1, 1, :], PS[0:NT1, 4, 0:P], MH[0:NT1, 0, :], ALU.subtract).then_inc(m_l, 1)

        def segments(s):
            hf, kt = s // NKT, s % NKT
            q0, q1 = hf * CH, (hf + 1) * CH
            d0, d1 = kt * P, (kt + 1) * P
            out_, at = [], 0
            for v, a_, b_ in ((1, q0, min(q1, d0)), (0, max(q0, d1), q1)):
                if a_ < b_:
                    out_.append((v, at, a_, b_))
                    at += b_ - a_
            return out_, at

        def diag_pe(t, n, sl, s):
            kt = s % NKT
            t.wait_ge(dg_free, DG_PER * n + diag_index(s) + 1)
            for g in range(GH):
                mm = t.matmul(PS[:, 2, g * P:(g + 1) * P], PK[0:MROW, sl, g, 2, kt * P:(kt + 1) * P],
                              PK[0:MROW, sl, g, 0, kt * P:(kt + 1) * P], start=(g == 0), stop=False,
                              skip_group_check=True)
            mm.then_inc(dg_s, 1)

        def diag_max_pe(t, n, sl, s):
            kt = s % NKT
            t.wait_ge(dg_fix, DG_PER * n + diag_index(s) + 1)
            for g in range(GH):
                mm = t.matmul(PS[:, 2, g * P:(g + 1) * P], PK[MROW:MROW + 2, sl, g, 2, kt * P:(kt + 1) * P],
                              PK[MROW:MROW + 2, sl, g, 0, kt * P:(kt + 1) * P], start=False, stop=True,
                              skip_group_check=True)
            mm.then_inc(dg_m, 1)

        def scores_pe(t, n, sl, s, g):
            kt = s % NKT
            t.wait_ge(s_free, NS * GH * n + GH * s + g + 1)
            for v, at, a_, b_ in segments(s)[0]:
                mm = t.matmul(PS[:, g % 2, at:at + b_ - a_], PK[0:MROW + 2, sl, g, 2 + v, kt * P:(kt + 1) * P],
                              PK[0:MROW + 2, sl, g, v, a_:b_], start=True, stop=True, skip_group_check=True)
            mm.then_inc(s_s, 1)

        def pv_pe(t, n, sl, s):
            hf, kt = s // NKT, s % NKT
            t.wait_ge(s_free, 2 + NS * GH * n + GH * (s + 1))
            if is_diag(s):
                t.wait_ge(dg_free, 1 + DG_PER * n + diag_index(s) + 1)
            if kt == 0:
                t.wait_ge(o_free, 2 * n + hf + 1)
            for g in range(GH):
                vg = VG[:, sl, kt, g, :]
                parts = [(PT[:, s % 2, g, at:at + b_ - a_], a_, b_) for _, at, a_, b_ in segments(s)[0]]
                if is_diag(s):
                    parts.append((PD[:, diag_index(s) % 2, g * P:(g + 1) * P], kt * P, (kt + 1) * P))
                for m, (rhs, a_, b_) in enumerate(parts):
                    mm = t.matmul(PS[32 * g:32 * g + 32, 3, a_ - hf * CH:b_ - hf * CH], vg, rhs,
                                  start=(kt == 0 and m == 0), stop=(kt == NKT - 1), skip_group_check=True)
            mm.then_inc(pv_free, 1)

        def group_pe(t, n, sl, turn, last=False):
            t.wait_ge(pk_m, 32 * (n + 1))
            t.wait_ge(vg_in, n + 1)
            diag_max_pe(t, n, sl, 0)
            for s in range(NS):
                tiles = [] if last else list(p1_tiles(s))

                def p1():
                    if tiles:
                        p1_tile_pe(t, n + 1, 1 - sl, tiles.pop(0), turn + sl)
                scores_pe(t, n, sl, s, 0)
                scores_pe(t, n, sl, s, 1)
                if is_diag(s + 1):
                    diag_pe(t, n, sl, s + 1)
                p1()
                scores_pe(t, n, sl, s, 2)
                if len(tiles) > 1:
                    p1()
                scores_pe(t, n, sl, s, 3)
                if s == P1_TO and not last:
                    maxima_pe(t, n + 1)
                if s == NS - 1 and not last:
                    diag_pe(t, n + 1, 1 - sl, 0)
                if s > 0:
                    pv_pe(t, n, sl, s - 1)
                p1()
                if is_diag(s + 1):
                    diag_max_pe(t, n, sl, s + 1)
            pv_pe(t, n, sl, NS - 1)

        def group_act(a, n):
            for s in range(NS):
                a.wait_ge(pv_free, PV0 + NS * n + s - 1)
                if is_diag(s):
                    a.wait_ge(dg_m, DG_PER * n + diag_index(s) + 1)
                    nc.scalar.activation(PD[:, diag_index(s) % 2, :], PS[:, 2, :], ACT.Exp).then_inc(dg_free, 1)
                w = segments(s)[1]
                for g in range(GH):
                    a.wait_ge(s_s, NS * GH * n + GH * s + g + 1)
                    nc.scalar.activation(PT[:, s % 2, g, 0:w], PS[:, g % 2, 0:w], ACT.Exp).then_inc(s_free, 1)
                if s == NKT:
                    half_out(a, n, 0)
            half_out(a, n, 1)

        def half_out(a, n, hf):
            a.wait_ge(pv_free, PV0 + NS * n + NKT * (hf + 1))
            apart(a)
            nc.scalar.copy(ON[:, bass.ds(n, 1), hf * CH:(hf + 1) * CH], PS[:, 3:4, :]).then_inc(o_free, 1)

        def fix_dve(v, n, s):
            v.wait_ge(dg_s, DG_PER * n + diag_index(s) + 1)
            v.tensor_tensor(PS[:, 2, :], PS[:, 2, :], fixT[:], ALU.mult).then_inc(dg_fix, 1)

        def group_dve(v, n, last=False):
            for s in range(NS):
                if is_diag(s + 1):
                    fix_dve(v, n, s + 1)
                if not last:
                    for tt in p1_tiles(s):
                        p1_tile_dve(v, n + 1, tt)
                    if s == P1_TO:
                        maxima_dve(v, n + 1)
            if not last:
                fix_dve(v, n + 1, 0)

        def a1_pe(t):
            a1_prep_pe(t)
            for tt in range(NT1):
                p1_tile_pe(t, 0, 0, tt, 0)
            diag_pe(t, 0, 0, 0)
            maxima_pe(t, 0)
            with t.Fori(0, NGRP // 2 - 1) as i:
                group_pe(t, i * 2, 0, i)
                group_pe(t, i * 2 + 1, 1, i)
            group_pe(t, NGRP - 2, 0, NGRP // 2 - 1)
            group_pe(t, NGRP - 1, 1, NGRP // 2 - 1, last=True)
            t.wait_ge(o_free, 1 + 2 * NGRP)
            for b in range(B):
                for hf in range(2):
                    c = b * 2 + hf
                    t.wait_ge(x_ready, 1 + NCH * 4 + c)
                    sums_pe(t, 7, lambda a: ON[:, b * NG + a, hf * CH:(hf + 1) * CH], a1_sum)
                    t.wait_ge(a1_rs, c + 1)
                    for a in range(NG):
                        t.wait_ge(a1_inv, NG * c + a + 1)
                        spread_sums_pe(t, 4 + a % 2, a, RSUM[:, 0, :], a1_bc)
                        if a > 0:
                            out_project(t, b, hf, c, a - 1)
                    out_project(t, b, hf, c, NG - 1)

        def out_project(t, b, hf, c, a):
            t.wait_ge(a1_inv, 2 + NG * c + a + 1)
            on = ON[:, b * NG + a, hf * CH:(hf + 1) * CH]
            mm = t.matmul(PS[:, 6, :], wo1[:, a * P:(a + 1) * P], on, start=(a == 0), stop=(a == NG - 1))
            if a == NG - 1:
                mm.then_inc(a1_y, 1)

        def a1_act(a):
            a1_prep_act(a)
            with a.Fori(0, NGRP) as n:
                group_act(a, n)

        def a1_dve(v):
            v.memset(MX, 0.0).then_inc(preload, 1)
            a1_prep_dve(v)
            v.wait_ge(preload, 2)
            for tt in range(NT1):
                p1_tile_dve(v, 0, tt)
            fix_dve(v, 0, 0)
            maxima_dve(v, 0)
            with v.Fori(0, NGRP - 1) as n:
                group_dve(v, n)
            group_dve(v, NGRP - 1, last=True)
            with v.Fori(0, B) as b:
                for hf in range(2):
                    c = b * 2 + hf
                    v.wait_ge(a1_sum, c + 1)
                    v.reciprocal(RSUM[:, 0, :], PS[:, 7, 0:P]).then_inc(a1_rs, 1)
                    for a in range(NG):
                        v.wait_ge(a1_bc, NG * c + a + 1)
                        on = ON[:, bass.ds(b * NG + a, 1), hf * CH:(hf + 1) * CH]
                        v.tensor_tensor(on, on, PS[:, 4 + a % 2:5 + a % 2, :], ALU.mult).then_inc(a1_inv, 1)
                    v.wait_ge(a1_y, c + 1)
                    v.tensor_tensor(XR[:, chunk(c)], PS[:, 6, :], XR[:, chunk(c)], ALU.add).then_inc(x_ready, 1)

        def a1_sp(sp):
            sp.wait_ge(x_ready, 1 + NCH * 4)
            for dst, name in ((STRIP, "strip"), (FALL, "fall"), (RISE, "rise")):
                sp.dma_start(dst, W[name]).then_inc(a1_tab, 16)
            with sp.Fori(0, B) as b:
                for j in range(2):
                    c = b * 2 + j
                    for v in range(4):
                        sp.wait_ge(a1_lo_free, 4 + 4 * c + v + 1)
                        dst = scr[v // 2, :, bass.ds(b, 1), :, v % 2, j * CH:(j + 1) * CH].rearrange("k b p t -> p (k b) t")
                        sp.dma_start(dst, SPL[:, v, :, :]).then_inc(a1_scr_free, 16)
            sp.wait_ge(a1_scr_free, 64 * (1 + NCH))
            sp.wait_ge(a1_zero, 4)

            def packs(n, sl):
                for g in range(GH):
                    for side, orders in ((0, ((0, 3, 0), (1, 2, 3), (2, 1, 5))), (2, ((None, 3, 0), (None, 2, 3), (None, 1, 5)))):
                        for piece, reps, at in orders:
                            rows = slice(at * HD, (at + reps) * HD)
                            dst = PK[rows, sl, g, side:side + 2, :].rearrange("p v t -> p (v t)")
                            if piece is None:
                                src = scr_heads[side // 2, 0:reps, bass.ds(n, 1), g].rearrange("k n d t -> (k n) d t")
                            else:
                                src = scr_heads[side // 2, piece:piece + 1, bass.ds(n, 1), g].rearrange(
                                    "k n d t -> (k n) d t").broadcast_to((reps, HD, 2 * S))
                            sp.dma_start(dst, src).then_inc(pk_in[sl][g], 16)

            def maxima(n, sl):
                sp.wait_ge(m_l, n + 1)
                for k in range(2):
                    sp.dma_start(mscr[bass.ds(n * 2 + k, 1)].rearrange("n g (t q) -> (n g t) q", q=P),
                                 MH[0:NT1, k, :]).then_inc(m_w, 16)
                sp.wait_ge(m_w, 32 * (n + 1))
                for v in range(2):
                    sp.dma_start(PK[MROW:MROW + 2, sl, :, v, :], mscr[bass.ds(n * 2, 2)]).then_inc(pk_m, 16)

            packs(0, 0)
            packs(1, 1)
            maxima(0, 0)
            with sp.Fori(0, NGRP // 2 - 1) as i:
                maxima(i * 2 + 1, 1)
                sp.wait_ge(pv_free, PV0 + NS * (i * 2 + 1))
                packs(i * 2 + 2, 0)
                maxima(i * 2 + 2, 0)
                sp.wait_ge(pv_free, PV0 + NS * (i * 2 + 2))
                packs(i * 2 + 3, 1)
            maxima(NGRP - 1, 1)
        arena_at[0] = 0
        HN = place([TOK])
        XC = place([B, KW - 1 + S])
        XA, DT, DU, SZ, YY = place([TOK]), place([TOK]), place([TOK]), place([TOK]), place([TOK])
        SG, SS = place([TOK]), place([TOK])
        CV = place([2, CH])
        ESP = place([2, CH])
        BCP = place([3, TOK], BF16)
        BR = place([CH])
        DA, DBX, HH = place([4, CH]), place([2, CH]), place([4, CH])
        HC_ = place([4, CH])
        HL = place([DS])
        AN = place([DS])
        STT_, MV, GS = place([B, 2 * 6]), place([B, 2]), place([B, 8])
        m_norm = (HN, (mvec[:, 0:1], mvec[:, 1:2]))
        V_CW, V_CB, V_GG, V_GB, V_D, V_A = 2, 2 + KW, 3 + KW, 4 + KW, 5 + KW, 6 + KW
        m_p, m_x, m_gate, m_conv, m_silu = sem("m_p"), sem("m_x"), sem("m_gate"), sem("m_conv"), sem("m_silu")
        m_exp, m_sp, m_du, m_bc, m_an = sem("m_exp"), sem("m_sp"), sem("m_du"), sem("m_bc"), sem("m_an")
        m_done, m_pad = sem("m_done"), sem("m_pad")
        m_bb, m_cb, m_da, m_dbx, m_st, m_hc = (sem("m_bb"), sem("m_cb"), sem("m_da"), sem("m_dbx"), sem("m_st"), sem("m_hc"))
        m_hl, m_sy, m_y, m_gn, m_gt, m_gd, m_yn, m_out, m_tmp = (sem(f"m_{x}") for x in (
            "hl", "sy", "y", "gn", "gt", "gd", "yn", "out", "tmp"))

        def m_prep_pe(t):
            t.wait_ge(ln_free, ln_count(7, NCH - 1))
            with t.Fori(0, NCH) as c:
                t.wait_ge(m_done, c + 1)
                for n, bank in ((0, 0), (1, 1), (2, 2), (4, 3), (5, 4)):
                    mm = t.matmul(PS[:, bank, :], minT[:, n * P:(n + 1) * P], HN[:, chunk(c)], start=True, stop=True)
                mm.then_inc(m_p, 1)

        def m_prep_act(a):
            a.wait_ge(ln_free, ln_count(7, NCH - 1))
            nc.scalar.activation(AN, mvec[:, V_A:V_A + DS], ACT.Exp).then_inc(m_an, 1)
            a.wait_ge(m_pad, 1)
            with a.Fori(0, B) as b:
                for j in range(2):
                    c = b * 2 + j
                    a.wait_ge(m_p, c + 1)
                    apart(a)
                    nc.scalar.copy(XC[:, bass.ds(b, 1), KW - 1 + j * CH:KW - 1 + (j + 1) * CH], PS[:, 0:1, :]
                                   ).then_inc(m_x, 1)
                    nc.scalar.activation(SG[:, chunk(c)], PS[:, 4, :], ACT.Sigmoid).then_inc(m_gate, 1)
                    nc.scalar.activation(SZ[:, chunk(c)], PS[:, 1, :], ACT.Silu).then_inc(m_gate, 1)
                    a.wait_ge(m_conv, KW * (c + 1))
                    apart(a)
                    nc.scalar.activation(XA[:, chunk(c)], CV[:, 1, :], ACT.Silu).then_inc(m_silu, 1)
                    nc.scalar.activation(ESP[:, 0, :], PS[:, 2, :], ACT.Abs).then_inc(m_exp, 1)
                    a.wait_ge(m_exp, 3 * c + 1)
                    nc.scalar.activation(ESP[:, 1, :], ESP[:, 0, :], ACT.Exp, scale=-1.0).then_inc(m_exp, 1)
                    a.wait_ge(m_exp, 3 * c + 2)
                    nc.scalar.activation(ESP[:, 0, :], ESP[:, 1, :], ACT.Ln, bias=1.0).then_inc(m_exp, 1)

        def m_prep_dve(v):
            v.memset(XC[:, :, 0:KW - 1], 0.0).then_inc(m_pad, 1)
            v.wait_ge(m_an, 1)
            v.tensor_scalar(AN, AN, -1.0, None, ALU.mult).then_inc(m_an, 1)
            with v.Fori(0, B) as b:
                for j in range(2):
                    c = b * 2 + j
                    v.wait_ge(m_x, c + 1)
                    x = [XC[:, bass.ds(b, 1), k + j * CH:k + (j + 1) * CH].rearrange("p o t -> p (o t)") for k in range(KW)]
                    cv = [CV[:, k % 2, :] for k in range(KW)]
                    v.tensor_scalar(cv[0], x[0], mvec[:, V_CW:V_CW + 1], mvec[:, V_CB:V_CB + 1], ALU.mult,
                                    ALU.add).then_inc(m_conv, 1)
                    for k in range(1, KW):
                        v.wait_ge(m_conv, KW * c + k)
                        v.scalar_tensor_tensor(out=cv[k], in0=x[k], scalar=mvec[:, V_CW + k:V_CW + k + 1], in1=cv[k - 1],
                                               op0=ALU.mult, op1=ALU.add).then_inc(m_conv, 1)
                    v.tensor_copy(BCP[:, 0, chunk(c)], PS[:, 3, :]).then_inc(m_bc, 1)
                    v.wait_ge(m_bc, 4 * c + 1)
                    v.tensor_tensor(BR, PS[:, 3, :], BCP[:, 0, chunk(c)], ALU.subtract).then_inc(m_bc, 1)
                    v.wait_ge(m_bc, 4 * c + 2)
                    v.tensor_copy(BCP[:, 1, chunk(c)], BR).then_inc(m_bc, 1)
                    v.wait_ge(m_bc, 4 * c + 3)
                    v.tensor_tensor(BCP[:, 2, chunk(c)], BR, BCP[:, 1, chunk(c)], ALU.subtract).then_inc(m_bc, 1)
                    v.wait_ge(m_exp, 3 * c + 3)
                    v.scalar_tensor_tensor(out=DT[:, chunk(c)], in0=PS[:, 2, :], scalar=0.0, in1=ESP[:, 0, :],
                                           op0=ALU.max, op1=ALU.add).then_inc(m_du, 1)
                    v.wait_ge(m_du, c + 1)
                    v.wait_ge(m_silu, c + 1)
                    v.wait_ge(m_gate, 2 * c + 2)
                    v.wait_ge(m_bc, 4 * c + 4)
                    v.tensor_tensor(DU[:, chunk(c)], DT[:, chunk(c)], XA[:, chunk(c)], ALU.mult).then_inc(m_done, 1)

        def m_scan_pe(t):
            t.wait_ge(m_done, 1 + NCH)
            with t.Fori(0, NCH // 2) as i:
                for j in range(2):
                    c = i * 2 + j
                    for n in range(DS + 2):
                        u = DS * c + n
                        if n < DS:
                            t.wait_ge(m_dbx, u + 1)
                            for k in range(3):
                                mm = t.matmul(PS[:, n % 2, :], identb[:, n:n + 1].broadcast_to((P, P)),
                                              BCP[:, k, chunk(c)], start=(k == 0), stop=(k == 2))
                            mm.then_inc(m_bb, 1)
                            t.wait_ge(m_hc, u + 1)
                            for k in range(3):
                                mm = t.matmul(PS[:, 2 + n % 2, :], identb[:, DS + n:DS + n + 1].broadcast_to((P, P)),
                                              BCP[:, k, chunk(c)], start=(k == 0), stop=(k == 2))
                            mm.then_inc(m_cb, 1)
                        if n >= 2:
                            q = n - 2
                            uq = DS * c + q
                            if q == 0:
                                t.wait_ge(m_y, 2 * c + 2)
                            t.wait_ge(m_st, 4 + uq + 1)
                            t.matmul(PS[32 * (q % 4):32 * (q % 4) + 32, 5, :], statecol[:, (q // 4) * 32:(q // 4 + 1) * 32],
                                     HH[:, q % 4, :], start=(q < 4), stop=(q >= DS - 4), skip_group_check=True)
                            t.wait_ge(m_hc, 2 + uq + 1)
                            mm = t.matmul(PS[:, 4, :], ident[:], HC_[:, q % 4, :], start=(q == 0), stop=(q == DS - 1))
                            mm.then_inc(m_sy, 1)

        def m_scan_act(a):
            a.wait_ge(m_an, 2)
            a.wait_ge(m_done, 1 + NCH)
            with a.Fori(0, NCH // 2) as i:
                for j in range(2):
                    c = i * 2 + j
                    for n in range(DS):
                        u = DS * c + n
                        a.wait_ge(m_st, u + 1)
                        apart(a)
                        nc.scalar.activation(DA[:, n % 4, :], DT[:, chunk(c)], ACT.Exp, scale=AN[:, n:n + 1]
                                             ).then_inc(m_da, 1)

        def m_scan_dve(v):
            with v.Fori(0, NCH // 2) as i:
                for j in range(2):
                    c = i * 2 + j
                    for n in range(DS):
                        u = DS * c + n
                        v.wait_ge(m_bb, u + 1)
                        v.tensor_tensor(DBX[:, n % 2, :], DU[:, chunk(c)], PS[:, n % 2, :], ALU.mult).then_inc(m_dbx, 1)
                        v.wait_ge(m_dbx, 2 + u + 1)
                        v.wait_ge(m_da, u + 1)
                        v.wait_ge(m_sy, u + 1)
                        if j == 1:
                            v.wait_ge(m_hl, DS * i + n + 1)
                        v.tensor_tensor_scan(HH[:, n % 4, :], DA[:, n % 4, :], DBX[:, n % 2, :],
                                             0.0 if j == 0 else HL[:, n:n + 1], ALU.mult, ALU.add).then_inc(m_st, 1)
                        v.wait_ge(m_st, 4 + u + 1)
                        v.wait_ge(m_cb, u + 1)
                        v.tensor_tensor(HC_[:, n % 4, :], HH[:, n % 4, :], PS[:, 2 + n % 2, :], ALU.mult).then_inc(m_hc, 1)
                        if j == 0:
                            v.tensor_copy(HL[:, n:n + 1], HH[:, n % 3, CH - 1:CH]).then_inc(m_hl, 1)
                    v.wait_ge(m_sy, 4 + DS * (c + 1))
                    v.scalar_tensor_tensor(out=YY[:, chunk(c)], in0=XA[:, chunk(c)], scalar=mvec[:, V_D:V_D + 1],
                                           in1=PS[:, 4, :], op0=ALU.mult, op1=ALU.add).then_inc(m_y, 1)
                    v.tensor_tensor(SS[:, chunk(c)], SG[:, chunk(c)], PS[:, 5, :], ALU.mult).then_inc(m_y, 1)

        def m_tail_dve(v):
            v.wait_ge(m_y, 2 + 2 * NCH)
            for b in range(B):
                for j in range(2):
                    v.bn_stats(STT_[:, b, 6 * j:6 * j + 6], YY[:, (2 * b + j) * CH:(2 * b + j + 1) * CH]).then_inc(m_gn, 1)
                v.wait_ge(m_gn, 5 * b + 2)
                v.bn_aggr(MV[:, b, :], STT_[:, b, :]).then_inc(m_gn, 1)
                v.wait_ge(m_gn, 5 * b + 3)
                g = GS[:, b, :]
                v.tensor_tensor(g[:, 0:1], MV[:, b, 0:1], MV[:, b, 0:1], ALU.mult).then_inc(m_gn, 1)
                v.wait_ge(m_gn, 5 * b + 4)
                v.tensor_tensor(MV[:, b, 1:2], MV[:, b, 1:2], g[:, 0:1], ALU.add).then_inc(m_gn, 1)
            for b in range(B):
                g = GS[:, b, :]
                v.wait_ge(m_gt, b + 1)
                v.tensor_copy(g[:, 0:2], PS[:, 6 + b, 0:2]).then_inc(m_gd, 1)
                v.wait_ge(m_gd, 7 * b + 1)
                v.tensor_tensor(g[:, 2:3], g[:, 0:1], g[:, 0:1], ALU.mult).then_inc(m_gd, 1)
                v.wait_ge(m_gd, 7 * b + 2)
                v.tensor_tensor(g[:, 3:4], g[:, 1:2], g[:, 2:3], ALU.subtract).then_inc(m_gd, 1)
                v.wait_ge(m_gd, 7 * b + 4)
                v.reciprocal(g[:, 5:6], g[:, 4:5]).then_inc(m_gd, 1)
                v.wait_ge(m_gd, 7 * b + 5)
                v.tensor_tensor(g[:, 6:7], g[:, 5:6], mvec[:, V_GG:V_GG + 1], ALU.mult).then_inc(m_gd, 1)
                v.wait_ge(m_gd, 7 * b + 6)
                v.scalar_tensor_tensor(out=g[:, 7:8], in0=g[:, 0:1], scalar=g[:, 6:7], in1=mvec[:, V_GB:V_GB + 1],
                                       op0=ALU.mult, op1=ALU.subtract).then_inc(m_gd, 1)
                v.wait_ge(m_gd, 7 * b + 7)
                for j in range(2):
                    c = 2 * b + j
                    v.tensor_scalar(YY[:, chunk(c)], YY[:, chunk(c)], g[:, 6:7], g[:, 7:8], ALU.mult,
                                    ALU.subtract).then_inc(m_tmp, 1)
                    v.wait_ge(m_tmp, c + 1)
                    v.tensor_tensor(YY[:, chunk(c)], YY[:, chunk(c)], SZ[:, chunk(c)], ALU.mult).then_inc(m_yn, 1)
            for c in range(NCH):
                v.wait_ge(m_out, c + 1)
                v.tensor_tensor(CV[:, c % 2, :], PS[:, c % 4, :], XN[:, chunk(c)], ALU.add).then_inc(m_tmp, 1)
                v.wait_ge(m_tmp, NCH + c + 1)
                v.tensor_tensor(XR[:, chunk(c)], XR[:, chunk(c)], CV[:, c % 2, :], ALU.add).then_inc(x_ready, 1)

        def m_tail_act(a):
            for b in range(B):
                a.wait_ge(m_gd, 7 * b + 3)
                nc.scalar.activation(GS[:, b, 4:5], GS[:, b, 3:4], ACT.Sqrt, bias=eps_col[:]).then_inc(m_gd, 1)

        def m_tail_pe(t):
            for b in range(B):
                t.wait_ge(m_gn, 5 * (b + 1))
                t.matmul(PS[:, 6 + b, 0:2], groupmean[:], MV[:, b, :], start=True, stop=True).then_inc(m_gt, 1)
            for c in range(NCH):
                t.matmul(PS[:, c, :], minT[:, 3 * P:4 * P], HN[:, chunk(c)], start=True, stop=False)
                t.matmul(PS[:, c, :], mout[:, P:2 * P], SS[:, chunk(c)], start=False, stop=False)
                t.wait_ge(m_yn, c + 1)
                t.matmul(PS[:, c, :], mout[:, 0:P], YY[:, chunk(c)], start=False, stop=True).then_inc(m_out, 1)

        def m_pe(t):
            m_prep_pe(t)
            m_scan_pe(t)
            m_tail_pe(t)

        def m_act(a):
            m_prep_act(a)
            m_scan_act(a)
            m_tail_act(a)

        def m_dve(v):
            m_prep_dve(v)
            m_scan_dve(v)
            m_tail_dve(v)

        PRELOADS = ((a1_lo_free, 4), (a1_v, 1), (a1_scr_free, 64), (p1_free, 2), (dg_free, 1), (s_free, 2), (pv_free, PV0),
                    (o_free, 1), (a1_inv, 2), (m_done, 1), (m_dbx, 2), (m_hc, 2), (m_st, 4), (m_sy, 4), (m_y, 2))
        out_done = sem("out_done")
        preload = sem("preload")

        block = ctx.enter_context(nc.Block())

        @block.sync
        def _(sp):
            sp.dma_start(XP[:], W["xT"]).then_inc(x_in, 16)
            for n, (t, name) in enumerate(loads):
                sp.dma_start(t if name in early_at else t[:], W[name]).then_inc(w_in if n < N_EARLY else w_late, 16)
            if last_stage > 4:
                a1_sp(sp)
            sp.wait_ge(x_ready, 1 + NCH * last_stage)
            sp.dma_start(out, (XR if last_stage > 1 else XP)[:]).then_inc(out_done, 16)
            sp.wait_ge(out_done, 16)

        @block.tensor
        def _(t):
            t.wait_ge(x_in, 16)
            t.wait_ge(w_in, 16 * N_EARLY)
            t.wait_ge(consts_ready, 5)
            ln_pe(t, 0, 0)
            a0_pe(t)
            if last_stage > 1:
                ln_pe(t, 1, 1, None, True)
                f0_pe(t, 0, 1)
            if last_stage > 2:
                ln_pe(t, 2, 2)
                b0_pe(t, 2)
            if last_stage > 3:
                ln_pe(t, 3, 3, None, True)
                f0_pe(t, 1, 3)
            if last_stage > 4:
                ln_pe(t, 4, 4)
                a1_pe(t)
            if last_stage > 5:
                ln_pe(t, 5, 5, None, True)
                f1_pe(t, 0, 5, 5)
            if last_stage > 6:
                ln_pe(t, 6, 6)
                ln_pe(t, 7, 6, XN)
                m_pe(t)
            if last_stage > 7:
                ln_pe(t, 8, 7, None, True)
                f1_pe(t, 1, 8, 7)

        @block.scalar
        def _(a):
            a.wait_ge(w_in, 16 * N_EARLY)
            nc.scalar.copy(identb[:], ident[:]).then_inc(consts_ready, 1)
            nc.scalar.copy(windowb[:], windowf).then_inc(consts_ready, 1)
            ln_act(a, 0)
            a0_act(a)
            if last_stage > 1:
                ln_act(a, 1)
                f0_act(a, 0)
            if last_stage > 2:
                ln_act(a, 2)
                b0_act(a)
            if last_stage > 3:
                ln_act(a, 3)
                f0_act(a, 1)
            if last_stage > 4:
                ln_act(a, 4)
                a1_act(a)
            if last_stage > 5:
                ln_act(a, 5)
                f1_act(a, 0)
            if last_stage > 6:
                ln_act(a, 6)
                ln_act(a, 7, HN)
                m_act(a)
            if last_stage > 7:
                ln_act(a, 8)
                f1_act(a, 1)

        @block.vector
        def _(v):
            for at, (s, n) in enumerate(((x_ready, 1), (ln_free, 2), (a0_kz_free, GH), (a0_s_free, 2),
                         (a0_e_free, 2), (a0_o_free, 2), (a0_on, 2), (f0_h_free, 2), (f1_h_free, 2)) + PRELOADS):
                v.memset(tiny[:, at:at + 1], 0.0).then_inc(s, n)
            v.memset(eps_col[:], EPS).then_inc(consts_ready, 1)
            v.memset(minus_half[:], -0.5).then_inc(consts_ready, 1)
            v.wait_ge(w_in, 16 * N_EARLY)
            v.wait_ge(x_in, 16)
            v.memset(VW, 0.0).then_inc(preload, 1)
            v.wait_ge(preload, 1)
            v.memset(VW[:, :, :, HD:HD + 1], 1.0).then_inc(a0_vw, 1)
            v.tensor_scalar(ffn0[:], ffn0i, QSCALE, None, ALU.mult).then_inc(consts_ready, 1)
            ln_dve(v, 0)
            a0_dve(v)
            if last_stage > 1:
                ln_dve(v, 1)
                f0_dve(v, 0, True)
            if last_stage > 2:
                ln_dve(v, 2)
                b0_dve(v)
            if last_stage > 3:
                ln_dve(v, 3)
                f0_dve(v, 1, False)
            if last_stage > 4:
                ln_dve(v, 4)
                a1_dve(v)
            if last_stage > 5:
                ln_dve(v, 5)
                f1_dve(v, 0)
            if last_stage > 6:
                ln_dve(v, 6)
                ln_dve(v, 7, *m_norm)
                m_dve(v)
            if last_stage > 7:
                ln_dve(v, 8)
                f1_dve(v, 1)

        @block.gpsimd
        def _(g):
            g.wait_ge(consts_ready, 5)
            for k in range((1, 1, 2, 3, 4, 5, 6, 8, 9)[last_stage]):
                ln_pool(g, k)
                if last_stage > 4:
                    if k == 1:
                        a1_zeros(g, 32, 2)
                    if k == 3:
                        a1_zeros(g, 64, 4)
                        a1_ones(g)
                if k == 4:
                    a1_pool(g)


def pad_heads(w):
    n = w.shape[1]
    r = np.zeros((P, NG, n), w.dtype)
    for h in range(H):
        r[32 * (h % GH):32 * (h % GH) + HD, h // GH] = w[h * HD:(h + 1) * HD]
    return r.reshape(P, NG * n)


def kernel(**inputs):
    import concourse.bacc as bacc
    from concourse.bass_utils import run_bass_kernel_spmd as run

    i = {k: np.asarray(v) for k, v in inputs.items()}
    col = lambda a: a.reshape(-1, 1)
    w = shape_constants()
    w["xT"] = i["L0_attn_a_x"].reshape(B, S // 2, 2, P).transpose(3, 0, 2, 1).reshape(P, TOK)
    w["qkvT"] = i["L0_attn_a_qkv_w"].T
    w["bqk"] = i["L0_attn_a_qkv_b"][:2 * P].reshape(2, P).T
    w["bvrow"] = np.broadcast_to(i["L0_attn_a_qkv_b"][2 * P:], (P, P))
    w["wo0"], w["bo0"] = pad_heads(i["L0_attn_a_out_w"].T), col(i["L0_attn_a_out_b"])
    w["ffn0i"] = np.concatenate([i["L0_ffn_w_gate"].T, i["L0_ffn_w_up"].T,
                                 i["L0_ffn_w_down"].T.reshape(NJ0, P, P).transpose(1, 0, 2).reshape(P, HID0)], 1)
    w["winb"], w["binb"] = i["L0_attn_b_W_in"].T, i["L0_attn_b_b_in"].reshape(2, P).T
    w["wsT"], w["bs"] = i["L0_attn_b_W_s"].T, col(i["L0_attn_b_b_s"])
    w["woT"], w["bob"] = i["L0_attn_b_W_o"].T, col(i["L0_attn_b_b_o"])
    rows = lambda a: a.T.reshape(NJ1, P, -1).transpose(1, 0, 2).reshape(P, -1)
    w["w1T"], w["w2T"] = i["L1_ffn_w1_w"].T, i["L1_ffn_w2_w"].T
    w["h1T"], w["h2T"], w["w3T"] = rows(i["L1_ffn_h1_w"]), rows(i["L1_ffn_h2_w"]), rows(i["L1_ffn_w3_w"])
    w["scl"] = np.concatenate([i[f"L1_ffn_{n}_s"].reshape(-1, P).T for n in ("w1", "w2", "h1", "h2", "w3")], 1)
    w["wqkv1"] = np.concatenate([i[f"L1_attn_a_W_{n}"] for n in "qkv"], 1)
    DL = i["L1_attn_a_W_down_kv"].shape[1]
    low = np.zeros((P, 3, P), np.float32)
    low[:, 0, :DL], low[:DL, 1], low[:DL, 2] = (i["L1_attn_a_W_down_kv"], i["L1_attn_a_W_up_k"], i["L1_attn_a_W_up_v"])
    w["wlow"] = low.reshape(P, 3 * P)
    w["wo1"] = pad_heads(i["L1_attn_a_W_o"])
    inw = i["L1_attn_b_in_proj_w"]
    minT = np.zeros((P, 6, P), np.float32)
    for n in range(4):
        minT[:, n] = inw[n * P:(n + 1) * P].T
    minT[:, 4, :2 * DS] = inw[4 * P:4 * P + 2 * DS].T
    outw = i["L1_attn_b_out_proj_w"]
    mout = np.zeros((P, 2, P), np.float32)
    mout[:, 0] = outw[:, :P].T
    for n in range(DS):
        r = 32 * (n % 4) + n // 4
        minT[:, 5, r] = inw[4 * P + 2 * DS + n]
        mout[r, 1] = outw[:, P + n]
    w["minT"], w["mout"] = minT.reshape(P, -1), mout.reshape(P, -1)
    w["mvec"] = np.concatenate([col(i["L1_attn_b_ln_g"]), col(i["L1_attn_b_ln_b"]), i["L1_attn_b_conv_w"][:, 0],
                                col(i["L1_attn_b_conv_b"]), col(i["L1_attn_b_gn_g"]), col(i["L1_attn_b_gn_b"]),
                                col(i["L1_attn_b_D"]), i["L1_attn_b_A_log"]], 1)
    nc = bacc.Bacc("TRN2", target_bir_lowering=False, num_devices=1)
    w = {k: np.ascontiguousarray(v) for k, v in w.items()}
    aps = {k: nc.dram_tensor(k, v.shape, mybir.dt.from_np(v.dtype), kind="ExternalInput").ap() for k, v in w.items()}
    out = nc.dram_tensor("out_xT", (P, TOK), F32, kind="ExternalOutput").ap()
    build(nc, aps, out)
    r = run(nc, [w], core_ids=[0])
    return np.ascontiguousarray(r.results[0]["out_xT"].T.reshape(B, S, P))
```

```python
from contextlib import ExitStack

import numpy as np
import concourse.bass as bass
from concourse import mybir

F32 = mybir.dt.float32
BF16 = mybir.dt.bfloat16
I32 = mybir.dt.int32
U8 = mybir.dt.uint8
ALU = mybir.AluOpType
ACT = mybir.ActivationFunctionType

P = 128
B, S = 2, 1024
TOK = B * S
CH = 512
NCH = TOK // CH
H, HD = 16, 8
GH = 4
NG = H // GH
EPS = 1e-5
NORM_EPS = 1e-6
WIN = 8
QT = P - 2 * WIN
NT0 = -(-CH // QT)
HID0, HID1 = 384, 512
NJ0, NJ1 = HID0 // P, HID1 // P
QSCALE = 1.0 / 127.0
DS, KW = 16, 4
NKT = S // P
LAMBDA = 0.01
MROW = 96
NGRP = B * NG


def win_start(t):
    return min(max(QT * t - WIN, 0), CH - P)


def win_queries(t):
    return QT * t, min(QT * (t + 1), CH)


def shape_constants():
    p = np.arange(P)
    f = np.float32
    same = lambda w: (p[:, None] // w == p[None, :] // w).astype(f)
    c = {}
    c["center"] = (np.eye(P) - 1.0 / P).astype(f)
    c["mean"] = np.full((P, P), 1.0 / P, f)
    rows = np.zeros((2, P, 2 * H), f)
    for n in range(2):
        rows[n, :, n * H:(n + 1) * H] = p[:, None] // HD == np.arange(H)[None, :]
    c["normrows"] = rows.transpose(1, 0, 2).reshape(P, -1)
    back = np.zeros((CH // P, 2, P, P), f)
    for w in range(CH // P):
        back[w, :, 32 * w:32 * w + 32] = rows.transpose(0, 2, 1)
    c["normback"] = back.transpose(2, 0, 1, 3).reshape(P, -1)
    c["groupmean"] = same(P // 8) / 16
    pick = np.zeros((P, NG, 2, NG, GH), f)
    for g in range(GH):
        for a in range(NG):
            pick[32 * g + HD, a, :, a, g] = 1
    c["pick"] = pick.reshape(P, NG * 32)
    c["ident"] = np.eye(P, dtype=f)
    c["headmask"] = (p[:, None] // HD == np.arange(H)[None, :]).astype(f)
    m = np.zeros((P, CH), f)
    for t in range(NT0):
        q0, q1 = win_queries(t)
        ok = np.abs(win_start(t) + p[:, None] - np.arange(q0, q1)[None, :]) <= WIN
        m[:, q0:q1][ok] = 1
    c["window"] = m
    oh = np.zeros((P, DS // 4, 32), f)
    for i in range(DS // 4):
        oh[:, i, i] = 1.0 / P
    c["statecol"] = oh.reshape(P, -1)
    t = np.arange(S, dtype=np.float64) - S // 2
    c["fall"] = np.tile(np.exp(-LAMBDA * t), (P, 1)).astype(f)
    c["rise"] = np.tile(np.exp(LAMBDA * t), (P, 1)).astype(f)
    i = p[:, None].astype(np.float64)
    strip = np.ones((P, 2 * S - P), f)
    strip[:, S - P:S] = np.exp(-2 * LAMBDA * np.maximum(p[None, :] - i, 0))
    c["strip"] = strip
    c["fixT"] = np.tile(np.exp(-2 * LAMBDA * np.maximum(i - p[None, :], 0)), (1, GH)).astype(f)
    return c


def build(nc, W, out, last_stage=8):
    ctx = ExitStack()
    with ctx:
        def sb(name, shape, dt=F32):
            return ctx.enter_context(nc.sbuf_tensor(name, shape, dt))

        sems = {}

        def sem(name):
            if name not in sems:
                sems[name] = ctx.enter_context(nc.semaphore(name))
            return sems[name]

        PS = ctx.enter_context(nc.psum_tensor("PS", [P, 8, CH], F32))
        XP = sb("XP", [P, TOK])
        XR = sb("XR", [P, TOK])
        XN = sb("XN", [P, TOK])
        SQ = sb("SQ", [P, NCH, CH])

        loads = []

        ARENA = 124 * 1024
        PK_AT, PK_SIZE = NGRP * S * 4, 2 * GH * 4 * S * 2
        arena = sb("arena", [P, ARENA], U8)
        early_at = {"ffn0i": ARENA - 4 * 3 * HID0, "window": ARENA - 4 * (3 * HID0 + CH)}
        early_at["normback"] = early_at["window"] - 4 * 2 * CH

        def load(name, width, dt=F32):
            if name in early_at:
                t = arena[:, early_at[name]:early_at[name] + 4 * width].bitcast(dt)
            else:
                t = sb("w_" + name, [P, width], dt)
            loads.append((t, name))
            return t

        center, mean, ident = load("center", P), load("mean", P), load("ident", P)
        N_FIRST = len(loads)
        qkvT = load("qkvT", 3 * P)
        bqk = load("bqk", 2)
        bvrow = load("bvrow", P)
        normrows, headmask = load("normrows", 4 * H), load("headmask", H)
        pick = load("pick", NG * 32)
        normback = load("normback", 2 * CH)
        windowf = load("window", CH)
        wo0, bo0 = load("wo0", NG * P), load("bo0", 1)
        N_A0 = len(loads)
        ffn0i = load("ffn0i", 3 * HID0, I32)
        winb, bin_ = load("winb", 2 * P), load("binb", 2)
        wsT, bs_ = load("wsT", P), load("bs", 1)
        woT, bo_ = load("woT", P), load("bob", 1)
        N_EARLY = len(loads)
        w1T, w2T = load("w1T", HID1), load("w2T", HID1)
        h1T, h2T = load("h1T", NJ1 * HID1), load("h2T", NJ1 * HID1)
        w3T = load("w3T", HID1)
        scl = load("scl", 4 * NJ1 + 1)
        wqkv1, wlow = load("wqkv1", 3 * P), load("wlow", 3 * P)
        wo1 = load("wo1", NG * P)
        fixT = load("fixT", GH * P)
        minT = load("minT", 6 * P)
        mout = load("mout", 2 * P)
        mvec = load("mvec", 2 + KW + 1 + 2 + 1 + DS)
        groupmean, statecol = load("groupmean", P), load("statecol", (DS // 4) * 32)
        identb = sb("identb", [P, P], BF16)
        ffn0 = sb("ffn0", [P, 3 * HID0])
        started = sb("started", [P, 32])

        arena_at = [0]

        def place(free, dt=F32):
            size = int(np.prod(free)) * (2 if dt == BF16 else 4)
            at = arena_at[0]
            arena_at[0] += size
            assert at + size <= ARENA, (at, size)
            v = arena[:, at:at + size].bitcast(dt)
            if len(free) == 2:
                v = v.rearrange("p (a b) -> p a b", a=free[0])
            if len(free) == 3:
                v = v.rearrange("p (a b c) -> p a b c", a=free[0], b=free[1])
            if len(free) == 4:
                v = v.rearrange("p (a b c d) -> p a b c d", a=free[0], b=free[1], c=free[2])
            return v

        def chunk(c):
            return bass.ts(c, CH)

        def pairs(eng, body):
            with eng.Fori(0, NCH // 2) as i:
                for j in range(2):
                    body(i * 2 + j, j)

        x_ready = sem("x_ready")
        eps_col = sb("eps_col", [P, 1])
        x_in, w_first, w_a0, w_in, w_late = (sem(n) for n in ("x_in", "w_first", "w_a0", "w_in", "w_late"))
        consts_ready, ffn0_ready = sem("consts_ready"), sem("ffn0_ready")
        load_parts = ((w_first, 0, N_FIRST), (w_a0, N_FIRST, N_A0), (w_in, N_A0, N_EARLY), (w_late, N_EARLY, len(loads)))

        def wait_loads(eng, part):
            s, n0, n1 = load_parts[part]
            eng.wait_ge(s, 16 * (n1 - n0))

        def apart(eng):
            eng.sem_inc(passed[eng.engine], 1)
        passed = {nc.scalar.engine: sem("passed_act"), nc.vector.engine: sem("passed_dve")}

        NW = CH // P
        LN_BANKS = {k: (4, 5, 6, 7) for k in (0, 1, 3, 5, 7, 8)}
        LN_BANKS.update({2: (6, 7, 5, 4), 4: (6, 7, 5, 4), 6: (2, 3, 6, 7)})
        ln_centered, ln_squared, ln_copied, ln_var = sem("ln_centered"), sem("ln_squared"), sem("ln_copied"), sem("ln_var")
        ln_moved, ln_inverse, ln_spread = sem("ln_moved"), sem("ln_inverse"), sem("ln_spread")
        ln_affine, ln_free = sem("ln_affine"), sem("ln_free")
        minus_half = sb("minus_half", [P, 2 * NW])
        VAR = sb("VAR", [P, 2, 2, 2 * NW])

        def spread_column(t, out_, column):
            return t.transpose(out_, column.broadcast_to((P, P)), ident[:])

        def ln_count(k, c):
            return 1 + NCH * k + c + 1

        def ln_at(bank):
            return NW * (bank % 2)

        def ln_pe(t, k, stage, src=None):
            src = src if src is not None else XP if stage < 2 else XR
            for c, bank in enumerate(LN_BANKS[k]):
                if src is XN:
                    t.wait_ge(ln_free, ln_count(k - 1, c))
                elif stage > 0:
                    t.wait_ge(x_ready, 2 + NCH * (stage - 1) + (c // 2 * 2 + 1 if stage == 2 else c))
                t.matmul(PS[:, bank, :], center[:], src[:, c * CH:(c + 1) * CH], start=True,
                         stop=True).then_inc(ln_centered, 1)
            for c, bank in enumerate(LN_BANKS[k]):
                t.wait_ge(ln_squared, NCH * k + c + 1)
                t.wait_ge(ln_copied, NCH * k + c + 1)
                for w in range(NW):
                    mm = t.matmul(PS[:, bank, w:w + 1], SQ[:, c, w * P:(w + 1) * P], mean[:, 0:1],
                                  start=True, stop=True, skip_group_check=True)
                mm.then_inc(ln_var, 1)
            for c, bank in enumerate(LN_BANKS[k]):
                t.wait_ge(ln_inverse, 2 * k + c // 2 + 1)
                for w in range(NW):
                    at = ln_at(bank) + w
                    mm = spread_column(t, PS[:, bank, w * P:(w + 1) * P], VAR[:, 1, c // 2, at:at + 1])
                mm.then_inc(ln_spread, 1)

        def ln_act(a, k, dst=None):
            for c, bank in enumerate(LN_BANKS[k]):
                a.wait_ge(ln_centered, NCH * k + c + 1)
                nc.scalar.activation(SQ[:, c, :], PS[:, bank, :], ACT.Square).then_inc(ln_squared, 1)

        def ln_pool(g, k):
            for half in range(2):
                g.wait_ge(ln_moved, 2 * k + half + 1)
                if half == 1:
                    g.wait_ge(ln_inverse, 2 * k + 1)
                nc.gpsimd.tensor_tensor(VAR[:, 1, half, :], VAR[:, 0, half, :], minus_half[:], ALU.pow
                                        ).then_inc(ln_inverse, 1)

        def ln_dve(v, k, dst=None, affine=None):
            dst = XN if dst is None else dst

            def move(half):
                v.wait_ge(ln_var, NCH * k + 2 * half + 2)
                b0 = min(LN_BANKS[k][2 * half:2 * half + 2])
                v.tensor_scalar(VAR[:, 0, half, :].rearrange("p (b w) -> p b w", b=2), PS[:, b0:b0 + 2, 0:NW], EPS, None,
                                ALU.add).then_inc(ln_moved, 1)
            for c, bank in enumerate(LN_BANKS[k]):
                v.wait_ge(ln_squared, NCH * k + c + 1)
                v.tensor_copy(dst[:, c * CH:(c + 1) * CH], PS[:, bank, :]).then_inc(ln_copied, 1)
                if c % 2 == 1 and c > 1:
                    move(0)
            move(1)
            for c, bank in enumerate(LN_BANKS[k]):
                d = dst[:, c * CH:(c + 1) * CH]
                v.wait_ge(ln_copied, NCH * k + c + 1)
                v.wait_ge(ln_spread, NCH * k + c + 1)
                if affine is None:
                    v.tensor_tensor(d, d, PS[:, bank, :], ALU.mult).then_inc(ln_free, 1)
                else:
                    v.scalar_tensor_tensor(out=d, in0=d, scalar=affine[0], in1=PS[:, bank, :],
                                           op0=ALU.mult, op1=ALU.mult).then_inc(ln_affine, 1)
                    v.wait_ge(ln_affine, c + 1)
                    v.tensor_scalar(d, d, affine[1], None, ALU.add).then_inc(ln_free, 1)

        RSUM = sb("RSUM", [P, 1, P])

        def sums_pe(t, bank, src, done):
            for a in range(NG):
                for w in range(NW):
                    mm = t.matmul(PS[32 * w:32 * w + 32, bank, 0:P], pick[:, 32 * a:32 * a + 32], src(a)[:, w * P:(w + 1) * P],
                                  start=(a == 0), stop=(a == NG - 1), skip_group_check=True)
            mm.then_inc(done, 1)

        def spread_sums_pe(t, bank, a, rsum, done):
            for w in range(NW):
                for g in range(GH):
                    row = 32 * w + GH * a + g
                    mm = t.matmul(PS[32 * g:32 * g + 32, bank, w * P:(w + 1) * P],
                                  ident[:, row:row + 1].broadcast_to((P, 32)), rsum, start=True, stop=True,
                                  skip_group_check=True)
            mm.then_inc(done, 1)

        arena_at[0] = 0
        NKZ = 2 * GH
        Q0, K0 = place([NCH, CH]), place([NCH, CH])
        QS, KS = place([CH]), place([CH])
        NRM = place([2, P])
        VC = place([NCH, NT0, P])
        VW = [place([NT0, H, 32]) for _ in range(2)]
        KZ = place([NKZ, CH])
        E0 = place([4, 2, CH])
        OS = [place([NG, CH]) for _ in range(2)]
        assert arena_at[0] <= early_at["normback"]
        a0_qk, a0_v, a0_sq, a0_ssq, a0_raw = sem("a0_qk"), sem("a0_v"), sem("a0_sq"), sem("a0_ssq"), sem("a0_raw")
        a0_vc, a0_vw, a0_root, a0_eps, a0_inv = sem("a0_vc"), sem("a0_vw"), sem("a0_root"), sem("a0_eps"), sem("a0_inv")
        a0_back, a0_kn, a0_kz = sem("a0_back"), sem("a0_kn"), sem("a0_kz")
        a0_kz_free, a0_s_free, a0_e_free = (sem("a0_kz_free"), sem("a0_s_free"), sem("a0_e_free"))
        a0_o_free, a0_bc, a0_sum, a0_rs = sem("a0_o_free"), sem("a0_bc"), sem("a0_sum"), sem("a0_rs")
        a0_on, a0_y, a0_masked = sem("a0_on"), sem("a0_y"), sem("a0_masked")
        SBANK = [0, 1, 6, 7]

        def a0_prep_pe(t):
            for c in range(NCH + 1):
                if c < NCH:
                    x = XN[:, c * CH:(c + 1) * CH]
                    t.wait_ge(ln_free, ln_count(0, c))
                    if c > 0:
                        t.wait_ge(a0_raw, 2 * c)
                    t.matmul(PS[:, 0, :], qkvT[:, 0:P], x, start=True, stop=True)
                    t.matmul(PS[:, 1, :], qkvT[:, P:2 * P], x, start=True, stop=True).then_inc(a0_qk, 1)
                    if c > 0:
                        t.wait_ge(a0_vc, c)
                    for w in range(NT0):
                        k0 = c * CH + win_start(w)
                        mm = t.matmul(PS[:, 2 + w // 4, (w % 4) * P:(w % 4 + 1) * P], XN[:, k0:k0 + P],
                                      qkvT[:, 2 * P:3 * P], start=(w % 4 == 0), stop=(w % 4 == 3 or w == NT0 - 1),
                                      skip_group_check=True)
                    mm.then_inc(a0_v, 1)
                if c > 0:
                    t.wait_ge(a0_inv, c)
                    if c > 1:
                        t.wait_ge(a0_kn, 2 * (c - 1))
                    for n in range(2):
                        for w in range(NW):
                            at = (2 * w + n) * P
                            mm = t.matmul(PS[:, 6 + n, w * P:(w + 1) * P], normback[:, at:at + P],
                                          NRM[:, (c - 1) % 2, :], start=True, stop=True, skip_group_check=True)
                        mm.then_inc(a0_back, 1)
                if c < NCH:
                    if c == 0:
                        t.wait_ge(ln_free, ln_count(0, NCH - 1))
                    t.wait_ge(a0_sq, 2 * c + 2)
                    if c > 1:
                        t.wait_ge(a0_root, c - 1)
                    for n, sq in enumerate((QS, KS)):
                        for w in range(NW):
                            mm = t.matmul(PS[32 * w:32 * w + 32, 4 + c % 2, 0:P], normrows[:, 32 * n:32 * n + 32],
                                          sq[:, w * P:(w + 1) * P], start=(n == 0), stop=(n == 1),
                                          skip_group_check=True)
                    mm.then_inc(a0_ssq, 1)

        def a0_prep_act(a):
            for c in range(NCH):
                a.wait_ge(a0_qk, c + 1)
                if c > 0:
                    a.wait_ge(a0_ssq, c)
                nc.scalar.activation(QS, PS[:, 0, :], ACT.Square, bias=bqk[:, 0:1]).then_inc(a0_sq, 1)
                nc.scalar.activation(KS, PS[:, 1, :], ACT.Square, bias=bqk[:, 1:2]).then_inc(a0_sq, 1)
                a.wait_ge(a0_ssq, c + 1)
                if c > 1:
                    a.wait_ge(a0_back, 2 * (c - 1))
                nc.scalar.activation(NRM[:, c % 2, :], PS[:, 4 + c % 2, 0:P], ACT.Sqrt).then_inc(a0_root, 1)

        def a0_prep_dve(v):
            for c in range(NCH + 1):
                if c < NCH:
                    for n, raw in enumerate((Q0, K0)):
                        v.wait_ge(a0_sq, 2 * c + n + 1)
                        v.tensor_scalar(raw[:, c, :], PS[:, n, :], bqk[:, n:n + 1], None, ALU.add).then_inc(a0_raw, 1)
                    v.wait_ge(a0_v, c + 1)
                    v.tensor_tensor(VC[:, c, 0:4, :], PS[:, 2, :].rearrange("p (w d) -> p w d", w=4),
                                    bvrow[:].rearrange("p (w d) -> p w d", w=1).broadcast_to((P, 4, P)), ALU.add)
                    v.tensor_tensor(VC[:, c, 4, :], PS[:, 3, 0:P], bvrow[:], ALU.add).then_inc(a0_vc, 1)
                if c > 0:
                    for n, raw in enumerate((Q0, K0)):
                        v.wait_ge(a0_raw, 2 * (c - 1) + n + 1)
                        v.wait_ge(a0_back, 2 * (c - 1) + n + 1)
                        v.tensor_tensor(raw[:, c - 1, :], raw[:, c - 1, :], PS[:, 6 + n, :], ALU.mult).then_inc(a0_kn, 1)
                if c < NCH:
                    v.wait_ge(a0_root, c + 1)
                    v.tensor_scalar(NRM[:, c % 2, :], NRM[:, c % 2, :], NORM_EPS, None, ALU.add).then_inc(a0_eps, 1)
                    v.wait_ge(a0_eps, c + 1)
                    v.reciprocal(NRM[:, c % 2, :], NRM[:, c % 2, :]).then_inc(a0_inv, 1)

        def a0_pool(g):
            g.wait_ge(a0_vw, 1)
            g.wait_ge(ln_inverse, 2 * 1)
            for c in range(NCH):
                g.wait_ge(a0_vc, c + 1)
                if c > 0:
                    g.wait_ge(a0_vw, c + 1)
                if c > 1:
                    g.wait_ge(a0_e_free, 4 + 8 * (c - 1))
                nc.gpsimd.tensor_copy(VW[c % 2][:, :, :, 0:HD],
                                      VC[:, c, :, :].rearrange("p w (h d) -> p w h d", h=H)).then_inc(a0_vw, 1)
            g.wait_ge(a0_vw, 1 + NCH)

        A0_SUM, A0_SPREAD, A0_OUT = (4, 0), ((4,), (1, 2)), (5, 3)

        def a0_sums_pe(t, c, j):
            t.wait_ge(a0_o_free, c * NG + NG + 2)
            t.wait_ge(a0_on, 2 + c * NG)
            sums_pe(t, A0_SUM[j], lambda a: OS[j][:, a, :], a0_sum)

        def a0_spread_pe(t, c, a, banks):
            if a == 0:
                t.wait_ge(a0_rs, c + 1)
            t.wait_ge(a0_on, 2 + c * NG + a + 1 - len(banks))
            spread_sums_pe(t, banks[a % len(banks)], a, RSUM[:, 0, :], a0_bc)

        def a0_project_pe(t, c, j, a):
            if a == 0:
                t.wait_ge(x_ready, c + 1)
            t.wait_ge(a0_on, 2 + c * NG + a + 1)
            mm = t.matmul(PS[:, A0_OUT[j], :], wo0[:, a * P:(a + 1) * P], OS[j][:, a, :], start=(a == 0), stop=(a == NG - 1))
            if a == NG - 1:
                mm.then_inc(a0_y, 1)

        def a0_heads_pe(t, i, j):
            c = i * 2 + j
            if j == 0:
                t.wait_ge(x_ready, c + 1)
            for hp in range(10):
                if hp < 8:
                    t.wait_ge(a0_s_free, c * 8 + hp + 1)
                    for h in (2 * hp, 2 * hp + 1):
                        bank = SBANK[h % 4]
                        t.wait_ge(a0_kz, c * H + h + 1)
                        for w in range(NT0):
                            q0, q1 = win_queries(w)
                            mm = t.matmul(PS[:, bank:bank + 1, q0:q1], KZ[:, h % NKZ, win_start(w):win_start(w) + P],
                                          Q0[:, bass.ds(c, 1), q0:q1], start=True, stop=True, skip_group_check=True)
                        mm.then_inc(a0_kz_free, 1)
                if hp >= 2:
                    pr = hp - 2
                    t.wait_ge(a0_masked, c * 8 + pr + 1)
                    if pr % 2 == 0:
                        t.wait_ge(a0_o_free, c * NG + pr // 2 + 1)
                    if pr == 0:
                        t.wait_ge(a0_vw, c + 2)
                    for w in range(NT0):
                        q0, q1 = win_queries(w)
                        for h in (2 * pr, 2 * pr + 1):
                            g = h % GH
                            mm = t.matmul(PS[32 * g:32 * g + 32, 2 + (h // GH) % 2, q0:q1], VW[j][:, w, h, :],
                                          E0[:, pr % 4, h % 2, q0:q1], start=(w == 0), stop=(w == NT0 - 1),
                                          skip_group_check=True)
                    mm.then_inc(a0_e_free, 1)
                if j == 1:
                    if hp == 1:
                        a0_sums_pe(t, i * 2, 0)
                    if 2 <= hp < 2 + NG:
                        a0_spread_pe(t, i * 2, hp - 2, A0_SPREAD[0])
                    if 4 <= hp < 4 + NG:
                        a0_project_pe(t, i * 2, 0, hp - 4)

        def a0_pe(t):
            a0_prep_pe(t)
            t.wait_ge(a0_kn, 2 * NCH)
            with t.Fori(0, NCH // 2) as i:
                a0_heads_pe(t, i, 0)
                a0_heads_pe(t, i, 1)
                a0_sums_pe(t, i * 2 + 1, 1)
                for a in range(NG + 1):
                    if a < NG:
                        a0_spread_pe(t, i * 2 + 1, a, A0_SPREAD[1])
                    if a > 0:
                        a0_project_pe(t, i * 2 + 1, 1, a - 1)

        def a0_act(a):
            a0_prep_act(a)
            with a.Fori(0, NCH) as c:
                for pr in range(8):
                    a.wait_ge(a0_kz_free, NKZ + c * H + 2 * pr + 2)
                    a.wait_ge(a0_e_free, c * 8 + pr + 1)
                    b0 = SBANK[(2 * pr) % 4]
                    nc.scalar.activation(E0[:, pr % 4, :, :], PS[:, b0:b0 + 2, :], ACT.Exp).then_inc(a0_s_free, 1)

        def a0_dve(v):
            a0_prep_dve(v)
            v.wait_ge(a0_kn, 2 * NCH)

            def kz(c, h):
                v.wait_ge(a0_kz_free, c * H + h + 1)
                v.tensor_scalar(KZ[:, h % NKZ:h % NKZ + 1, :], K0[:, bass.ds(c, 1), :], headmask[:, h:h + 1], None,
                                ALU.mult).then_inc(a0_kz, 1)

            def mask(c, pr):
                v.wait_ge(a0_s_free, 2 + c * 8 + pr + 1)
                window = windowf.rearrange("p (o q) -> p o q", o=1).broadcast_to((P, 2, CH))
                v.tensor_tensor(E0[:, pr % 4, :, :], E0[:, pr % 4, :, :], window, ALU.mult).then_inc(a0_masked, 1)

            def take_o(c, j, a):
                v.wait_ge(a0_e_free, 4 + c * 8 + 2 * a + 2)
                v.tensor_copy(OS[j][:, a, :], PS[:, 2 + a % 2, :]).then_inc(a0_o_free, 1)

            def invert(c, j):
                v.wait_ge(a0_sum, c + 1)
                v.reciprocal(RSUM[:, 0, :], PS[:, A0_SUM[j], 0:P]).then_inc(a0_rs, 1)

            def norm_o(c, j, a):
                v.wait_ge(a0_bc, c * NG + a + 1)
                bank = A0_SPREAD[j][a % len(A0_SPREAD[j])]
                v.tensor_tensor(OS[j][:, a, :], OS[j][:, a, :], PS[:, bank, :], ALU.mult
                                ).then_inc(a0_on, 1)

            def residual(c, j):
                v.wait_ge(a0_y, c + 1)
                v.scalar_tensor_tensor(out=XP[:, chunk(c)], in0=PS[:, A0_OUT[j], :], scalar=bo0[:, 0:1], in1=XP[:, chunk(c)],
                                       op0=ALU.add, op1=ALU.add).then_inc(x_ready, 1)

            with v.Fori(0, NCH // 2) as i:
                for j in range(2):
                    c = i * 2 + j
                    if j == 0:
                        for h in range(NKZ):
                            kz(c, h)
                    for hp in range(1, 10):
                        if hp < 9:
                            mask(c, hp - 1)
                        if j == 1:
                            if hp == 2:
                                invert(i * 2, 0)
                            if 3 <= hp < 3 + NG:
                                norm_o(i * 2, 0, hp - 3)
                            if hp == 8:
                                residual(i * 2, 0)
                        if hp % 2 == 0 and (j == 0 or hp < 6):
                            for h in range(GH):
                                h += NKZ + (hp - 2) // 2 * GH
                                kz(c + h // H, h % H)
                        if hp % 2 == 1 and hp > 1:
                            take_o(c, j, (hp - 3) // 2)
                invert(i * 2 + 1, 1)
                for a in range(NG):
                    norm_o(i * 2 + 1, 1, a)
                residual(i * 2 + 1, 1)

        arena_at[0] = 0
        F0_SG, F0_H = place([2, CH]), place([2, NJ0, CH])
        f0_gu, f0_silu, f0_h_free, f0_y = sem("f0_gu"), sem("f0_silu"), sem("f0_h_free"), sem("f0_y")

        def f0_pe(t, use, k):
            def up(c, j):
                t.wait_ge(ln_free, ln_count(k, 0) + c)
                for b in range(NJ0):
                    m = NJ0 * NCH * use + NJ0 * c + b
                    r = (NJ0 * j + b) % 2
                    t.wait_ge(f0_h_free, m + 1)
                    x = XN[:, chunk(c)]
                    t.matmul(PS[:, r, :], ffn0[:, b * P:(b + 1) * P], x, start=True, stop=True)
                    t.matmul(PS[:, 2 + r, :], ffn0[:, HID0 + b * P:HID0 + (b + 1) * P], x, start=True,
                             stop=True).then_inc(f0_gu, 1)

            def down(c, j):
                t.wait_ge(f0_h_free, 2 + NJ0 * NCH * use + NJ0 * c + NJ0)
                if j == 0:
                    t.wait_ge(ln_free, ln_count(k, NCH - 1))
                stage = (1, 3)[use]
                t.wait_ge(x_ready, 1 + NCH * stage + c)
                for b in range(NJ0):
                    mm = t.matmul(PS[:, 4, :], ffn0[:, 2 * HID0 + b * P:2 * HID0 + (b + 1) * P], F0_H[:, j, b, :],
                                  start=(b == 0), stop=(b == NJ0 - 1))
                mm.then_inc(f0_y, 1)
            with t.Fori(0, NCH // 2) as i:
                up(i * 2, 0)
                up(i * 2 + 1, 1)
                down(i * 2, 0)
                down(i * 2 + 1, 1)

        def f0_act(a, use):
            def body(c, j):
                for b in range(NJ0):
                    m = NJ0 * NCH * use + NJ0 * c + b
                    r = (NJ0 * j + b) % 2
                    a.wait_ge(f0_gu, m + 1)
                    a.wait_ge(f0_h_free, m + 1)
                    nc.scalar.activation(F0_SG[:, r, :], PS[:, r, :], ACT.Silu).then_inc(f0_silu, 1)
            pairs(a, body)

        def f0_dve(v, use, natural):
            def up(c, j):
                for b in range(NJ0):
                    m = NJ0 * NCH * use + NJ0 * c + b
                    r = (NJ0 * j + b) % 2
                    v.wait_ge(f0_silu, m + 1)
                    v.tensor_tensor(F0_H[:, j, b, :], F0_SG[:, r, :], PS[:, 2 + r, :], ALU.mult).then_inc(f0_h_free, 1)

            def down(c, j):
                v.wait_ge(f0_y, NCH * use + c + 1)
                if natural:
                    dst = XR[:, bass.ds((c - j) * CH, S)].rearrange("p (a two) -> p a two", two=2)[:, :, j]
                    v.tensor_tensor(dst, PS[:, 4, :], XP[:, chunk(c)], ALU.add).then_inc(x_ready, 1)
                else:
                    v.tensor_tensor(XR[:, chunk(c)], PS[:, 4, :], XR[:, chunk(c)], ALU.add).then_inc(x_ready, 1)
            with v.Fori(0, NCH // 2) as i:
                up(i * 2, 0)
                up(i * 2 + 1, 1)
                down(i * 2, 0)
                down(i * 2 + 1, 1)

        arena_at[0] = 0
        XV, GT, SV, SA = (place([NCH, CH]) for _ in range(4))
        assert arena_at[0] <= PK_AT
        arena_at[0] = PK_AT + PK_SIZE
        SBB, HS, XS = (place([NCH, CH]) for _ in range(3))
        b0_gv, b0_gate, b0_val, b0_s, b0_sv = sem("b0_gv"), sem("b0_gate"), sem("b0_val"), sem("b0_s"), sem("b0_sv")
        b0_a, b0_b, b0_h, b0_y, b0_t = sem("b0_a"), sem("b0_b"), sem("b0_h"), sem("b0_y"), sem("b0_t")

        def b0_pe(t, k):
            for c in range(NCH + 3):
                if c < NCH:
                    t.wait_ge(ln_free, ln_count(k, c if c < 2 else NCH - 1))
                    x = XN[:, c * CH:(c + 1) * CH]
                    t.matmul(PS[:, 2 * c, :], winb[:, 0:P], x, start=True, stop=True)
                    t.matmul(PS[:, 2 * c + 1, :], winb[:, P:2 * P], x, start=True, stop=True).then_inc(b0_gv, 1)
                if 1 <= c <= NCH:
                    t.wait_ge(b0_val, c)
                    t.matmul(PS[:, 2 * c - 1, :], wsT[:], XV[:, c - 1, :], start=True, stop=True).then_inc(b0_s, 1)
                if c >= 3:
                    t.wait_ge(b0_h, c - 2)
                    t.matmul(PS[:, c - 3, :], woT[:], HS[:, c - 3, :], start=True, stop=True).then_inc(b0_y, 1)

        def b0_act(a):
            for c in range(NCH + 1):
                if c < NCH:
                    a.wait_ge(b0_gv, c + 1)
                    nc.scalar.activation(GT[:, c, :], PS[:, 2 * c, :], ACT.Sigmoid, bias=bin_[:, 0:1]).then_inc(b0_gate, 1)
                if c >= 1:
                    a.wait_ge(b0_s, c)
                    nc.scalar.activation(SV[:, c - 1, :], PS[:, 2 * c - 1, :], ACT.Tanh, bias=bs_[:, 0:1]).then_inc(b0_sv, 1)

        def b0_dve(v):
            def scan(c):
                v.wait_ge(b0_gate, c + 1)
                v.tensor_scalar(SA[:, c, :], GT[:, c, :], -1.0, 1.0, ALU.mult, ALU.add).then_inc(b0_a, 1)
                v.wait_ge(b0_sv, c + 1)
                v.tensor_tensor(SBB[:, c, :], GT[:, c, :], SV[:, c, :], ALU.mult).then_inc(b0_b, 1)
                v.wait_ge(b0_a, c + 1)
                v.wait_ge(b0_b, c + 1)
                if c % 2 == 1:
                    v.wait_ge(b0_h, c)
                v.tensor_tensor_scan(HS[:, c, :], SA[:, c, :], SBB[:, c, :],
                                     0.0 if c % 2 == 0 else HS[:, c - 1, CH - 1:CH], ALU.mult, ALU.add).then_inc(b0_h, 1)

            def residual(c):
                x = slice(c * CH, (c + 1) * CH)
                v.wait_ge(b0_y, c + 1)
                v.scalar_tensor_tensor(out=XS[:, c, :], in0=PS[:, c, :], scalar=bo_[:, 0:1], in1=XN[:, x],
                                       op0=ALU.add, op1=ALU.add).then_inc(b0_t, 1)
                v.wait_ge(b0_t, c + 1)
                v.tensor_tensor(XR[:, x], XR[:, x], XS[:, c, :], ALU.add).then_inc(x_ready, 1)

            for c in range(NCH + 3):
                if c < NCH:
                    v.wait_ge(b0_gv, c + 1)
                    v.tensor_scalar(XV[:, c, :], PS[:, 2 * c + 1, :], bin_[:, 1:2], None, ALU.add).then_inc(b0_val, 1)
                if 1 <= c <= NCH:
                    scan(c - 1)
                if c >= 3:
                    residual(c - 3)

        arena_at[0] = 0
        F1_SG, F1_H = place([2, CH]), [place([2, NJ1, CH]), place([2, NJ1, CH])]
        f1_gu, f1_silu, f1_h_free = sem("f1_gu"), sem("f1_silu"), sem("f1_h_free")
        f1_p, f1_g, f1_y = sem("f1_p"), sem("f1_g"), sem("f1_y")
        S_W1, S_W2, S_H1, S_H2, S_W3 = 0, NJ1, 2 * NJ1, 3 * NJ1, 4 * NJ1

        def f1_pe(t, use, k, stage):
            wait_loads(t, 3)
            with t.Fori(0, NCH // 2) as i:
                t.wait_ge(x_ready, 1 + NCH * stage + i * 2)
                for j in range(2):
                    c = i * 2 + j
                    t.wait_ge(ln_free, ln_count(k, 0) + c)
                    x = XN[:, chunk(c)]
                    for b in range(NJ1):
                        t.wait_ge(f1_h_free, NJ1 * NCH * use + NJ1 * c + b + 1)
                        r = b % 2
                        t.matmul(PS[:, r, :], w1T[:, b * P:(b + 1) * P], x, start=True, stop=True)
                        t.matmul(PS[:, 2 + r, :], w2T[:, b * P:(b + 1) * P], x, start=True, stop=True).then_inc(f1_gu, 1)
                for layer, w in ((0, h1T), (1, h2T)):
                    for j in range(2):
                        c = i * 2 + j
                        if layer == 0:
                            t.wait_ge(ln_free, ln_count(k, NCH - 1))
                            t.wait_ge(f1_h_free, 2 + NJ1 * NCH * use + NJ1 * c + NJ1)
                            if j == 0:
                                t.wait_ge(f1_h_free, 2 + NJ1 * NCH * use + NJ1 * c + 2 * NJ1)
                        else:
                            t.wait_ge(f1_g, 2 * NJ1 * NCH * use + i * 4 * NJ1 + NJ1 * (j + 1))
                        for b in range(NJ1):
                            for kk in range(NJ1):
                                mm = t.matmul(PS[:, 4 * j + b, :], w[:, kk * HID1 + b * P:kk * HID1 + (b + 1) * P],
                                              F1_H[layer][:, j, kk, :], start=(kk == 0), stop=(kk == NJ1 - 1))
                            mm.then_inc(f1_p, 1)
                for j in range(2):
                    c = i * 2 + j
                    t.wait_ge(f1_g, 2 * NJ1 * NCH * use + i * 4 * NJ1 + 2 * NJ1 + NJ1 * (j + 1))
                    for kk in range(NJ1):
                        mm = t.matmul(PS[:, 4 * j, :], w3T[:, kk * P:(kk + 1) * P], F1_H[0][:, j, kk, :],
                                      start=(kk == 0), stop=(kk == NJ1 - 1))
                    mm.then_inc(f1_y, 1)

        def f1_act(a, use):
            with a.Fori(0, NCH // 2) as i:
                for j in range(2):
                    for b in range(NJ1):
                        m = NJ1 * NCH * use + NJ1 * (i * 2 + j) + b
                        a.wait_ge(f1_gu, m + 1)
                        a.wait_ge(f1_h_free, m + 1)
                        nc.scalar.activation(F1_SG[:, b % 2, :], PS[:, b % 2, :], ACT.Silu,
                                             scale=scl[:, S_W1 + b:S_W1 + b + 1]).then_inc(f1_silu, 1)
                for layer, s0 in ((0, S_H1), (1, S_H2)):
                    for j in range(2):
                        for b in range(NJ1):
                            m = 2 * NJ1 * NCH * use + i * 4 * NJ1 + layer * 2 * NJ1 + j * NJ1 + b
                            a.wait_ge(f1_p, m + 1)
                            nc.scalar.activation(F1_H[1 - layer][:, j, b, :], PS[:, 4 * j + b, :], ACT.Gelu,
                                                 scale=scl[:, s0 + b:s0 + b + 1]).then_inc(f1_g, 1)

        def f1_dve(v, use):
            with v.Fori(0, NCH // 2) as i:
                for j in range(2):
                    for b in range(NJ1):
                        m = NJ1 * NCH * use + NJ1 * (i * 2 + j) + b
                        v.wait_ge(f1_silu, m + 1)
                        v.scalar_tensor_tensor(out=F1_H[0][:, j, b, :], in0=PS[:, 2 + b % 2, :],
                                               scalar=scl[:, S_W2 + b:S_W2 + b + 1], in1=F1_SG[:, b % 2, :],
                                               op0=ALU.mult, op1=ALU.mult).then_inc(f1_h_free, 1)
                for j in range(2):
                    c = i * 2 + j
                    v.wait_ge(f1_y, NCH * use + c + 1)
                    v.scalar_tensor_tensor(out=XR[:, chunk(c)], in0=PS[:, 4 * j, :], scalar=scl[:, S_W3:S_W3 + 1],
                                           in1=XR[:, chunk(c)], op0=ALU.mult, op1=ALU.add).then_inc(x_ready, 1)

        arena_at[0] = 0
        ON = place([NGRP, S])
        assert arena_at[0] == PK_AT
        PK = place([2, GH, 4, S], BF16)
        VG = place([2, NKT, GH, 32])
        PT = place([2, GH, CH])
        PD = place([2, GH * P])
        arena_at[0] = 0
        V32 = SQ, place([4, CH])
        SPL_EVEN = PT.rearrange("p a g s -> p (a g s)").bitcast(BF16)[:, 0:4 * 3 * CH]
        SPL = SPL_EVEN.rearrange("p (v k s) -> p v k s", v=4, k=3), place([4, 3, CH], BF16)
        KV, LAT = place([CH]), place([CH])
        FALL, RISE = place([S]), place([S])
        STRIP = XP[:, 0:2 * S - P]
        JUNK = SQ[:, 2:4, :].rearrange("p a b -> p (a b)").bitcast(BF16).rearrange("p (a b) -> p a b", a=4)
        MX = SQ[:, 0, 0:P]
        MH = SQ[:, 1, 0:P].bitcast(BF16).rearrange("p (k q) -> p k q", k=2)
        scr = nc.dram_tensor("scr", (2, 3, B, P, 2, S), BF16).ap()
        scr_heads = scr.rearrange("s k b (a g d) v t -> s k (b a) g d (v t)", a=NG, g=GH)
        mscr = nc.dram_tensor("mscr", (NGRP * 2, GH, S), BF16).ap()
        a1_qkv, a1_kv, a1_lat, a1_latc, a1_kr = sem("a1_qkv"), sem("a1_kv"), sem("a1_lat"), sem("a1_latc"), sem("a1_kr")
        a1_ver, a1_hi, a1_r1, a1_mid, a1_lo_free = sem("a1_ver"), sem("a1_hi"), sem("a1_r1"), sem("a1_mid"), sem("a1_lo_free")
        a1_v, a1_tab, a1_zero = sem("a1_v"), sem("a1_tab"), sem("a1_zero")
        a1_stored = sem("a1_stored_even"), sem("a1_stored_odd")
        pk_in = [[sem(f"pk_in{sl}{g}") for g in range(GH)] for sl in range(2)]
        pk_m, p1_s, p1_free = sem("pk_m"), sem("p1_s"), sem("p1_free")
        m_c, m_t, m_h, m_l, m_w = sem("m_c"), sem("m_t"), sem("m_h"), sem("m_l"), sem("m_w")
        dg_s, dg_fix, dg_m, dg_free = sem("dg_s"), sem("dg_fix"), sem("dg_m"), sem("dg_free")
        s_s, s_free, pv_free, o_free, vg_in = sem("s_s"), sem("s_free"), sem("pv_free"), sem("o_free"), sem("vg_in")
        a1_bc, a1_inv, a1_y, a1_vg0 = sem("a1_bc"), sem("a1_inv"), sem("a1_y"), sem("a1_vg0")
        a1_sum, a1_rs = sem("a1_sum"), sem("a1_rs")
        SCALE = 1.0 / float(np.sqrt(P))
        NT1 = GH * NKT
        S_BANKS, P1_BANKS = (0, 1, 4), (5, 6, 7)
        NS = 2 * NKT
        PV0 = NS + 2
        P10 = 2 + 2 * NT1 * NGRP
        DG_PER = NKT
        PACKS = 6

        def is_diag(s):
            return s < NS and s % NKT // (NKT // 2) == s // NKT

        def diag_index(s):
            return sum(is_diag(r) for r in range(s))

        def a1_prep_pe(t):
            wait_loads(t, 3)
            for c in range(NCH):
                x = XN[:, c * CH:(c + 1) * CH]
                t.wait_ge(ln_free, ln_count(4, c))
                if c > 0:
                    t.wait_ge(a1_ver, 4 * c - 2)
                t.matmul(PS[:, 0, :], wqkv1[:, 0:P], x, start=True, stop=True)
                t.matmul(PS[:, 1, :], wqkv1[:, P:2 * P], x, start=True, stop=False)
                t.matmul(PS[:, 1, :], wqkv1[:, 2 * P:3 * P], x, start=False, stop=True).then_inc(a1_qkv, 1)
                t.wait_ge(a1_kv, c + 1)
                t.matmul(PS[:, 2, :], wlow[:, 0:P], KV, start=True, stop=True).then_inc(a1_lat, 1)
                t.wait_ge(a1_latc, c + 1)
                t.wait_ge(ln_free, ln_count(4, NCH - 1))
                t.wait_ge(a1_v, c + 1)
                t.matmul(PS[:, 3, :], wlow[:, P:2 * P], LAT, start=True, stop=True)
                for w in range(CH // P):
                    mm = t.matmul(PS[:, 4, w * P:(w + 1) * P], LAT[:, w * P:(w + 1) * P], wlow[:, 2 * P:3 * P],
                                  start=True, stop=True, skip_group_check=True)
                mm.then_inc(a1_kr, 1)

        def a1_prep_act(a):
            def take_kv(c):
                a.wait_ge(a1_qkv, c + 1)
                nc.scalar.copy(KV, PS[:, 1, :]).then_inc(a1_kv, 1)

            def take_latent(c):
                a.wait_ge(a1_lat, c + 1)
                nc.scalar.copy(LAT, PS[:, 2, :]).then_inc(a1_latc, 1)

            def split(c):
                if c > 1:
                    a.wait_ge(a1_stored[c % 2], 64)
                for v in range(4):
                    a.wait_ge(a1_ver, 4 * c + v + 1)
                    nc.scalar.copy(SPL[c % 2][:, v, 0, :], V32[c % 2][:, v, :]).then_inc(a1_hi, 1)
                if c + 1 < NCH:
                    take_kv(c + 1)
                    take_latent(c + 1)
                for v in range(4):
                    a.wait_ge(a1_r1, 4 * c + v + 1)
                    nc.scalar.copy(SPL[c % 2][:, v, 1, :], V32[c % 2][:, v, :]).then_inc(a1_mid, 1)
            take_kv(0)
            take_latent(0)
            for c in range(NCH):
                split(c)

        def a1_prep_dve(v):
            v.wait_ge(a1_tab, 48)
            with v.Fori(0, B) as b:
                for j in range(2):
                    c = b * 2 + j
                    v.wait_ge(a1_qkv, c + 1)
                    for n, tab in ((0, FALL), (1, RISE), (2, RISE), (3, FALL)):
                        v.wait_ge(a1_lo_free, 4 * c + n + 1)
                        if n == 2:
                            v.wait_ge(a1_kr, c + 1)
                        v.scalar_tensor_tensor(out=V32[j][:, n, :], in0=PS[:, 0 if n < 2 else 3, :],
                                               scalar=SCALE if n < 2 else 1.0, in1=tab[:, j * CH:(j + 1) * CH],
                                               op0=ALU.mult, op1=ALU.mult).then_inc(a1_ver, 1)
                    v.tensor_copy(XN[:, chunk(c)], PS[:, 4, :]).then_inc(a1_v, 1)
                    for n in range(4):
                        v.wait_ge(a1_hi, 4 * c + n + 1)
                        v.tensor_tensor(V32[j][:, n, :], V32[j][:, n, :], SPL[j][:, n, 0, :], ALU.subtract).then_inc(a1_r1, 1)

        def a1_zeros(g, r, norms):
            if r == 32:
                g.wait_ge(x_ready, 1 + NCH)
            g.wait_ge(ln_inverse, 2 * norms)
            nc.gpsimd.memset(PK[r:r + 32].rearrange("p a g v s -> p (a g v s)").bitcast(F32), 0.0).then_inc(a1_zero, 1)
            g.wait_ge(a1_zero, r // 32)

        def a1_ones(g):
            for sl in range(2):
                nc.gpsimd.memset(PK[MROW:MROW + 2, sl, :, 2:4, :], -1.0).then_inc(a1_zero, 1)
            g.wait_ge(a1_zero, 4)
            nc.gpsimd.memset(VG[:, :, :, :, :].rearrange("p a k g d -> p (a k g d)"), 0.0).then_inc(a1_vg0, 1)
            g.wait_ge(a1_vg0, 1)
            for sl in range(2):
                nc.gpsimd.memset(VG[:, sl, :, :, HD:HD + 1], 1.0).then_inc(a1_vg0, 1)
            g.wait_ge(a1_vg0, 3)

        def a1_prep_pool(g):
            g.wait_ge(ln_inverse, 2 * 5)
            with g.Fori(0, NCH // 2) as i:
                for j in range(2):
                    for v in range(4):
                        g.wait_ge(a1_mid, 4 * (i * 2 + j) + v + 1)
                        nc.gpsimd.tensor_tensor(SPL[j][:, v, 2, :], V32[j][:, v, :], SPL[j][:, v, 1, :],
                                                ALU.subtract).then_inc(a1_lo_free, 1)

        def a1_pool(g):
            a1_prep_pool(g)
            g.wait_ge(a1_v, 1 + NCH)
            g.wait_ge(a1_vg0, 3)
            with g.Fori(0, B) as b:
                with g.Fori(0, NG // 2) as i:
                    for sl in range(2):
                        n = b * NG + i * 2 + sl
                        g.wait_ge(pv_free, PV0 + NS * (n - 1))
                        src = XN[:, bass.ds(b * S, S)].rearrange("p (t a w) -> p t a w", t=NKT, a=NG)
                        src = src[:, :, bass.ds(i * 2 + sl, 1), :]
                        src = src.rearrange("p t a (g d) -> p t (a g) d", g=GH)
                        nc.gpsimd.tensor_copy(VG[:, sl, :, :, 0:HD], src).then_inc(vg_in, 1)

        P1_FROM, P1_TO = 1, 14

        def p1_tiles(s):
            at = lambda k: min(max(k - P1_FROM, 0), P1_TO - P1_FROM) * NT1 // (P1_TO - P1_FROM)
            return range(at(s), at(s + 1))

        def p1_tile_pe(t, n, sl, tt, turn):
            g, q = tt // NKT, tt % NKT
            if q == 0:
                t.wait_ge(pk_in[sl][g], 16 * PACKS * (turn + 1))
            edge = P * (q + 1)
            for half in range(2):
                k = 2 * tt + half
                t.wait_ge(p1_free, P10 - 2 + 2 * NT1 * n + max(k, 2))
                bank = P1_BANKS[k % 3]
                lo, hi = half * CH, (half + 1) * CH
                for v, k0, k1 in ((0, lo, min(hi, edge)), (1, max(lo, edge), hi)):
                    if k0 < k1:
                        mm = t.matmul(PS[:, bank, k0 - lo:k1 - lo], PK[0:MROW, sl, g, v, q * P:(q + 1) * P],
                                      PK[0:MROW, sl, g, 2 + v, k0:k1], start=True, stop=True, skip_group_check=True)
                mm.then_inc(p1_s, 1)

        def p1_tile_dve(v, n, tt):
            q = tt % NKT
            for half in range(2):
                k = 2 * tt + half
                v.wait_ge(p1_s, 2 * NT1 * n + k + 1)
                apart(v)
                at = S - P - q * P + half * CH
                v.tensor_tensor_reduce(JUNK[:, k % 3, :], PS[:, P1_BANKS[k % 3], :], STRIP[:, at:at + CH], 1.0, -3.0e38,
                                       ALU.mult, ALU.max, MX[:, half * NT1 + tt:half * NT1 + tt + 1]).then_inc(p1_free, 1)

        def maxima_pe(t, n):
            t.wait_ge(m_c, n + 1)
            t.transpose(PS[:, P1_BANKS[0], 0:P], MX, ident[:]).then_inc(m_t, 1)

        def maxima_dve(v, n):
            v.wait_ge(p1_free, P10 + 2 * NT1 * (n + 1))
            v.tensor_tensor(MX[:, 0:NT1], MX[:, 0:NT1], MX[:, NT1:2 * NT1], ALU.max).then_inc(m_c, 1)
            v.wait_ge(m_t, n + 1)
            v.tensor_copy(MH[0:NT1, 0, :], PS[0:NT1, P1_BANKS[0], 0:P]).then_inc(m_h, 1)
            v.wait_ge(m_h, n + 1)
            v.tensor_tensor(MH[0:NT1, 1, :], PS[0:NT1, P1_BANKS[0], 0:P], MH[0:NT1, 0, :], ALU.subtract).then_inc(m_l, 1)

        def segments(s):
            hf, kt = s // NKT, s % NKT
            q0, q1 = hf * CH, (hf + 1) * CH
            d0, d1 = kt * P, (kt + 1) * P
            out_, at = [], 0
            for v, a_, b_ in ((1, q0, min(q1, d0)), (0, max(q0, d1), q1)):
                if a_ < b_:
                    out_.append((v, at, a_, b_))
                    at += b_ - a_
            return out_, at

        def diag_pe(t, n, sl, s):
            kt = s % NKT
            t.wait_ge(dg_free, DG_PER * n + diag_index(s) + 1)
            for g in range(GH):
                mm = t.matmul(PS[:, 2, g * P:(g + 1) * P], PK[0:MROW, sl, g, 2, kt * P:(kt + 1) * P],
                              PK[0:MROW, sl, g, 0, kt * P:(kt + 1) * P], start=(g == 0), stop=False,
                              skip_group_check=True)
            mm.then_inc(dg_s, 1)

        def diag_max_pe(t, n, sl, s):
            kt = s % NKT
            t.wait_ge(dg_fix, DG_PER * n + diag_index(s) + 1)
            for g in range(GH):
                mm = t.matmul(PS[:, 2, g * P:(g + 1) * P], PK[MROW:MROW + 2, sl, g, 2, kt * P:(kt + 1) * P],
                              PK[MROW:MROW + 2, sl, g, 0, kt * P:(kt + 1) * P], start=False, stop=True,
                              skip_group_check=True)
            mm.then_inc(dg_m, 1)

        def scores_pe(t, n, sl, s, g):
            kt = s % NKT
            k = GH * s + g
            t.wait_ge(s_free, NS * GH * n + max(k, 2))
            for v, at, a_, b_ in segments(s)[0]:
                mm = t.matmul(PS[:, S_BANKS[k % 3], at:at + b_ - a_], PK[0:MROW + 2, sl, g, 2 + v, kt * P:(kt + 1) * P],
                              PK[0:MROW + 2, sl, g, v, a_:b_], start=True, stop=True, skip_group_check=True)
            mm.then_inc(s_s, 1)

        def pv_pe(t, n, sl, s):
            hf, kt = s // NKT, s % NKT
            t.wait_ge(s_free, 2 + NS * GH * n + GH * (s + 1))
            if is_diag(s):
                t.wait_ge(dg_free, 1 + DG_PER * n + diag_index(s) + 1)
            if kt == 0:
                t.wait_ge(o_free, 2 * n + hf + 1)
            for g in range(GH):
                vg = VG[:, sl, kt, g, :]
                parts = [(PT[:, s % 2, g, at:at + b_ - a_], a_, b_) for _, at, a_, b_ in segments(s)[0]]
                if is_diag(s):
                    parts.append((PD[:, diag_index(s) % 2, g * P:(g + 1) * P], kt * P, (kt + 1) * P))
                for m, (rhs, a_, b_) in enumerate(parts):
                    mm = t.matmul(PS[32 * g:32 * g + 32, 3, a_ - hf * CH:b_ - hf * CH], vg, rhs,
                                  start=(kt == 0 and m == 0), stop=(kt == NKT - 1), skip_group_check=True)
            mm.then_inc(pv_free, 1)

        PROJ_STEPS = NG + 3
        A1_SUM, A1_SPREAD, A1_OUT = (7, 0), ((5,), (1, 2)), (6, 3)

        def output(c, a):
            return ON[:, c // 2 * NG + a, c % 2 * CH:(c % 2 + 1) * CH]

        def project_pe(t, c, st):
            if st == 0:
                sums_pe(t, A1_SUM[c // 2], lambda a: output(c, a), a1_sum)
            if 1 <= st <= NG:
                a = st - 1
                t.wait_ge(a1_rs, c + 1)
                banks = A1_SPREAD[c // 2]
                t.wait_ge(a1_inv, 2 + NG * c + a + 1 - len(banks))
                spread_sums_pe(t, banks[a % len(banks)], a, RSUM[:, 0, :], a1_bc)
            if 2 <= st <= NG + 1:
                a = st - 2
                if a == 0:
                    t.wait_ge(x_ready, 1 + NCH * 4 + c)
                t.wait_ge(a1_inv, 2 + NG * c + a + 1)
                mm = t.matmul(PS[:, A1_OUT[c // 2], :], wo1[:, a * P:(a + 1) * P], output(c, a), start=(a == 0), stop=(a == NG - 1))
                if a == NG - 1:
                    mm.then_inc(a1_y, 1)

        def project_dve(v, c, st):
            if st == 1:
                v.wait_ge(a1_sum, c + 1)
                v.reciprocal(RSUM[:, 0, :], PS[:, A1_SUM[c // 2], 0:P]).then_inc(a1_rs, 1)
            if 1 <= st <= NG:
                a = st - 1
                v.wait_ge(a1_bc, NG * c + a + 1)
                v.tensor_tensor(output(c, a), output(c, a), PS[:, A1_SPREAD[c // 2][a % len(A1_SPREAD[c // 2])], :], ALU.mult).then_inc(a1_inv, 1)
            if st == NG + 2:
                v.wait_ge(a1_y, c + 1)
                x = XR[:, c * CH:(c + 1) * CH]
                v.tensor_tensor(x, PS[:, A1_OUT[c // 2], :], x, ALU.add).then_inc(x_ready, 1)

        def group_pe(t, n, sl, turn, last=False):
            t.wait_ge(pk_m, 32 * (n + 1))
            t.wait_ge(vg_in, n + 1)
            diag_max_pe(t, n, sl, 0)
            for s in range(NS):
                tiles = [] if last else list(p1_tiles(s))

                def p1():
                    if tiles:
                        p1_tile_pe(t, n + 1, 1 - sl, tiles.pop(0), turn + sl)
                scores_pe(t, n, sl, s, 0)
                scores_pe(t, n, sl, s, 1)
                scores_pe(t, n, sl, s, 2)
                if is_diag(s + 1):
                    diag_pe(t, n, sl, s + 1)
                p1()
                scores_pe(t, n, sl, s, 3)
                if len(tiles) > 1:
                    p1()
                if s == P1_TO and not last:
                    maxima_pe(t, n + 1)
                if s == NS - 1 and not last:
                    diag_pe(t, n + 1, 1 - sl, 0)
                if s > 0:
                    pv_pe(t, n, sl, s - 1)
                if last and s < 2 * PROJ_STEPS:
                    if s == 0:
                        t.wait_ge(o_free, 1 + 2 * NG)
                    project_pe(t, s // PROJ_STEPS, s % PROJ_STEPS)
                p1()
                if is_diag(s + 1):
                    diag_max_pe(t, n, sl, s + 1)

            pv_pe(t, n, sl, NS - 1)

        def group_act(a, n):
            for s in range(NS):
                a.wait_ge(pv_free, PV0 + NS * n + s - 1)
                if is_diag(s):
                    a.wait_ge(dg_m, DG_PER * n + diag_index(s) + 1)
                    nc.scalar.activation(PD[:, diag_index(s) % 2, :], PS[:, 2, :], ACT.Exp).then_inc(dg_free, 1)
                w = segments(s)[1]
                for g in range(GH):
                    a.wait_ge(s_s, NS * GH * n + GH * s + g + 1)
                    nc.scalar.activation(PT[:, s % 2, g, 0:w], PS[:, S_BANKS[(GH * s + g) % 3], 0:w], ACT.Exp).then_inc(s_free, 1)
                if s == NKT:
                    half_out(a, n, 0)
            half_out(a, n, 1)

        def half_out(a, n, hf):
            a.wait_ge(pv_free, PV0 + NS * n + NKT * (hf + 1))
            apart(a)
            nc.scalar.copy(ON[:, bass.ds(n, 1), hf * CH:(hf + 1) * CH], PS[:, 3:4, :]).then_inc(o_free, 1)

        def fix_dve(v, n, s):
            v.wait_ge(dg_s, DG_PER * n + diag_index(s) + 1)
            v.tensor_tensor(PS[:, 2, :], PS[:, 2, :], fixT[:], ALU.mult).then_inc(dg_fix, 1)

        def group_dve(v, n, last=False):
            for s in range(NS):
                if is_diag(s + 1):
                    fix_dve(v, n, s + 1)
                if last and s < 2 * PROJ_STEPS:
                    project_dve(v, s // PROJ_STEPS, s % PROJ_STEPS)
                if not last:
                    for tt in p1_tiles(s):
                        p1_tile_dve(v, n + 1, tt)
                    if s == P1_TO:
                        maxima_dve(v, n + 1)
            if not last:
                fix_dve(v, n + 1, 0)

        def a1_pe(t):
            a1_prep_pe(t)
            t.wait_ge(a1_v, 1 + NCH)
            for tt in range(NT1):
                p1_tile_pe(t, 0, 0, tt, 0)
            diag_pe(t, 0, 0, 0)
            maxima_pe(t, 0)
            with t.Fori(0, NGRP // 2 - 1) as i:
                group_pe(t, i * 2, 0, i)
                group_pe(t, i * 2 + 1, 1, i)
            group_pe(t, NGRP - 2, 0, NGRP // 2 - 1)
            group_pe(t, NGRP - 1, 1, NGRP // 2 - 1, last=True)
            t.wait_ge(o_free, 1 + 2 * NGRP)
            for c in range(NCH // 2, NCH):
                for st in range(PROJ_STEPS):
                    project_pe(t, c, st)

        def a1_act(a):
            a1_prep_act(a)
            with a.Fori(0, NGRP) as n:
                group_act(a, n)

        def a1_dve(v):
            a1_prep_dve(v)
            v.wait_ge(a1_lo_free, 8 + 4 * (NCH - 1))
            v.memset(MX, 0.0).then_inc(preload, 1)
            v.wait_ge(preload, 3)
            for tt in range(NT1):
                p1_tile_dve(v, 0, tt)
            fix_dve(v, 0, 0)
            maxima_dve(v, 0)
            with v.Fori(0, NGRP - 1) as n:
                group_dve(v, n)
            group_dve(v, NGRP - 1, last=True)
            for c in range(NCH // 2, NCH):
                for st in range(PROJ_STEPS):
                    project_dve(v, c, st)

        def a1_sp(sp):
            sp.wait_ge(x_ready, 1 + NCH * 4)
            for dst, name in ((STRIP, "strip"), (FALL, "fall"), (RISE, "rise")):
                sp.dma_start(dst, W[name]).then_inc(a1_tab, 16)
            def stores(c):
                b, j = c // 2, c % 2
                for v in range(4):
                    sp.wait_ge(a1_lo_free, 8 + 4 * c + v + 1)
                    dst = scr[v // 2, :, b, :, v % 2, j * CH:(j + 1) * CH].rearrange("k p t -> p k t")
                    sp.dma_start(dst, SPL[c % 2][:, v, :, :]).then_inc(a1_stored[c % 2], 16)

            def packs(n, sl, heads=range(GH)):
                for g in heads:
                    for side, orders in ((0, ((0, 3, 0), (1, 2, 3), (2, 1, 5))), (2, ((None, 3, 0), (None, 2, 3), (None, 1, 5)))):
                        for piece, reps, at in orders:
                            rows = slice(at * HD, (at + reps) * HD)
                            dst = PK[rows, sl, g, side:side + 2, :].rearrange("p v t -> p (v t)")
                            if piece is None:
                                src = scr_heads[side // 2, 0:reps, bass.ds(n, 1), g].rearrange("k n d t -> (k n) d t")
                            else:
                                src = scr_heads[side // 2, piece:piece + 1, bass.ds(n, 1), g].rearrange(
                                    "k n d t -> (k n) d t").broadcast_to((reps, HD, 2 * S))
                            sp.dma_start(dst, src).then_inc(pk_in[sl][g], 16)

            def maxima(n, sl):
                sp.wait_ge(m_l, n + 1)
                for k in range(2):
                    sp.dma_start(mscr[bass.ds(n * 2 + k, 1)].rearrange("n g (t q) -> (n g t) q", q=P),
                                 MH[0:NT1, k, :]).then_inc(m_w, 16)
                sp.wait_ge(m_w, 32 * (n + 1))
                for v in range(2):
                    sp.dma_start(PK[MROW:MROW + 2, sl, :, v, :], mscr[bass.ds(n * 2, 2)]).then_inc(pk_m, 16)

            stores(0)
            stores(1)
            sp.wait_ge(a1_stored[0], 64)
            sp.wait_ge(a1_stored[1], 64)
            sp.wait_ge(a1_zero, 4)
            packs(0, 0, (0, 1))
            stores(2)
            packs(0, 0, (2, 3))
            stores(3)
            packs(1, 1)
            sp.wait_ge(a1_stored[0], 128)
            sp.wait_ge(a1_stored[1], 128)
            maxima(0, 0)
            with sp.Fori(0, NGRP // 2 - 1) as i:
                maxima(i * 2 + 1, 1)
                sp.wait_ge(pv_free, PV0 + NS * (i * 2 + 1))
                packs(i * 2 + 2, 0)
                maxima(i * 2 + 2, 0)
                sp.wait_ge(pv_free, PV0 + NS * (i * 2 + 2))
                packs(i * 2 + 3, 1)
            maxima(NGRP - 1, 1)

        arena_at[0] = 0
        HN = place([TOK])
        XC = place([B, KW - 1 + S])
        XA, DT, DU, SZ, YY = place([TOK]), place([TOK]), place([TOK]), place([TOK]), place([TOK])
        SG, SS = place([TOK]), place([TOK])
        CV = place([2, CH])
        HP_ = place([2, CH])
        BCP = place([3, TOK], BF16)
        BR = place([CH])
        DA, DBX, HH = place([4, CH]), place([2, CH]), place([4, CH])
        HC_ = place([4, CH])
        HL = place([DS])
        AN = place([DS])
        STT_, MV, GS = place([B, 2 * 6]), place([B, 2]), place([B, 8])
        m_norm = (HN, (mvec[:, 0:1], mvec[:, 1:2]))
        V_CW, V_CB, V_GG, V_GB, V_D, V_A = 2, 2 + KW, 3 + KW, 4 + KW, 5 + KW, 6 + KW
        m_p, m_x, m_z, m_abs, m_sg, m_gate = (sem(f"m_{x}") for x in ("p", "x", "z", "abs", "sg", "gate"))
        m_conv, m_silu, m_exp, m_ln, m_dt = (sem(f"m_{x}") for x in ("conv", "silu", "exp", "ln", "dt"))
        m_du, m_bc, m_an, m_done, m_pad = (sem(f"m_{x}") for x in ("du", "bc", "an", "done", "pad"))
        m_hp, m_ys = sem("m_hp"), sem("m_ys")
        m_bb, m_cb, m_da, m_dbx, m_st, m_hc = (sem("m_bb"), sem("m_cb"), sem("m_da"), sem("m_dbx"), sem("m_st"), sem("m_hc"))
        m_hl, m_sy, m_y, m_gn, m_gt, m_gd, m_yn, m_out, m_tmp = (sem(f"m_{x}") for x in (
            "hl", "sy", "y", "gn", "gt", "gd", "yn", "out", "tmp"))

        M_PER = 5

        def m_prep_pe(t):
            for c in range(NCH):
                t.wait_ge(ln_free, ln_count(7, c))
                for bank, (n, read, by) in enumerate(((0, m_x, 1), (1, m_z, 1), (2, m_dt, 1), (4, m_bc, 4), (5, m_sg, 1))):
                    if c > 0:
                        t.wait_ge(read, by * c)
                    if bank == LN_BANKS[7][0]:
                        t.wait_ge(ln_free, ln_count(7, 0))
                    t.matmul(PS[:, bank, :], minT[:, n * P:(n + 1) * P], HN[:, c * CH:(c + 1) * CH], start=True,
                             stop=True).then_inc(m_p, 1)

        def m_prep_act(a):
            a.wait_ge(m_pad, 1)
            for c in range(NCH):
                b, j = c // 2, c % 2
                at = slice(c * CH, (c + 1) * CH)
                a.wait_ge(m_p, M_PER * c + 1)
                nc.scalar.copy(XC[:, b, KW - 1 + j * CH:KW - 1 + (j + 1) * CH], PS[:, 0, :]).then_inc(m_x, 1)
                a.wait_ge(m_p, M_PER * c + 2)
                nc.scalar.activation(SZ[:, at], PS[:, 1, :], ACT.Silu).then_inc(m_z, 1)
                a.wait_ge(m_p, M_PER * c + 3)
                nc.scalar.activation(YY[:, at], PS[:, 2, :], ACT.Abs).then_inc(m_abs, 1)
                a.wait_ge(m_p, M_PER * c + 5)
                nc.scalar.copy(SG[:, at], PS[:, 4, :]).then_inc(m_sg, 1)
            a.wait_ge(m_abs, NCH)
            nc.scalar.activation(AN, mvec[:, V_A:V_A + DS], ACT.Exp).then_inc(m_an, 1)
            for b in range(B):
                yy = YY[:, b * S:(b + 1) * S]
                nc.scalar.activation(yy, yy, ACT.Exp, scale=-1.0).then_inc(m_exp, 1)
            for b in range(B):
                yy = YY[:, b * S:(b + 1) * S]
                a.wait_ge(m_exp, b + 1)
                nc.scalar.activation(yy, yy, ACT.Ln, bias=1.0).then_inc(m_ln, 1)
            a.wait_ge(m_sg, NCH)
            nc.scalar.activation(SG, SG, ACT.Sigmoid).then_inc(m_gate, 1)
            for c in range(NCH):
                xa = XA[:, c * CH:(c + 1) * CH]
                a.wait_ge(m_conv, KW * (c + 1))
                nc.scalar.activation(xa, xa, ACT.Silu).then_inc(m_silu, 1)

        def m_prep_dve(v):
            v.memset(XC[:, :, 0:KW - 1], 0.0).then_inc(m_pad, 1)
            for c in range(NCH):
                b, j = c // 2, c % 2
                at = slice(c * CH, (c + 1) * CH)
                v.wait_ge(m_p, M_PER * c + 4)
                v.tensor_copy(BCP[:, 0, at], PS[:, 3, :]).then_inc(m_bc, 1)
                v.wait_ge(m_bc, 4 * c + 1)
                v.tensor_tensor(BR, PS[:, 3, :], BCP[:, 0, at], ALU.subtract).then_inc(m_bc, 1)
                v.wait_ge(m_bc, 4 * c + 2)
                v.tensor_copy(BCP[:, 1, at], BR).then_inc(m_bc, 1)
                v.wait_ge(m_abs, c + 1)
                v.tensor_copy(DT[:, at], PS[:, 2, :]).then_inc(m_dt, 1)
                v.wait_ge(m_bc, 4 * c + 3)
                v.tensor_tensor(BCP[:, 2, at], BR, BCP[:, 1, at], ALU.subtract).then_inc(m_bc, 1)
                v.wait_ge(m_x, c + 1)
                x = [XC[:, b, k + j * CH:k + (j + 1) * CH] for k in range(KW)]
                cv = [CV[:, 0, :], CV[:, 1, :], CV[:, 0, :], XA[:, at]]
                v.tensor_scalar(cv[0], x[0], mvec[:, V_CW:V_CW + 1], mvec[:, V_CB:V_CB + 1], ALU.mult,
                                ALU.add).then_inc(m_conv, 1)
                for k in range(1, KW):
                    v.wait_ge(m_conv, KW * c + k)
                    v.scalar_tensor_tensor(out=cv[k], in0=x[k], scalar=mvec[:, V_CW + k:V_CW + k + 1], in1=cv[k - 1],
                                           op0=ALU.mult, op1=ALU.add).then_inc(m_conv, 1)
            v.wait_ge(m_an, 1)
            v.tensor_scalar(AN, AN, -1.0, None, ALU.mult).then_inc(m_an, 1)
            for c in range(NCH):
                at = slice(c * CH, (c + 1) * CH)
                v.wait_ge(m_ln, c // 2 + 1)
                v.wait_ge(m_dt, c + 1)
                v.scalar_tensor_tensor(out=DT[:, at], in0=DT[:, at], scalar=0.0, in1=YY[:, at], op0=ALU.max,
                                       op1=ALU.add).then_inc(m_du, 1)
                v.wait_ge(m_du, c + 1)
                v.wait_ge(m_silu, c + 1)
                v.tensor_tensor(DU[:, at], DT[:, at], XA[:, at], ALU.mult).then_inc(m_done, 1)

        NPAIR = DS // 2 - 1

        def m_scan_pe(t):
            t.wait_ge(m_du, 1)
            t.wait_ge(m_sg, NCH)
            with t.Fori(0, NCH // 2) as i:
                for j in range(2):
                    c = i * 2 + j
                    for n in range(DS + 2):
                        u = DS * c + n
                        if n < DS:
                            t.wait_ge(m_dbx, u + 1)
                            for k in range(3):
                                mm = t.matmul(PS[:, n % 2, :], identb[:, n:n + 1].broadcast_to((P, P)),
                                              BCP[:, k, chunk(c)], start=(k == 0), stop=(k == 2))
                            mm.then_inc(m_bb, 1)
                        if 1 <= n <= DS:
                            t.wait_ge(m_hc, u)
                            for k in range(3):
                                mm = t.matmul(PS[:, 2 + (n - 1) % 2, :],
                                              identb[:, DS + n - 1:DS + n].broadcast_to((P, P)),
                                              BCP[:, k, chunk(c)], start=(k == 0), stop=(k == 2))
                            mm.then_inc(m_cb, 1)
                        if n >= 2:
                            q = n - 2
                            uq = DS * c + q
                            if q == 0:
                                t.wait_ge(m_y, 2 * c + 2)
                            t.wait_ge(m_st, 4 + uq + 1)
                            t.matmul(PS[32 * (q % 4):32 * (q % 4) + 32, 5 + 2 * j, :], statecol[:, (q // 4) * 32:(q // 4 + 1) * 32],
                                     HH[:, q % 4, :], start=(q < 4), stop=(q >= DS - 4), skip_group_check=True
                                     ).then_inc(m_sy, 1)
                        if n >= 4 and n % 2 == 0:
                            q = n // 2 - 2
                            t.wait_ge(m_hp, 2 + NPAIR * c + q + 1)
                            t.matmul(PS[:, 4 + 2 * j, :], ident[:], HP_[:, q % 2, :], start=(q == 0), stop=False
                                     ).then_inc(m_ys, 1)
                    for n in (DS - 2, DS - 1):
                        t.wait_ge(m_hc, 2 + DS * c + n + 1)
                        mm = t.matmul(PS[:, 4 + 2 * j, :], ident[:], HC_[:, n % 4, :], start=False, stop=(n == DS - 1))
                    mm.then_inc(m_ys, 1)

        def m_scan_pool(g):
            with g.Fori(0, NCH) as c:
                for q in range(NPAIR):
                    g.wait_ge(m_hc, 2 + DS * c + 2 * q + 2)
                    g.wait_ge(m_ys, (NPAIR + 1) * c + q + 1)
                    nc.gpsimd.tensor_tensor(HP_[:, q % 2, :], HC_[:, 2 * q % 4, :], HC_[:, (2 * q + 1) % 4, :],
                                            ALU.add).then_inc(m_hp, 1)

        def m_scan_act(a):
            a.wait_ge(m_an, 2)
            a.wait_ge(m_done, 1 + NCH)
            with a.Fori(0, NCH // 2) as i:
                for j in range(2):
                    c = i * 2 + j
                    for n in range(DS):
                        u = DS * c + n
                        a.wait_ge(m_st, u + 1)
                        apart(a)
                        nc.scalar.activation(DA[:, n % 4, :], DT[:, chunk(c)], ACT.Exp, scale=AN[:, n:n + 1]
                                             ).then_inc(m_da, 1)

        def m_scan_dve(v):
            def outputs(c, j):
                v.wait_ge(m_sy, 4 + DS * (c + 1))
                v.wait_ge(m_ys, 2 + (NPAIR + 1) * (c + 1))
                v.wait_ge(m_gate, 1)
                v.scalar_tensor_tensor(out=YY[:, chunk(c)], in0=XA[:, chunk(c)], scalar=mvec[:, V_D:V_D + 1],
                                       in1=PS[:, 4 + 2 * j, :], op0=ALU.mult, op1=ALU.add).then_inc(m_y, 1)
                v.tensor_tensor(SS[:, chunk(c)], SG[:, chunk(c)], PS[:, 5 + 2 * j, :], ALU.mult).then_inc(m_y, 1)

            with v.Fori(0, NCH // 2) as i:
                for j in range(2):
                    c = i * 2 + j
                    v.wait_ge(m_bb, DS * c + 1)
                    v.tensor_tensor(DBX[:, 0, :], DU[:, chunk(c)], PS[:, 0, :], ALU.mult).then_inc(m_dbx, 1)
                    for n in range(DS):
                        u = DS * c + n
                        v.wait_ge(m_dbx, 2 + u + 1)
                        v.wait_ge(m_da, u + 1)
                        v.wait_ge(m_sy, u + 1)
                        if n in (2, 3):
                            v.wait_ge(m_ys, 2 + (NPAIR + 1) * c)
                        else:
                            v.wait_ge(m_hp, 2 + NPAIR * c + max(n // 2 - 1, 0))
                        if j == 1:
                            v.wait_ge(m_hl, DS * i + n + 1)
                        v.tensor_tensor_scan(HH[:, n % 4, :], DA[:, n % 4, :], DBX[:, n % 2, :],
                                             0.0 if j == 0 else HL[:, n:n + 1], ALU.mult, ALU.add).then_inc(m_st, 1)
                        if n + 1 < DS:
                            v.wait_ge(m_bb, u + 2)
                            v.tensor_tensor(DBX[:, (n + 1) % 2, :], DU[:, chunk(c)], PS[:, (n + 1) % 2, :],
                                            ALU.mult).then_inc(m_dbx, 1)
                        v.wait_ge(m_st, 4 + u + 1)
                        v.wait_ge(m_cb, u + 1)
                        v.tensor_tensor(HC_[:, n % 4, :], HH[:, n % 4, :], PS[:, 2 + n % 2, :], ALU.mult).then_inc(m_hc, 1)
                        if j == 0:
                            v.tensor_copy(HL[:, n:n + 1], HH[:, n % 4, CH - 1:CH]).then_inc(m_hl, 1)
                        if j == 1 and n == 1:
                            outputs(i * 2, 0)
                outputs(i * 2 + 1, 1)

        def m_tail_dve(v):
            v.wait_ge(m_y, 4 + 2 * NCH)
            for b in range(B):
                for j in range(2):
                    v.bn_stats(STT_[:, b, 6 * j:6 * j + 6], YY[:, (2 * b + j) * CH:(2 * b + j + 1) * CH]).then_inc(m_gn, 1)
                v.wait_ge(m_gn, 5 * b + 2)
                v.bn_aggr(MV[:, b, :], STT_[:, b, :]).then_inc(m_gn, 1)
                v.wait_ge(m_gn, 5 * b + 3)
                g = GS[:, b, :]
                v.tensor_tensor(g[:, 0:1], MV[:, b, 0:1], MV[:, b, 0:1], ALU.mult).then_inc(m_gn, 1)
                v.wait_ge(m_gn, 5 * b + 4)
                v.tensor_tensor(MV[:, b, 1:2], MV[:, b, 1:2], g[:, 0:1], ALU.add).then_inc(m_gn, 1)
            for b in range(B):
                g = GS[:, b, :]
                v.wait_ge(m_gt, b + 1)
                v.tensor_copy(g[:, 0:2], PS[:, 6 + b, 0:2]).then_inc(m_gd, 1)
                v.wait_ge(m_gd, 7 * b + 1)
                v.tensor_tensor(g[:, 2:3], g[:, 0:1], g[:, 0:1], ALU.mult).then_inc(m_gd, 1)
                v.wait_ge(m_gd, 7 * b + 2)
                v.tensor_tensor(g[:, 3:4], g[:, 1:2], g[:, 2:3], ALU.subtract).then_inc(m_gd, 1)
                v.wait_ge(m_gd, 7 * b + 4)
                v.reciprocal(g[:, 5:6], g[:, 4:5]).then_inc(m_gd, 1)
                v.wait_ge(m_gd, 7 * b + 5)
                v.tensor_tensor(g[:, 6:7], g[:, 5:6], mvec[:, V_GG:V_GG + 1], ALU.mult).then_inc(m_gd, 1)
                v.wait_ge(m_gd, 7 * b + 6)
                v.scalar_tensor_tensor(out=g[:, 7:8], in0=g[:, 0:1], scalar=g[:, 6:7], in1=mvec[:, V_GB:V_GB + 1],
                                       op0=ALU.mult, op1=ALU.subtract).then_inc(m_gd, 1)
                v.wait_ge(m_gd, 7 * b + 7)
                for j in range(2):
                    c = 2 * b + j
                    v.tensor_scalar(YY[:, chunk(c)], YY[:, chunk(c)], g[:, 6:7], g[:, 7:8], ALU.mult,
                                    ALU.subtract).then_inc(m_tmp, 1)
                    v.wait_ge(m_tmp, c + 1)
                    v.tensor_tensor(YY[:, chunk(c)], YY[:, chunk(c)], SZ[:, chunk(c)], ALU.mult).then_inc(m_yn, 1)
            for c in range(NCH):
                v.wait_ge(m_out, c + 1)
                v.tensor_tensor(CV[:, c % 2, :], PS[:, c % 4, :], XN[:, chunk(c)], ALU.add).then_inc(m_tmp, 1)
                v.wait_ge(m_tmp, NCH + c + 1)
                v.tensor_tensor(XR[:, chunk(c)], XR[:, chunk(c)], CV[:, c % 2, :], ALU.add).then_inc(x_ready, 1)

        def m_tail_act(a):
            for b in range(B):
                a.wait_ge(m_gd, 7 * b + 3)
                nc.scalar.activation(GS[:, b, 4:5], GS[:, b, 3:4], ACT.Sqrt, bias=eps_col[:]).then_inc(m_gd, 1)

        def m_tail_pe(t):
            for b in range(B):
                t.wait_ge(m_gn, 5 * (b + 1))
                t.matmul(PS[:, 6 + b, 0:2], groupmean[:], MV[:, b, :], start=True, stop=True).then_inc(m_gt, 1)
            for c in range(NCH):
                t.matmul(PS[:, c, :], minT[:, 3 * P:4 * P], HN[:, chunk(c)], start=True, stop=False)
                t.matmul(PS[:, c, :], mout[:, P:2 * P], SS[:, chunk(c)], start=False, stop=False)
                t.wait_ge(m_yn, c + 1)
                t.matmul(PS[:, c, :], mout[:, 0:P], YY[:, chunk(c)], start=False, stop=True).then_inc(m_out, 1)

        def m_pe(t):
            m_prep_pe(t)
            m_scan_pe(t)
            m_tail_pe(t)

        def m_act(a):
            m_prep_act(a)
            m_scan_act(a)
            m_tail_act(a)

        def m_dve(v):
            m_prep_dve(v)
            m_scan_dve(v)
            m_tail_dve(v)

        PRELOADS = ((a1_lo_free, 8), (a1_v, 1), (p1_free, P10), (dg_free, 1), (s_free, 2), (pv_free, PV0),
                    (o_free, 1), (a1_inv, 2), (m_done, 1), (m_dbx, 2), (m_hc, 2), (m_st, 4), (m_sy, 4), (m_y, 4), (m_hp, 2), (m_ys, 2))
        out_done = sem("out_done")
        preload = sem("preload")

        block = ctx.enter_context(nc.Block())

        @block.sync
        def _(sp):
            sp.dma_start(XP[:], W["xT"]).then_inc(x_in, 16)
            for done, n0, n1 in load_parts:
                for t, name in loads[n0:n1]:
                    sp.dma_start(t if name in early_at else t[:], W[name]).then_inc(done, 16)
            if last_stage > 4:
                a1_sp(sp)
            sp.wait_ge(x_ready, 1 + NCH * last_stage)
            sp.dma_start(out, (XR if last_stage > 1 else XP)[:]).then_inc(out_done, 16)
            sp.wait_ge(out_done, 16)

        @block.tensor
        def _(t):
            t.wait_ge(x_in, 16)
            wait_loads(t, 0)
            ln_pe(t, 0, 0)
            wait_loads(t, 1)
            t.wait_ge(consts_ready, 3)
            a0_pe(t)
            if last_stage > 1:
                ln_pe(t, 1, 1)
                t.wait_ge(ffn0_ready, 1)
                f0_pe(t, 0, 1)
            if last_stage > 2:
                ln_pe(t, 2, 2)
                wait_loads(t, 2)
                b0_pe(t, 2)
            if last_stage > 3:
                ln_pe(t, 3, 3)
                f0_pe(t, 1, 3)
            if last_stage > 4:
                ln_pe(t, 4, 4)
                a1_pe(t)
            if last_stage > 5:
                ln_pe(t, 5, 5)
                f1_pe(t, 0, 5, 5)
            if last_stage > 6:
                ln_pe(t, 6, 6)
                ln_pe(t, 7, 6, XN)
                m_pe(t)
            if last_stage > 7:
                ln_pe(t, 8, 7)
                f1_pe(t, 1, 8, 7)

        @block.scalar
        def _(a):
            wait_loads(a, 0)
            nc.scalar.copy(identb[:], ident[:]).then_inc(consts_ready, 1)
            ln_act(a, 0)
            wait_loads(a, 1)
            a0_act(a)
            if last_stage > 1:
                ln_act(a, 1)
                f0_act(a, 0)
            if last_stage > 2:
                ln_act(a, 2)
                wait_loads(a, 2)
                b0_act(a)
            if last_stage > 3:
                ln_act(a, 3)
                f0_act(a, 1)
            if last_stage > 4:
                ln_act(a, 4)
                a1_act(a)
            if last_stage > 5:
                ln_act(a, 5)
                f1_act(a, 0)
            if last_stage > 6:
                ln_act(a, 6)
                ln_act(a, 7, HN)
                m_act(a)
            if last_stage > 7:
                ln_act(a, 8)
                f1_act(a, 1)

        @block.vector
        def _(v):
            for at, (s, n) in enumerate(((x_ready, 1), (ln_free, 1), (a0_kz_free, NKZ), (a0_s_free, 2),
                         (a0_e_free, 4), (a0_o_free, 2), (a0_on, 2), (f0_h_free, 2), (f1_h_free, 2)) + PRELOADS):
                v.memset(started[:, at:at + 1], 0.0).then_inc(s, n)
            v.memset(eps_col[:], EPS).then_inc(consts_ready, 1)
            v.memset(minus_half[:], -0.5).then_inc(consts_ready, 1)
            v.wait_ge(x_in, 16)
            for z in VW:
                v.memset(z, 0.0).then_inc(preload, 1)
            v.wait_ge(preload, 2)
            v.memset(VW[0][:, :, :, HD:HD + 1], 1.0)
            v.memset(VW[1][:, :, :, HD:HD + 1], 1.0).then_inc(a0_vw, 1)
            ln_dve(v, 0)
            wait_loads(v, 1)
            wait_loads(v, 2)
            v.tensor_scalar(ffn0[:], ffn0i, QSCALE, None, ALU.mult).then_inc(ffn0_ready, 1)
            a0_dve(v)
            if last_stage > 1:
                ln_dve(v, 1)
                f0_dve(v, 0, True)
            if last_stage > 2:
                ln_dve(v, 2)
                b0_dve(v)
            if last_stage > 3:
                ln_dve(v, 3)
                f0_dve(v, 1, False)
            if last_stage > 4:
                ln_dve(v, 4)
                a1_dve(v)
            if last_stage > 5:
                ln_dve(v, 5)
                f1_dve(v, 0)
            if last_stage > 6:
                ln_dve(v, 6)
                ln_dve(v, 7, *m_norm)
                m_dve(v)
            if last_stage > 7:
                ln_dve(v, 8)
                f1_dve(v, 1)

        @block.gpsimd
        def _(g):
            g.wait_ge(consts_ready, 3)
            for k in range((1, 1, 2, 3, 4, 5, 6, 8, 9)[last_stage]):
                ln_pool(g, k)
                if k == 0:
                    a0_pool(g)
                if last_stage > 4:
                    if k == 1:
                        a1_zeros(g, 32, 2)
                    if k == 3:
                        a1_zeros(g, 64, 4)
                        a1_ones(g)
                if k == 4:
                    a1_pool(g)
                if k == 7:
                    g.wait_ge(ln_inverse, 2 * 8)
                    m_scan_pool(g)
                    g.wait_ge(m_hp, 2 + NCH * NPAIR)


def pad_heads(w):
    n = w.shape[1]
    r = np.zeros((P, NG, n), w.dtype)
    for h in range(H):
        r[32 * (h % GH):32 * (h % GH) + HD, h // GH] = w[h * HD:(h + 1) * HD]
    return r.reshape(P, NG * n)


def kernel(**inputs):
    import concourse.bacc as bacc
    from concourse.bass_utils import run_bass_kernel_spmd as run

    i = {k: np.asarray(v) for k, v in inputs.items()}
    col = lambda a: a.reshape(-1, 1)
    w = shape_constants()
    w["xT"] = i["L0_attn_a_x"].reshape(B, S // 2, 2, P).transpose(3, 0, 2, 1).reshape(P, TOK)
    w["qkvT"] = i["L0_attn_a_qkv_w"].T
    w["bqk"] = i["L0_attn_a_qkv_b"][:2 * P].reshape(2, P).T
    w["bvrow"] = np.broadcast_to(i["L0_attn_a_qkv_b"][2 * P:], (P, P))
    w["wo0"], w["bo0"] = pad_heads(i["L0_attn_a_out_w"].T), col(i["L0_attn_a_out_b"])
    w["ffn0i"] = np.concatenate([i["L0_ffn_w_gate"].T, i["L0_ffn_w_up"].T,
                                 i["L0_ffn_w_down"].T.reshape(NJ0, P, P).transpose(1, 0, 2).reshape(P, HID0)], 1)
    w["winb"], w["binb"] = i["L0_attn_b_W_in"].T, i["L0_attn_b_b_in"].reshape(2, P).T
    w["wsT"], w["bs"] = i["L0_attn_b_W_s"].T, col(i["L0_attn_b_b_s"])
    w["woT"], w["bob"] = i["L0_attn_b_W_o"].T, col(i["L0_attn_b_b_o"])
    rows = lambda a: a.T.reshape(NJ1, P, -1).transpose(1, 0, 2).reshape(P, -1)
    w["w1T"], w["w2T"] = i["L1_ffn_w1_w"].T, i["L1_ffn_w2_w"].T
    w["h1T"], w["h2T"], w["w3T"] = rows(i["L1_ffn_h1_w"]), rows(i["L1_ffn_h2_w"]), rows(i["L1_ffn_w3_w"])
    w["scl"] = np.concatenate([i[f"L1_ffn_{n}_s"].reshape(-1, P).T for n in ("w1", "w2", "h1", "h2", "w3")], 1)
    w["wqkv1"] = np.concatenate([i[f"L1_attn_a_W_{n}"] for n in "qkv"], 1)
    DL = i["L1_attn_a_W_down_kv"].shape[1]
    low = np.zeros((P, 3, P), np.float32)
    low[:, 0, :DL], low[:DL, 1], low[:DL, 2] = (i["L1_attn_a_W_down_kv"], i["L1_attn_a_W_up_k"], i["L1_attn_a_W_up_v"])
    w["wlow"] = low.reshape(P, 3 * P)
    w["wo1"] = pad_heads(i["L1_attn_a_W_o"])
    inw = i["L1_attn_b_in_proj_w"]
    minT = np.zeros((P, 6, P), np.float32)
    for n in range(4):
        minT[:, n] = inw[n * P:(n + 1) * P].T
    minT[:, 4, :2 * DS] = inw[4 * P:4 * P + 2 * DS].T
    outw = i["L1_attn_b_out_proj_w"]
    mout = np.zeros((P, 2, P), np.float32)
    mout[:, 0] = outw[:, :P].T
    for n in range(DS):
        r = 32 * (n % 4) + n // 4
        minT[:, 5, r] = inw[4 * P + 2 * DS + n]
        mout[r, 1] = outw[:, P + n]
    w["minT"], w["mout"] = minT.reshape(P, -1), mout.reshape(P, -1)
    w["mvec"] = np.concatenate([col(i["L1_attn_b_ln_g"]), col(i["L1_attn_b_ln_b"]), i["L1_attn_b_conv_w"][:, 0],
                                col(i["L1_attn_b_conv_b"]), col(i["L1_attn_b_gn_g"]), col(i["L1_attn_b_gn_b"]),
                                col(i["L1_attn_b_D"]), i["L1_attn_b_A_log"]], 1)
    nc = bacc.Bacc("TRN2", target_bir_lowering=False, num_devices=1)
    w = {k: np.ascontiguousarray(v) for k, v in w.items()}
    aps = {k: nc.dram_tensor(k, v.shape, mybir.dt.from_np(v.dtype), kind="ExternalInput").ap() for k, v in w.items()}
    out = nc.dram_tensor("out_xT", (P, TOK), F32, kind="ExternalOutput").ap()
    build(nc, aps, out)
    r = run(nc, [w], core_ids=[0])
    return np.ascontiguousarray(r.results[0]["out_xT"].T.reshape(B, S, P))
```
